# Optimizing a Trainium2 kernel written in Bass

```python
import numpy as np
import jax
import jax.numpy as jnp

def _softmax(x, axis=-1):
    return jax.nn.softmax(x, axis=axis)

def _gelu(x):
    return jax.nn.gelu(x, approximate=True)

def _silu(x):
    return jax.nn.silu(x)

def _sigmoid(x):
    return jax.nn.sigmoid(x)

def _layernorm(x, axis=-1, eps=1e-05):
    m = jnp.mean(x, axis=axis, keepdims=True)
    v = jnp.var(x, axis=axis, keepdims=True)
    return (x - m) / jnp.sqrt(v + eps)

def _scatter_add(tgt, idx, src, axis=0):
    return tgt.at[idx].add(src)

def _segment_sum(src, seg, n):
    return jax.ops.segment_sum(src, seg, n)
kernel_name = 'mk_decoder_postln_d4_seqx_r8_d1dc69'

def setup_inputs(seed: int=0):
    np.random.seed(seed)
    _w = jnp.asarray

    def _rec_inputs():
        import jax
        import jax.numpy as jnp
        _rk = jax.random.key(seed)
        x = 0.002226 + 0.9996 * jax.random.normal(jax.random.fold_in(_rk, 1), (8, 128, 128), jnp.float32)
        _lenS = 128 - jax.random.randint(jax.random.fold_in(_rk, 7), (8,), 0, max(1, 128 // 4) + 1, jnp.int32)
        _lenS2 = 128 - jax.random.randint(jax.random.fold_in(_rk, 8), (8,), 0, max(1, 128 // 4) + 1, jnp.int32)
        _ctx_1024P = jax.random.normal(jax.random.fold_in(_rk, 11), (8, 16, 128), jnp.float32)
        _ctx_1024c = jax.random.dirichlet(jax.random.fold_in(_rk, 511), 0.3 * jnp.ones((16,), jnp.float32), (8, 128))
        _ctx_1024t = jnp.einsum('bsk,bkd->bsd', _ctx_1024c, _ctx_1024P)
        _ctx_1024t = _ctx_1024t * jax.lax.rsqrt(jnp.mean(jnp.square(_ctx_1024t)) + 1e-12) * 0.953939
        ctx_1024 = -0.000125008 + 0.999885 * (_ctx_1024t + 0.3 * jax.random.normal(jax.random.fold_in(_rk, 611), (8, 128, 128), jnp.float32))
        _validS = jnp.arange(128)[None, :] < _lenS[:, None]
        _validS2 = jnp.arange(128)[None, :] < _lenS2[:, None]
        _causal = jnp.tril(jnp.ones((128, 128), dtype=bool))
        mask_Bx1xSxS2_bk1 = jnp.broadcast_to(_validS2[:, None, None, :], (8, 1, 128, 128))
        return (x, ctx_1024, mask_Bx1xSxS2_bk1)
    x, ctx_1024, mask_Bx1xSxS2_bk1 = _rec_inputs()

    def _L0_attn_setup():
        import jax, jax.numpy as jnp
        import numpy as np
        key = jax.random.key(seed)
        ks = jax.random.split(key, 4)
        B, T, C = (8, 256, 128)
        scale = 1.0 / np.sqrt(C)
        return {'x': jax.random.normal(ks[0], (B, T, C), dtype=jnp.float32), 'Wk': jax.random.normal(ks[1], (C, C), dtype=jnp.float32) * scale, 'Wv': jax.random.normal(ks[2], (C, C), dtype=jnp.float32) * scale, 'Wr': jax.random.normal(ks[3], (C, C), dtype=jnp.float32) * scale, 'time_decay': jnp.zeros((C,), dtype=jnp.float32), 'time_first': jnp.zeros((C,), dtype=jnp.float32)}
    _L0_attn_all = _L0_attn_setup()
    _L0_attn_in = {k: v for k, v in _L0_attn_all.items() if k in ('Wk', 'Wv', 'Wr', 'time_decay', 'time_first')}
    del _L0_attn_all

    def _L0_xattn_setup():
        import jax, jax.numpy as jnp
        import numpy as np
        B, M, N, DIM, DH, H = (8, 512, 64, 128, 128, 8)
        INNER = DH * H
        EPS = 1e-05

        def _layernorm(x, g, b):
            mu = jnp.mean(x, axis=-1, keepdims=True)
            var = jnp.var(x, axis=-1, keepdims=True)
            return (x - mu) * jax.lax.rsqrt(var + EPS) * g + b
        key = jax.random.key(seed)
        ks = jax.random.split(key, 8)
        sd = 0.02
        return {'x': jax.random.normal(ks[0], (B, M, DIM), jnp.float32), 'latents': jax.random.normal(ks[1], (B, N, DIM), jnp.float32), 'gamma_media': jnp.ones((DIM,), jnp.float32), 'beta_media': jnp.zeros((DIM,), jnp.float32), 'gamma_lat': jnp.ones((DIM,), jnp.float32), 'beta_lat': jnp.zeros((DIM,), jnp.float32), 'Wq': jax.random.normal(ks[2], (DIM, INNER), jnp.float32) * sd, 'bq': jnp.zeros((INNER,), jnp.float32), 'Wkv': jax.random.normal(ks[3], (DIM, 2 * INNER), jnp.float32) * sd, 'bkv': jnp.zeros((2 * INNER,), jnp.float32), 'Wo': jax.random.normal(ks[4], (INNER, DIM), jnp.float32) * sd, 'bo': jnp.zeros((DIM,), jnp.float32)}
    _L0_xattn_all = _L0_xattn_setup()
    _L0_xattn_in = {k: v for k, v in _L0_xattn_all.items() if k in ('gamma_media', 'beta_media', 'gamma_lat', 'beta_lat', 'Wq', 'bq', 'Wkv', 'bkv', 'Wo', 'bo')}
    del _L0_xattn_all

    def _L0_ffn_setup():
        import jax, jax.numpy as jnp
        import numpy as np
        E, H, I, K = (8, 128, 256, 2)
        B, S = (4, 256)
        key = jax.random.key(seed)
        k1, k2, k3, k4 = jax.random.split(key, 4)
        x = jax.random.normal(k1, (B, S, H), dtype=jnp.float32)
        router_w = jax.random.uniform(k2, (E, H), dtype=jnp.float32, minval=-1.0, maxval=1.0) / np.sqrt(H).astype(np.float32)
        w13 = jax.random.normal(k3, (E, H, 2 * I), dtype=jnp.float32) * 0.02
        w2 = jax.random.normal(k4, (E, I, H), dtype=jnp.float32) * 0.02
        return {'x': x, 'router_w': router_w, 'w13': w13, 'w2': w2}
    _L0_ffn_all = _L0_ffn_setup()
    _L0_ffn_in = {k: v for k, v in _L0_ffn_all.items() if k in ('router_w', 'w13', 'w2')}
    del _L0_ffn_all

    def _L1_attn_setup():
        import jax, jax.numpy as jnp
        import numpy as np
        B, S, D = (4, 256, 128)

        def givens_rotate(r, x):
            g = r.reshape(-1, 2)
            g = g / jnp.linalg.norm(g, axis=-1, keepdims=True)
            xp = x.reshape(x.shape[:-1] + (x.shape[-1] // 2, 2))
            c, s = (g[:, 0], g[:, 1])
            y0 = c * xp[..., 0] - s * xp[..., 1]
            y1 = c * xp[..., 1] + s * xp[..., 0]
            return jnp.stack([y0, y1], axis=-1).reshape(x.shape)
        key = jax.random.key(seed)
        k1, k2 = jax.random.split(key, 2)
        Q = jax.random.normal(k1, (B, S, D), dtype=jnp.float32)
        rot_w = jax.random.uniform(k2, (3, D), dtype=jnp.float32, minval=-1.0, maxval=1.0)
        scale = jnp.array([np.sqrt(D)], dtype=jnp.float32)
        bias = jnp.zeros((), dtype=jnp.float32)
        return {'Q': Q, 'rot_w': rot_w, 'scale': scale, 'bias': bias}
    _L1_attn_all = _L1_attn_setup()
    _L1_attn_in = {k: v for k, v in _L1_attn_all.items() if k in ('rot_w', 'scale', 'bias')}
    del _L1_attn_all

    def _L1_xattn_setup():
        import jax, jax.numpy as jnp
        import numpy as np
        B, S, D, H = (4, 256, 128, 16)
        HD = D // H
        key = jax.random.key(seed)
        ks = jax.random.split(key, 12)
        scale = 1.0 / np.sqrt(D)
        inp = {'queries': jax.random.normal(ks[0], (B, S, D), jnp.float32), 'keys': jax.random.normal(ks[1], (B, S, D), jnp.float32), 'values': jax.random.normal(ks[2], (B, S, D), jnp.float32), 'mask': jax.random.randint(ks[3], (B, 1, S, S), 0, 2).astype(bool), 'Wq': jax.random.normal(ks[4], (D, D), jnp.float32) * scale, 'bq': jnp.zeros((D,), jnp.float32), 'Wk': jax.random.normal(ks[5], (D, D), jnp.float32) * scale, 'bk': jnp.zeros((D,), jnp.float32), 'Wv': jax.random.normal(ks[6], (D, D), jnp.float32) * scale, 'bv': jnp.zeros((D,), jnp.float32), 'Wo': jax.random.normal(ks[7], (D, D), jnp.float32) * scale, 'bo': jnp.zeros((D,), jnp.float32)}
        return inp
    _L1_xattn_all = _L1_xattn_setup()
    _L1_xattn_in = {k: v for k, v in _L1_xattn_all.items() if k in ('Wq', 'bq', 'Wk', 'bk', 'Wv', 'bv', 'Wo', 'bo')}
    del _L1_xattn_all

    def _L1_ffn_setup():
        import jax, jax.numpy as jnp
        import numpy as np
        BLOCK = 32
        W_BITS = 4
        ACT_BITS = 16

        def act_qdq(x):
            qmax = 2.0 ** (ACT_BITS - 1) - 1.0
            scale = jnp.maximum(jnp.max(jnp.abs(x)) / qmax, 1e-12)
            return jnp.clip(jnp.round(x / scale), -qmax - 1.0, qmax) * scale

        def fixed_qdq_u16(x):
            scale = 1.0 / 65536.0
            return jnp.clip(jnp.round(x / scale), 0.0, 65535.0) * scale

        def lpbq_dequant(w):
            O, I = w.shape
            qmax = 2.0 ** (W_BITS - 1) - 1.0
            wb = w.reshape(O, I // BLOCK, BLOCK)
            s = jnp.maximum(jnp.max(jnp.abs(wb), axis=-1, keepdims=True) / qmax, 1e-12)
            wq = jnp.clip(jnp.round(wb / s), -qmax - 1.0, qmax) * s
            return wq.reshape(O, I)
        key = jax.random.key(seed)
        k1, k2, k3, k4 = jax.random.split(key, 4)
        B, S, H, I = (2, 512, 128, 384)
        x = jax.random.normal(k1, (B, S, H), jnp.float32)
        w_gate = jax.random.normal(k2, (I, H), jnp.float32) * 0.02
        w_up = jax.random.normal(k3, (I, H), jnp.float32) * 0.02
        w_down = jax.random.normal(k4, (H, I), jnp.float32) * 0.02
        return {'x': x, 'w_gate': w_gate, 'w_up': w_up, 'w_down': w_down}
    _L1_ffn_all = _L1_ffn_setup()
    _L1_ffn_in = {k: v for k, v in _L1_ffn_all.items() if k in ('w_gate', 'w_up', 'w_down')}
    del _L1_ffn_all

    def _L2_attn_setup():
        import jax, jax.numpy as jnp
        import numpy as np
        B, T, C, H = (4, 256, 128, 16)
        D = C // H

        def _wkv_parallel(k, v, exp_w, exp_u):
            Tn = k.shape[1]
            exp_k = jnp.exp(k)
            exp_ek_v = exp_k * v
            t_idx = jnp.arange(Tn, dtype=k.dtype)
            log_alpha = jnp.log(exp_w)
            alpha_pow = jnp.exp(t_idx[None, :, None, None] * log_alpha)
            alpha_next_pow = alpha_pow * exp_w
            f_a = exp_ek_v / alpha_next_pow
            f_b = exp_k.sum(-1, keepdims=True) / alpha_next_pow
            cs_a = jnp.cumsum(f_a, axis=1)
            cs_b = jnp.cumsum(f_b, axis=1)
            zero_a = jnp.zeros_like(cs_a[:, :1])
            zero_b = jnp.zeros_like(cs_b[:, :1])
            excl_a = jnp.concatenate([zero_a, cs_a[:, :-1]], axis=1)
            excl_b = jnp.concatenate([zero_b, cs_b[:, :-1]], axis=1)
            state_a = jnp.nan_to_num(alpha_pow * excl_a, nan=0.0, posinf=0.0)
            state_b = jnp.nan_to_num(alpha_pow * excl_b, nan=0.0, posinf=0.0)
            exp_u_k = exp_u * exp_k
            num = state_a + exp_u_k * v
            den = jnp.maximum(state_b + exp_u_k.sum(-1, keepdims=True), 1e-06)
            return num / den
        key = jax.random.key(seed)
        ks = jax.random.split(key, 10)
        s = 1.0 / np.sqrt(C)
        return {'x': jax.random.normal(ks[0], (B, T, C), jnp.float32), 'mix_k': jax.random.uniform(ks[1], (1, 1, C), jnp.float32), 'mix_v': jax.random.uniform(ks[2], (1, 1, C), jnp.float32), 'mix_r': jax.random.uniform(ks[3], (1, 1, C), jnp.float32), 'W_key': jax.random.normal(ks[4], (C, C), jnp.float32) * s, 'W_value': jax.random.normal(ks[5], (C, C), jnp.float32) * s, 'W_receptance': jax.random.normal(ks[6], (C, C), jnp.float32) * s, 'W_output': jax.random.normal(ks[7], (C, C), jnp.float32) * s, 'time_decay': jax.random.normal(ks[8], (H,), jnp.float32) - 5.0, 'time_first': jax.random.normal(ks[9], (H,), jnp.float32)}
    _L2_attn_all = _L2_attn_setup()
    _L2_attn_in = {k: v for k, v in _L2_attn_all.items() if k in ('mix_k', 'mix_v', 'mix_r', 'W_key', 'W_value', 'W_receptance', 'W_output', 'time_decay', 'time_first')}
    del _L2_attn_all

    def _L2_xattn_setup():
        import jax, jax.numpy as jnp
        import numpy as np
        D_MODEL = 128
        NUM_HEADS = 16
        DEPTH = D_MODEL // NUM_HEADS

        def _split_heads(x, B):
            return x.reshape(B, -1, NUM_HEADS, DEPTH).transpose(0, 2, 1, 3)
        key = jax.random.key(seed)
        ks = jax.random.split(key, 10)
        B, LQ, LK = (4, 256, 256)
        bound = float(np.sqrt(6.0 / (D_MODEL + D_MODEL)))

        def w(k):
            return jax.random.uniform(k, (D_MODEL, D_MODEL), jnp.float32, -bound, bound)
        return {'query': jax.random.normal(ks[0], (B, LQ, D_MODEL), jnp.float32), 'value': jax.random.normal(ks[1], (B, LK, D_MODEL), jnp.float32), 'wq': w(ks[2]), 'bq': jnp.zeros((D_MODEL,), jnp.float32), 'wk': w(ks[3]), 'bk': jnp.zeros((D_MODEL,), jnp.float32), 'wv': w(ks[4]), 'bv': jnp.zeros((D_MODEL,), jnp.float32), 'wo': w(ks[5]), 'bo': jnp.zeros((D_MODEL,), jnp.float32)}
    _L2_xattn_all = _L2_xattn_setup()
    _L2_xattn_in = {k: v for k, v in _L2_xattn_all.items() if k in ('wq', 'bq', 'wk', 'bk', 'wv', 'bv', 'wo', 'bo')}
    del _L2_xattn_all

    def _L2_ffn_setup():
        import jax, jax.numpy as jnp
        import numpy as np
        D = 128
        H = 16
        KV = 8
        HD = D // H
        M = 448
        E = 8
        TOPK = 2
        EPS = 1e-06
        ROPE_THETA = 10000.0

        def _rmsnorm(x, w, eps=EPS):
            xf = x.astype(jnp.float32)
            var = jnp.mean(xf * xf, axis=-1, keepdims=True)
            return (xf * jax.lax.rsqrt(var + eps)).astype(x.dtype) * w

        def _rope(q, k):
            S = q.shape[1]
            inv_freq = 1.0 / ROPE_THETA ** (jnp.arange(0, HD, 2, dtype=jnp.float32) / HD)
            ang = jnp.arange(S, dtype=jnp.float32)[:, None] * inv_freq[None, :]
            cos = jnp.concatenate([jnp.cos(ang), jnp.cos(ang)], axis=-1)[None, :, None, :]
            sin = jnp.concatenate([jnp.sin(ang), jnp.sin(ang)], axis=-1)[None, :, None, :]

            def rot_half(t):
                t1, t2 = jnp.split(t, 2, axis=-1)
                return jnp.concatenate([-t2, t1], axis=-1)
            return (q * cos + rot_half(q) * sin, k * cos + rot_half(k) * sin)
        key = jax.random.key(seed)
        ks = jax.random.split(key, 12)
        s = 0.02
        B, S = (2, 128)
        return {'x': jax.random.normal(ks[0], (B, S, D), jnp.float32), 'ln1_w': jnp.ones((D,), jnp.float32), 'ln2_w': jnp.ones((D,), jnp.float32), 'wq': jax.random.normal(ks[1], (D, H * HD), jnp.float32) * s, 'wk': jax.random.normal(ks[2], (D, KV * HD), jnp.float32) * s, 'wv': jax.random.normal(ks[3], (D, KV * HD), jnp.float32) * s, 'wo': jax.random.normal(ks[4], (H * HD, D), jnp.float32) * s, 'router_w': jax.random.normal(ks[5], (D, E), jnp.float32) * s, 'w_gate': jax.random.normal(ks[6], (E, D, M), jnp.float32) * s, 'w_up': jax.random.normal(ks[7], (E, D, M), jnp.float32) * s, 'w_down': jax.random.normal(ks[8], (E, M, D), jnp.float32) * s}
    _L2_ffn_all = _L2_ffn_setup()
    _L2_ffn_in = {k: v for k, v in _L2_ffn_all.items() if k in ('ln1_w', 'ln2_w', 'wq', 'wk', 'wv', 'wo', 'router_w', 'w_gate', 'w_up', 'w_down')}
    del _L2_ffn_all

    def _L3_attn_setup():
        import jax, jax.numpy as jnp
        import numpy as np
        B, T, H, S = (4, 512, 128, 64)
        LN_EPS = 1e-05

        def _reference_tuple_inner(x, A_log, WB, WC, D, Wg, bg, Wout, bout, gamma, beta):
            A = jnp.exp(A_log)
            gate = jax.nn.sigmoid(jnp.einsum('bth,sh->bts', x, Wg) + bg)
            Bx = jnp.einsum('bth,sh->bts', x, WB)
            u = gate * Bx

            def step(state, u_t):
                state = A * state + u_t
                return (state, state)
            s0 = jnp.zeros((x.shape[0], A.shape[0]), x.dtype)
            final_state, states = jax.lax.scan(step, s0, jnp.swapaxes(u, 0, 1))
            states = jnp.swapaxes(states, 0, 1)
            y = jnp.einsum('bts,hs->bth', states, WC) + D * x
            h = y + x
            mu = jnp.mean(h, axis=-1, keepdims=True)
            var = jnp.mean(jnp.square(h - mu), axis=-1, keepdims=True)
            hn = (h - mu) * jax.lax.rsqrt(var + LN_EPS) * gamma + beta
            out = jnp.einsum('bth,oh->bto', hn, Wout) + bout
            return (out, final_state)
        key = jax.random.key(seed)
        ks = jax.random.split(key, 12)
        x = jax.random.normal(ks[0], (B, T, H), jnp.float32)
        A_log = jnp.log(jnp.exp(-0.5 * jnp.ones(S, jnp.float32)) + 0.1 * jax.random.normal(ks[1], (S,), jnp.float32))
        sH = 1.0 / np.sqrt(H)
        sS = 1.0 / np.sqrt(S)
        WB = jax.random.uniform(ks[2], (S, H), jnp.float32, -sH, sH)
        WC = jax.random.uniform(ks[3], (H, S), jnp.float32, -sS, sS)
        D = jax.random.normal(ks[4], (H,), jnp.float32)
        Wg = jax.random.uniform(ks[5], (S, H), jnp.float32, -sH, sH)
        bg = jax.random.uniform(ks[6], (S,), jnp.float32, -sH, sH)
        Wout = jax.random.uniform(ks[7], (H, H), jnp.float32, -sH, sH)
        bout = jax.random.uniform(ks[8], (H,), jnp.float32, -sH, sH)
        gamma = jnp.ones((H,), jnp.float32)
        beta = jnp.zeros((H,), jnp.float32)
        return {'x': x, 'A_log': A_log, 'WB': WB, 'WC': WC, 'D': D, 'Wg': Wg, 'bg': bg, 'Wout': Wout, 'bout': bout, 'gamma': gamma, 'beta': beta}
    _L3_attn_all = _L3_attn_setup()
    _L3_attn_in = {k: v for k, v in _L3_attn_all.items() if k in ('A_log', 'WB', 'WC', 'D', 'Wg', 'bg', 'Wout', 'bout', 'gamma', 'beta')}
    del _L3_attn_all

    def _L3_xattn_setup():
        import jax, jax.numpy as jnp
        import numpy as np
        E, T, H, F = (8, 256, 128, 512)
        key = jax.random.key(seed)
        k1, k2, k3 = jax.random.split(key, 3)
        x = jax.random.normal(k1, (E, T, H), dtype=jnp.float32)
        w1 = jax.random.normal(k2, (E, F, H), dtype=jnp.float32) * 0.02
        w2 = jax.random.normal(k3, (E, F, H), dtype=jnp.float32) * 0.02
        return {'x': x, 'w1': w1, 'w2': w2}
    _L3_xattn_all = _L3_xattn_setup()
    _L3_xattn_in = {k: v for k, v in _L3_xattn_all.items() if k in ()}
    del _L3_xattn_all

    def _L3_ffn_setup():
        import jax, jax.numpy as jnp
        import numpy as np
        NUM_EXPERTS = 160
        TOP_K = 8
        ROUTED_SCALE = 2.5
        HIDDEN = 128
        INTER = 64
        key = jax.random.key(seed)
        ks = jax.random.split(key, 7)
        B, S = (1, 256)
        return {'hidden_states': jax.random.normal(ks[0], (B, S, HIDDEN), dtype=jnp.float32), 'router_w': jax.random.normal(ks[1], (NUM_EXPERTS, HIDDEN), dtype=jnp.float32) * 0.02, 'expert_bias': jnp.zeros((NUM_EXPERTS,), dtype=jnp.float32), 'w_gate': jax.random.normal(ks[2], (NUM_EXPERTS, INTER, HIDDEN), dtype=jnp.float32) * 0.02, 'w_down': jax.random.normal(ks[3], (NUM_EXPERTS, HIDDEN, INTER), dtype=jnp.float32) * 0.02, 'w_gate_shared': jax.random.normal(ks[4], (INTER, HIDDEN), dtype=jnp.float32) * 0.02, 'w_down_shared': jax.random.normal(ks[5], (HIDDEN, INTER), dtype=jnp.float32) * 0.02}
    _L3_ffn_all = _L3_ffn_setup()
    _L3_ffn_in = {k: v for k, v in _L3_ffn_all.items() if k in ('router_w', 'expert_bias', 'w_gate', 'w_down', 'w_gate_shared', 'w_down_shared')}
    del _L3_ffn_all
    return {'x': x, 'ctx_1024': ctx_1024, 'mask_Bx1xSxS2_bk1': mask_Bx1xSxS2_bk1, 'L0_attn_Wk': _L0_attn_in['Wk'], 'L0_attn_Wv': _L0_attn_in['Wv'], 'L0_attn_Wr': _L0_attn_in['Wr'], 'L0_attn_time_decay': _L0_attn_in['time_decay'], 'L0_attn_time_first': _L0_attn_in['time_first'], 'L0_xattn_gamma_media': _L0_xattn_in['gamma_media'], 'L0_xattn_beta_media': _L0_xattn_in['beta_media'], 'L0_xattn_gamma_lat': _L0_xattn_in['gamma_lat'], 'L0_xattn_beta_lat': _L0_xattn_in['beta_lat'], 'L0_xattn_Wq': _L0_xattn_in['Wq'], 'L0_xattn_bq': _L0_xattn_in['bq'], 'L0_xattn_Wkv': _L0_xattn_in['Wkv'], 'L0_xattn_bkv': _L0_xattn_in['bkv'], 'L0_xattn_Wo': _L0_xattn_in['Wo'], 'L0_xattn_bo': _L0_xattn_in['bo'], 'L0_ffn_router_w': _L0_ffn_in['router_w'], 'L0_ffn_w13': _L0_ffn_in['w13'], 'L0_ffn_w2': _L0_ffn_in['w2'], 'L1_attn_rot_w': _L1_attn_in['rot_w'], 'L1_attn_scale': _L1_attn_in['scale'], 'L1_attn_bias': _L1_attn_in['bias'], 'L1_xattn_Wq': _L1_xattn_in['Wq'], 'L1_xattn_bq': _L1_xattn_in['bq'], 'L1_xattn_Wk': _L1_xattn_in['Wk'], 'L1_xattn_bk': _L1_xattn_in['bk'], 'L1_xattn_Wv': _L1_xattn_in['Wv'], 'L1_xattn_bv': _L1_xattn_in['bv'], 'L1_xattn_Wo': _L1_xattn_in['Wo'], 'L1_xattn_bo': _L1_xattn_in['bo'], 'L1_ffn_w_gate': _L1_ffn_in['w_gate'], 'L1_ffn_w_up': _L1_ffn_in['w_up'], 'L1_ffn_w_down': _L1_ffn_in['w_down'], 'L2_attn_mix_k': _L2_attn_in['mix_k'], 'L2_attn_mix_v': _L2_attn_in['mix_v'], 'L2_attn_mix_r': _L2_attn_in['mix_r'], 'L2_attn_W_key': _L2_attn_in['W_key'], 'L2_attn_W_value': _L2_attn_in['W_value'], 'L2_attn_W_receptance': _L2_attn_in['W_receptance'], 'L2_attn_W_output': _L2_attn_in['W_output'], 'L2_attn_time_decay': _L2_attn_in['time_decay'], 'L2_attn_time_first': _L2_attn_in['time_first'], 'L2_xattn_wq': _L2_xattn_in['wq'], 'L2_xattn_bq': _L2_xattn_in['bq'], 'L2_xattn_wk': _L2_xattn_in['wk'], 'L2_xattn_bk': _L2_xattn_in['bk'], 'L2_xattn_wv': _L2_xattn_in['wv'], 'L2_xattn_bv': _L2_xattn_in['bv'], 'L2_xattn_wo': _L2_xattn_in['wo'], 'L2_xattn_bo': _L2_xattn_in['bo'], 'L2_ffn_ln1_w': _L2_ffn_in['ln1_w'], 'L2_ffn_ln2_w': _L2_ffn_in['ln2_w'], 'L2_ffn_wq': _L2_ffn_in['wq'], 'L2_ffn_wk': _L2_ffn_in['wk'], 'L2_ffn_wv': _L2_ffn_in['wv'], 'L2_ffn_wo': _L2_ffn_in['wo'], 'L2_ffn_router_w': _L2_ffn_in['router_w'], 'L2_ffn_w_gate': _L2_ffn_in['w_gate'], 'L2_ffn_w_up': _L2_ffn_in['w_up'], 'L2_ffn_w_down': _L2_ffn_in['w_down'], 'L3_attn_A_log': _L3_attn_in['A_log'], 'L3_attn_WB': _L3_attn_in['WB'], 'L3_attn_WC': _L3_attn_in['WC'], 'L3_attn_D': _L3_attn_in['D'], 'L3_attn_Wg': _L3_attn_in['Wg'], 'L3_attn_bg': _L3_attn_in['bg'], 'L3_attn_Wout': _L3_attn_in['Wout'], 'L3_attn_bout': _L3_attn_in['bout'], 'L3_attn_gamma': _L3_attn_in['gamma'], 'L3_attn_beta': _L3_attn_in['beta'], 'L3_ffn_router_w': _L3_ffn_in['router_w'], 'L3_ffn_expert_bias': _L3_ffn_in['expert_bias'], 'L3_ffn_w_gate': _L3_ffn_in['w_gate'], 'L3_ffn_w_down': _L3_ffn_in['w_down'], 'L3_ffn_w_gate_shared': _L3_ffn_in['w_gate_shared'], 'L3_ffn_w_down_shared': _L3_ffn_in['w_down_shared']}

def reference(x, ctx_1024, mask_Bx1xSxS2_bk1, L0_attn_Wk, L0_attn_Wv, L0_attn_Wr, L0_attn_time_decay, L0_attn_time_first, L0_xattn_gamma_media, L0_xattn_beta_media, L0_xattn_gamma_lat, L0_xattn_beta_lat, L0_xattn_Wq, L0_xattn_bq, L0_xattn_Wkv, L0_xattn_bkv, L0_xattn_Wo, L0_xattn_bo, L0_ffn_router_w, L0_ffn_w13, L0_ffn_w2, L1_attn_rot_w, L1_attn_scale, L1_attn_bias, L1_xattn_Wq, L1_xattn_bq, L1_xattn_Wk, L1_xattn_bk, L1_xattn_Wv, L1_xattn_bv, L1_xattn_Wo, L1_xattn_bo, L1_ffn_w_gate, L1_ffn_w_up, L1_ffn_w_down, L2_attn_mix_k, L2_attn_mix_v, L2_attn_mix_r, L2_attn_W_key, L2_attn_W_value, L2_attn_W_receptance, L2_attn_W_output, L2_attn_time_decay, L2_attn_time_first, L2_xattn_wq, L2_xattn_bq, L2_xattn_wk, L2_xattn_bk, L2_xattn_wv, L2_xattn_bv, L2_xattn_wo, L2_xattn_bo, L2_ffn_ln1_w, L2_ffn_ln2_w, L2_ffn_wq, L2_ffn_wk, L2_ffn_wv, L2_ffn_wo, L2_ffn_router_w, L2_ffn_w_gate, L2_ffn_w_up, L2_ffn_w_down, L3_attn_A_log, L3_attn_WB, L3_attn_WC, L3_attn_D, L3_attn_Wg, L3_attn_bg, L3_attn_Wout, L3_attn_bout, L3_attn_gamma, L3_attn_beta, L3_ffn_router_w, L3_ffn_expert_bias, L3_ffn_w_gate, L3_ffn_w_down, L3_ffn_w_gate_shared, L3_ffn_w_down_shared):
    import jax
    import jax.numpy as jnp

    def _L0_attn_ref(x, Wk, Wv, Wr, time_decay, time_first):
        import jax, jax.numpy as jnp
        import numpy as np
        B, T, C = x.shape
        k = jnp.einsum('btc,dc->btd', x, Wk)
        r = jax.nn.sigmoid(jnp.einsum('btc,dc->btd', x, Wr))
        w = -jnp.exp(time_decay)

        def step(s, kt):
            s = s * w + kt
            return (s, s)
        k_tbc = jnp.swapaxes(k, 0, 1)
        _, s = jax.lax.scan(step, jnp.zeros((B, C), dtype=x.dtype), k_tbc)
        s = jnp.swapaxes(s, 0, 1)
        return jnp.einsum('btc,dc->btd', r * s, Wv)

    def _L0_xattn_ref(x, latents, gamma_media, beta_media, gamma_lat, beta_lat, Wq, bq, Wkv, bkv, Wo, bo):
        import jax, jax.numpy as jnp
        import numpy as np
        B, M, N, DIM, DH, H = (8, 512, 64, 128, 128, 8)
        INNER = DH * H
        EPS = 1e-05

        def _layernorm(x, g, b):
            mu = jnp.mean(x, axis=-1, keepdims=True)
            var = jnp.var(x, axis=-1, keepdims=True)
            return (x - mu) * jax.lax.rsqrt(var + EPS) * g + b
        b = x.shape[0]
        xn = _layernorm(x, gamma_media, beta_media)
        ln = _layernorm(latents, gamma_lat, beta_lat)
        q = ln @ Wq + bq
        kv_input = jnp.concatenate([xn, ln], axis=1)
        kv = kv_input @ Wkv + bkv
        k, v = jnp.split(kv, 2, axis=-1)

        def to_heads(t):
            return t.reshape(b, t.shape[1], H, DH).transpose(0, 2, 1, 3)
        q, k, v = (to_heads(q), to_heads(k), to_heads(v))
        q = q * DH ** (-0.5)
        sim = jnp.einsum('bhid,bhjd->bhij', q, k)
        attn = jax.nn.softmax(sim, axis=-1)
        out = jnp.einsum('bhij,bhjd->bhid', attn, v)
        out = out.transpose(0, 2, 1, 3).reshape(b, -1, INNER)
        return out @ Wo + bo

    def _L0_ffn_ref(x, router_w, w13, w2):
        import jax, jax.numpy as jnp
        import numpy as np
        E, H, I, K = (8, 128, 256, 2)
        B, S = (4, 256)
        logits = jnp.einsum('bsh,eh->bse', x, router_w)
        probs = jax.nn.softmax(logits, axis=-1)
        weights, indices = jax.lax.top_k(probs, K)
        weights = weights / (weights.sum(axis=-1, keepdims=True) + 1e-06)
        h13 = jnp.einsum('bsh,ehi->bsei', x, w13)
        gate, up = jnp.split(h13, 2, axis=-1)
        h = jax.nn.silu(gate) * up
        y = jnp.einsum('bsei,eih->bseh', h, w2)
        y_sel = jnp.take_along_axis(y, indices[..., None], axis=2)
        return (y_sel * weights[..., None]).sum(axis=2)

    def _L1_attn_ref(Q, rot_w, scale, bias):
        import jax, jax.numpy as jnp
        import numpy as np
        B, S, D = (4, 256, 128)

        def givens_rotate(r, x):
            g = r.reshape(-1, 2)
            g = g / jnp.linalg.norm(g, axis=-1, keepdims=True)
            xp = x.reshape(x.shape[:-1] + (x.shape[-1] // 2, 2))
            c, s = (g[:, 0], g[:, 1])
            y0 = c * xp[..., 0] - s * xp[..., 1]
            y1 = c * xp[..., 1] + s * xp[..., 0]
            return jnp.stack([y0, y1], axis=-1).reshape(x.shape)
        q = givens_rotate(rot_w[0], Q)
        k = givens_rotate(rot_w[1], Q)
        v = givens_rotate(rot_w[2], Q)
        zeros = jnp.zeros(Q.shape[:-1] + (1,), Q.dtype)
        q = jnp.concatenate([zeros, q], axis=-1)[:, None]
        k = jnp.concatenate([zeros, k], axis=-1)[:, None]
        v = jnp.concatenate([zeros, v], axis=-1)[:, None]
        sgn = jnp.concatenate([-jnp.ones((1,), Q.dtype), jnp.ones((q.shape[-1] - 1,), Q.dtype)])
        cin = jnp.einsum('bhqd,bhkd->bhqk', q * sgn, k)
        attn = jax.nn.softmax((2.0 + 2.0 * cin) / scale + bias, axis=-1)
        ave = jnp.einsum('bhqk,bhkd->bhqd', attn, v)
        inner = jnp.sum(ave * ave * sgn, axis=-1, keepdims=True)
        denom = jnp.sqrt(jnp.clip(jnp.abs(inner), 1e-08, None))
        out = (ave / denom)[:, 0]
        return out[..., 1:]

    def _L1_xattn_ref(queries, keys, values, mask, Wq, bq, Wk, bk, Wv, bv, Wo, bo):
        import jax, jax.numpy as jnp
        import numpy as np
        B, S, D, H = (4, 256, 128, 16)
        HD = D // H
        b, sq, d = queries.shape

        def split_heads(x):
            return x.reshape(b, x.shape[1], H, HD).transpose(0, 2, 1, 3)
        q = split_heads(queries @ Wq + bq)
        k = split_heads(keys @ Wk + bk)
        v = split_heads(values @ Wv + bv)
        scores = jnp.einsum('bhqd,bhkd->bhqk', q, k) / jnp.sqrt(jnp.float32(HD))
        scores = jnp.where(mask, jnp.float32(-1000000000000000.0), scores)
        attn = jax.nn.softmax(scores, axis=-1)
        ctx = jnp.einsum('bhqk,bhkd->bhqd', attn, v)
        ctx = ctx.transpose(0, 2, 1, 3).reshape(b, sq, d)
        return ctx @ Wo + bo

    def _L1_ffn_ref(x, w_gate, w_up, w_down):
        import jax, jax.numpy as jnp
        import numpy as np
        BLOCK = 32
        W_BITS = 4
        ACT_BITS = 16

        def act_qdq(x):
            qmax = 2.0 ** (ACT_BITS - 1) - 1.0
            scale = jnp.maximum(jnp.max(jnp.abs(x)) / qmax, 1e-12)
            return jnp.clip(jnp.round(x / scale), -qmax - 1.0, qmax) * scale

        def fixed_qdq_u16(x):
            scale = 1.0 / 65536.0
            return jnp.clip(jnp.round(x / scale), 0.0, 65535.0) * scale

        def lpbq_dequant(w):
            O, I = w.shape
            qmax = 2.0 ** (W_BITS - 1) - 1.0
            wb = w.reshape(O, I // BLOCK, BLOCK)
            s = jnp.maximum(jnp.max(jnp.abs(wb), axis=-1, keepdims=True) / qmax, 1e-12)
            wq = jnp.clip(jnp.round(wb / s), -qmax - 1.0, qmax) * s
            return wq.reshape(O, I)
        x = act_qdq(x)
        up = act_qdq(x @ lpbq_dequant(w_up).T)
        gate = act_qdq(x @ lpbq_dequant(w_gate).T)
        sig = fixed_qdq_u16(jax.nn.sigmoid(gate))
        gate = act_qdq(gate * sig)
        o = act_qdq(gate * up)
        return o @ lpbq_dequant(w_down).T

    def _L2_attn_ref(x, mix_k, mix_v, mix_r, W_key, W_value, W_receptance, W_output, time_decay, time_first):
        import jax, jax.numpy as jnp
        import numpy as np
        B, T, C, H = (4, 256, 128, 16)
        D = C // H

        def _wkv_parallel(k, v, exp_w, exp_u):
            Tn = k.shape[1]
            exp_k = jnp.exp(k)
            exp_ek_v = exp_k * v
            t_idx = jnp.arange(Tn, dtype=k.dtype)
            log_alpha = jnp.log(exp_w)
            alpha_pow = jnp.exp(t_idx[None, :, None, None] * log_alpha)
            alpha_next_pow = alpha_pow * exp_w
            f_a = exp_ek_v / alpha_next_pow
            f_b = exp_k.sum(-1, keepdims=True) / alpha_next_pow
            cs_a = jnp.cumsum(f_a, axis=1)
            cs_b = jnp.cumsum(f_b, axis=1)
            zero_a = jnp.zeros_like(cs_a[:, :1])
            zero_b = jnp.zeros_like(cs_b[:, :1])
            excl_a = jnp.concatenate([zero_a, cs_a[:, :-1]], axis=1)
            excl_b = jnp.concatenate([zero_b, cs_b[:, :-1]], axis=1)
            state_a = jnp.nan_to_num(alpha_pow * excl_a, nan=0.0, posinf=0.0)
            state_b = jnp.nan_to_num(alpha_pow * excl_b, nan=0.0, posinf=0.0)
            exp_u_k = exp_u * exp_k
            num = state_a + exp_u_k * v
            den = jnp.maximum(state_b + exp_u_k.sum(-1, keepdims=True), 1e-06)
            return num / den
        Bn, Tn, Cn = x.shape
        x_prev = jnp.pad(x, ((0, 0), (1, 0), (0, 0)))[:, :-1]
        k = (x * mix_k + x_prev * (1.0 - mix_k)) @ W_key.T
        v = (x * mix_v + x_prev * (1.0 - mix_v)) @ W_value.T
        r = jax.nn.sigmoid((x * mix_r + x_prev * (1.0 - mix_r)) @ W_receptance.T)
        k4 = k.reshape(Bn, Tn, H, D)
        v4 = v.reshape(Bn, Tn, H, D)
        exp_w = jnp.exp(-jnp.exp(time_decay)).reshape(1, 1, H, 1)
        exp_u = jnp.exp(time_first).reshape(1, 1, H, 1)
        wkv = _wkv_parallel(k4, v4, exp_w, exp_u).reshape(Bn, Tn, Cn)
        return r * wkv @ W_output.T

    def _L2_xattn_ref(query, value, wq, bq, wk, bk, wv, bv, wo, bo):
        import jax, jax.numpy as jnp
        import numpy as np
        D_MODEL = 128
        NUM_HEADS = 16
        DEPTH = D_MODEL // NUM_HEADS

        def _split_heads(x, B):
            return x.reshape(B, -1, NUM_HEADS, DEPTH).transpose(0, 2, 1, 3)
        B = query.shape[0]
        q = _split_heads(query @ wq.T + bq, B)
        k = _split_heads(value @ wk.T + bk, B)
        v = _split_heads(value @ wv.T + bv, B)
        scale = jnp.sqrt(jnp.asarray(DEPTH, dtype=q.dtype))
        scores = jnp.einsum('bhqd,bhkd->bhqk', q, k) / scale
        attn = jax.nn.softmax(scores, axis=-1)
        ctx = jnp.einsum('bhqk,bhkd->bhqd', attn, v)
        ctx = ctx.transpose(0, 2, 1, 3).reshape(B, -1, D_MODEL)
        return ctx @ wo.T + bo

    def _L2_ffn_ref(x, ln1_w, ln2_w, wq, wk, wv, wo, router_w, w_gate, w_up, w_down):
        import jax, jax.numpy as jnp
        import numpy as np
        D = 128
        H = 16
        KV = 8
        HD = D // H
        M = 448
        E = 8
        TOPK = 2
        EPS = 1e-06
        ROPE_THETA = 10000.0

        def _rmsnorm(x, w, eps=EPS):
            xf = x.astype(jnp.float32)
            var = jnp.mean(xf * xf, axis=-1, keepdims=True)
            return (xf * jax.lax.rsqrt(var + eps)).astype(x.dtype) * w

        def _rope(q, k):
            S = q.shape[1]
            inv_freq = 1.0 / ROPE_THETA ** (jnp.arange(0, HD, 2, dtype=jnp.float32) / HD)
            ang = jnp.arange(S, dtype=jnp.float32)[:, None] * inv_freq[None, :]
            cos = jnp.concatenate([jnp.cos(ang), jnp.cos(ang)], axis=-1)[None, :, None, :]
            sin = jnp.concatenate([jnp.sin(ang), jnp.sin(ang)], axis=-1)[None, :, None, :]

            def rot_half(t):
                t1, t2 = jnp.split(t, 2, axis=-1)
                return jnp.concatenate([-t2, t1], axis=-1)
            return (q * cos + rot_half(q) * sin, k * cos + rot_half(k) * sin)
        B, S, _ = x.shape
        h = _rmsnorm(x, ln1_w)
        q = (h @ wq).reshape(B, S, H, HD)
        k = (h @ wk).reshape(B, S, KV, HD)
        v = (h @ wv).reshape(B, S, KV, HD)
        q, k = _rope(q, k)
        rep = H // KV
        k = jnp.repeat(k, rep, axis=2)
        v = jnp.repeat(v, rep, axis=2)
        scores = jnp.einsum('bqhd,bkhd->bhqk', q, k) / jnp.sqrt(jnp.float32(HD))
        causal = jnp.tril(jnp.ones((S, S), bool))
        scores = jnp.where(causal[None, None], scores, jnp.finfo(scores.dtype).min)
        attn = jax.nn.softmax(scores, axis=-1)
        ao = jnp.einsum('bhqk,bkhd->bqhd', attn, v).reshape(B, S, H * HD)
        x = x + ao @ wo
        h = _rmsnorm(x, ln2_w)
        logits = h @ router_w
        probs = jax.nn.softmax(logits, axis=-1)
        topv, topi = jax.lax.top_k(probs, TOPK)
        topv = topv / jnp.sum(topv, axis=-1, keepdims=True)
        weights = jnp.sum(jax.nn.one_hot(topi, E, dtype=h.dtype) * topv[..., None], axis=-2)
        gate = jnp.einsum('bsd,edm->bsem', h, w_gate)
        up = jnp.einsum('bsd,edm->bsem', h, w_up)
        act = jax.nn.silu(gate) * up * weights[..., None]
        moe = jnp.einsum('bsem,emd->bsd', act, w_down)
        return x + moe

    def _L3_attn_ref(x, A_log, WB, WC, D, Wg, bg, Wout, bout, gamma, beta):
        import jax, jax.numpy as jnp
        import numpy as np
        B, T, H, S = (4, 512, 128, 64)
        LN_EPS = 1e-05

        def _reference_tuple_inner(x, A_log, WB, WC, D, Wg, bg, Wout, bout, gamma, beta):
            A = jnp.exp(A_log)
            gate = jax.nn.sigmoid(jnp.einsum('bth,sh->bts', x, Wg) + bg)
            Bx = jnp.einsum('bth,sh->bts', x, WB)
            u = gate * Bx

            def step(state, u_t):
                state = A * state + u_t
                return (state, state)
            s0 = jnp.zeros((x.shape[0], A.shape[0]), x.dtype)
            final_state, states = jax.lax.scan(step, s0, jnp.swapaxes(u, 0, 1))
            states = jnp.swapaxes(states, 0, 1)
            y = jnp.einsum('bts,hs->bth', states, WC) + D * x
            h = y + x
            mu = jnp.mean(h, axis=-1, keepdims=True)
            var = jnp.mean(jnp.square(h - mu), axis=-1, keepdims=True)
            hn = (h - mu) * jax.lax.rsqrt(var + LN_EPS) * gamma + beta
            out = jnp.einsum('bth,oh->bto', hn, Wout) + bout
            return (out, final_state)
        return _reference_tuple_inner(x, A_log, WB, WC, D, Wg, bg, Wout, bout, gamma, beta)[0]

    def _L3_xattn_ref(x, w1, w2):
        import jax, jax.numpy as jnp
        import numpy as np
        E, T, H, F = (8, 256, 128, 512)
        h = jnp.einsum('eth,efh->etf', x, w1)
        a = jax.nn.gelu(h, approximate=True)
        return jnp.einsum('etf,efh->eth', a, w2)

    def _L3_ffn_ref(hidden_states, router_w, expert_bias, w_gate, w_down, w_gate_shared, w_down_shared):
        import jax, jax.numpy as jnp
        import numpy as np
        NUM_EXPERTS = 160
        TOP_K = 8
        ROUTED_SCALE = 2.5
        HIDDEN = 128
        INTER = 64
        B, S, H = hidden_states.shape
        x = hidden_states.reshape(-1, H)
        T = x.shape[0]
        logits = x @ router_w.T + expert_bias[None, :]
        probs = jax.nn.sigmoid(logits)
        top_w, top_idx = jax.lax.top_k(probs, TOP_K)
        top_w = top_w / (jnp.sum(top_w, axis=-1, keepdims=True) + 1e-09)
        top_w = top_w * ROUTED_SCALE
        combine = jnp.zeros((T, NUM_EXPERTS), dtype=x.dtype)
        combine = combine.at[jnp.arange(T)[:, None], top_idx].set(top_w)
        h1 = jax.nn.silu(jnp.einsum('th,eih->eti', x, w_gate))
        h1w = h1 * combine.T[:, :, None]
        routed = jnp.einsum('eti,ehi->th', h1w, w_down)
        shared = jax.nn.silu(x @ w_gate_shared.T) @ w_down_shared.T
        return (routed + shared).reshape(B, S, H)
    x = _layernorm(x + _L0_attn_ref(x, L0_attn_Wk, L0_attn_Wv, L0_attn_Wr, L0_attn_time_decay, L0_attn_time_first), axis=-1)
    x = _layernorm(x + _L0_xattn_ref(ctx_1024, x, L0_xattn_gamma_media, L0_xattn_beta_media, L0_xattn_gamma_lat, L0_xattn_beta_lat, L0_xattn_Wq, L0_xattn_bq, L0_xattn_Wkv, L0_xattn_bkv, L0_xattn_Wo, L0_xattn_bo), axis=-1)
    x = _layernorm(x + _L0_ffn_ref(x, L0_ffn_router_w, L0_ffn_w13, L0_ffn_w2), axis=-1)
    x = _layernorm(x + _L1_attn_ref(x, L1_attn_rot_w, L1_attn_scale, L1_attn_bias), axis=-1)
    x = _layernorm(x + _L1_xattn_ref(x, ctx_1024, ctx_1024, mask_Bx1xSxS2_bk1, L1_xattn_Wq, L1_xattn_bq, L1_xattn_Wk, L1_xattn_bk, L1_xattn_Wv, L1_xattn_bv, L1_xattn_Wo, L1_xattn_bo), axis=-1)
    x = _layernorm(x + _L1_ffn_ref(x, L1_ffn_w_gate, L1_ffn_w_up, L1_ffn_w_down), axis=-1)
    x = _layernorm(x + _L2_attn_ref(x, L2_attn_mix_k, L2_attn_mix_v, L2_attn_mix_r, L2_attn_W_key, L2_attn_W_value, L2_attn_W_receptance, L2_attn_W_output, L2_attn_time_decay, L2_attn_time_first), axis=-1)
    x = _layernorm(x + _L2_xattn_ref(x, ctx_1024, L2_xattn_wq, L2_xattn_bq, L2_xattn_wk, L2_xattn_bk, L2_xattn_wv, L2_xattn_bv, L2_xattn_wo, L2_xattn_bo), axis=-1)
    x = _layernorm(x + _L2_ffn_ref(x, L2_ffn_ln1_w, L2_ffn_ln2_w, L2_ffn_wq, L2_ffn_wk, L2_ffn_wv, L2_ffn_wo, L2_ffn_router_w, L2_ffn_w_gate, L2_ffn_w_up, L2_ffn_w_down), axis=-1)
    x = _layernorm(x + _L3_attn_ref(x, L3_attn_A_log, L3_attn_WB, L3_attn_WC, L3_attn_D, L3_attn_Wg, L3_attn_bg, L3_attn_Wout, L3_attn_bout, L3_attn_gamma, L3_attn_beta), axis=-1)
    x = _layernorm(x + _L3_xattn_ref(x, ctx_1024, ctx_1024), axis=-1)
    x = _layernorm(x + _L3_ffn_ref(x, L3_ffn_router_w, L3_ffn_expert_bias, L3_ffn_w_gate, L3_ffn_w_down, L3_ffn_w_gate_shared, L3_ffn_w_down_shared), axis=-1)
    return x

_drawn_inputs = setup_inputs


def setup_inputs(seed=0):
    import zlib

    import numpy as np

    out = dict(_drawn_inputs(seed))
    spreads = {'L0_attn_time_decay': (0.0, 0.1),
     'L0_attn_time_first': (0.0, 0.1),
     'L0_xattn_gamma_media': (1.0, 0.2),
     'L0_xattn_beta_media': (0.0, 0.1),
     'L0_xattn_gamma_lat': (1.0, 0.2),
     'L0_xattn_beta_lat': (0.0, 0.1),
     'L0_xattn_bq': (0.0, 0.1),
     'L0_xattn_bkv': (0.0, 0.1),
     'L0_xattn_bo': (0.0, 0.1),
     'L1_xattn_bq': (0.0, 0.1),
     'L1_xattn_bk': (0.0, 0.1),
     'L1_xattn_bv': (0.0, 0.1),
     'L1_xattn_bo': (0.0, 0.1),
     'L2_xattn_bq': (0.0, 0.1),
     'L2_xattn_bk': (0.0, 0.1),
     'L2_xattn_bv': (0.0, 0.1),
     'L2_xattn_bo': (0.0, 0.1),
     'L2_ffn_ln1_w': (1.0, 0.2),
     'L2_ffn_ln2_w': (1.0, 0.2),
     'L3_attn_gamma': (1.0, 0.2),
     'L3_attn_beta': (0.0, 0.1),
     'L3_ffn_expert_bias': (0.0, 0.1)}
    factors = {}
    for name, (base, spread) in spreads.items():
        noise = np.random.default_rng([zlib.crc32(name.encode()), seed]).standard_normal(out[name].shape)
        drawn = base * np.exp(spread * noise) if base else spread * noise
        out[name] = jnp.asarray(drawn.astype(out[name].dtype))
    for name, factor in factors.items():
        out[name] = (out[name] * factor).astype(out[name].dtype)
    return out
```

```python
from contextlib import ExitStack

import concourse.bass as bass
from concourse import mybir

F32 = mybir.dt.float32
BF16 = mybir.dt.bfloat16
U8 = mybir.dt.uint8
ALU = mybir.AluOpType
ACT = mybir.ActivationFunctionType
AX = mybir.AxisListType

P = 128
B = 8
T = B * P
HALF = T // 2
HB = B // 2
NH, HD = 16, 8
NG = 4
VA = HD + 1
XH = 8
E = 8
NE, TOPK = 160, 8
GROUPS, CHUNKS = 10, 8
SETS = 4
SETE = NE // SETS
EPS = 1e-5
ROUND = 1.5 * 2.0 ** 23
QMAX = 32767.0
NEG = -1e15

PACK = [
    ("center", P), ("mean", P), ("ident", P),
    ("l0_wk", P), ("l0_wr", P), ("l0_wv", P), ("l0_td", 1),
    ("x0_wq", XH * P), ("x0_wk", XH * P), ("x0_wv", XH * P), ("x0_wo", XH * P),
    ("x0_bq", XH), ("x0_bv", XH), ("x0_bo", 1), ("x0_gm", 1), ("x0_bm", 1), ("x0_gl", 1), ("x0_bl", 1),
    ("m0_router", E), ("before", E * E),
    ("l1_rc", 3), ("l1_rs", 3), ("l1_scale", 1), ("l1_bias", 1), ("swap", P),
    ("x1_wq", NG * P), ("x1_wk", NG * P), ("x1_wv", P), ("x1_wo", P),
    ("x1_bq", NG), ("x1_bk", NG), ("x1_bv", 1), ("x1_bo", 1),
    ("f1_gate", 3 * P), ("f1_up", 3 * P), ("f1_down", 3 * P),
    ("l2_mk", 1), ("l2_mv", 1), ("l2_mr", 1), ("l2_td", 1), ("l2_tf", 1),
    ("l2_wk", P), ("l2_wv", P), ("l2_wr", P), ("l2_wo", P), ("headsum", P),
    ("x2_wq", NG * P), ("x2_wk", NG * P), ("x2_wv", P), ("x2_wo", P),
    ("x2_bq", NG), ("x2_bk", NG), ("x2_bv", 1), ("x2_bo", 1),
    ("f2_ln1", 1), ("f2_ln2", 1), ("f2_wq", NG * P), ("f2_wqr", NG * P), ("f2_wk", NG * P), ("f2_wkr", NG * P),
    ("f2_wv", P), ("f2_wo", P), ("m2_router", E), ("cos", P), ("sin", P),
    ("l3_alog", 1), ("l3_bg", 1), ("l3_d", 1), ("l3_bout", 1), ("l3_gamma", 1), ("l3_beta", 1),
    ("l3_wb", 64), ("l3_wg", 64), ("l3_wc", P), ("l3_wout", P),
    ("m3_router", NE), ("m3_sgate", 64), ("m3_sdown", P), ("m3_bias", NE),
]
PACK_AT = {}
PACK_COLS = 0
for _name, _cols in PACK:
    PACK_AT[_name] = (PACK_COLS, _cols)
    PACK_COLS += _cols
PIECES = ["l0_wk", "x0_wq", "m0_router", "x1_wq", "l2_mk", "f2_ln1", None]
PIECE_ENDS = [PACK_AT[n][0] if n else PACK_COLS for n in PIECES]

M0_CH, M0_ROWS = 2, 128
M2_CH, M2_ROWS = 4, 112
LAYERS = 12


def program(nc, xT_in, ctxT_in, ctx_in, mask_in, pack_in, sel8_in, sel160_in, caus_in, identb_in,
            m0_up_in, m0_down_in, m2_up_in, m2_down_in, m3_in, out):
    ctx = ExitStack()
    with ctx:
        def sb(name, shape, dt=F32):
            return ctx.enter_context(nc.sbuf_tensor(name, shape, dt))

        sems = {}

        def S(name):
            if name not in sems:
                sems[name] = ctx.enter_context(nc.semaphore(name))
            return sems[name]

        ps = ctx.enter_context(nc.psum_tensor("ps", [P, 8, 512], F32))

        pack = sb("pack", [P, PACK_COLS])

        def W(name, lo=0, n=None):
            at, cols = PACK_AT[name]
            return pack[:, at + lo:at + (cols if n is None else lo + n)]

        xT = sb("xT", [P, T])
        ctxT = sb("ctxT", [P, T])
        ctx_tm = sb("ctx_tm", [P, T])
        mask8 = sb("mask8", [P, T], U8)
        maskb = sb("maskb", [P, T], BF16)
        caus = sb("caus", [P, P], BF16)
        identb = sb("identb", [P, P], BF16)
        sel8 = sb("sel8", [P, E * P], BF16)
        sel160 = sb("sel160", [P, 20 * P], BF16)
        hsum = sb("hsum", [P, T])
        sq = sb("sq", [P, T])
        rstd = sb("rstd", [P, T])
        small = sb("small", [P, 64])
        eps5 = small[:, 0:1]
        eps6 = small[:, 1:2]
        ring = sb("ring", [P, 2, 1408])
        arena = sb("arena", [P, 22600])

        def A(lo, *shape):
            n = 1
            for s in shape:
                n *= s
            v = arena[:, lo:lo + n]
            if len(shape) == 2:
                v = v.rearrange("p (a b) -> p a b", a=shape[0])
            elif len(shape) == 3:
                v = v.rearrange("p (a b c) -> p a b c", a=shape[0], b=shape[1])
            elif len(shape) == 4:
                v = v.rearrange("p (a b c d) -> p a b c d", a=shape[0], b=shape[1], c=shape[2])
            return v

        def half(buf, p):
            return buf[:, p * HALF:(p + 1) * HALF]

        def bank(n):
            return ps[:, n, :]

        ident = W("ident")

        def linked(eng, name):
            count = [0]

            def link(ins):
                count[0] += 1
                ins.then_inc(S(name), 1)
                eng.wait_ge(S(name), count[0])
            return link

        def piece(eng, name):
            n = next(i for i, e in enumerate(PIECE_ENDS) if PACK_AT[name][0] < e)
            eng.wait_ge(S(f"pack_{n}"), 16)

        block = ctx.enter_context(nc.Block())

        NORMS = ["ctx", "0", "lat", "1", "2", "3", "4", "5", "6", "7", "rms1", "rms2", "8", "inner", "9", "10", "11"]

        def nth(tag, p):
            return 2 * NORMS.index(tag) + p + 1

        def wait_x(eng, l, p=1):
            if l == 0:
                eng.wait_ge(S("x_loaded"), 16)
            else:
                eng.wait_ge(S("x_ready"), 2 * (l - 1) + p + 1)


        def norm_tensor(pe, tag, src, ready):
            for p in range(2):
                ready(p)
                nc.tensor.matmul(bank(2 + p), W("center"), half(src, p), start=True, stop=True).then_inc(S("norm_d"), 1)
            norm_mean(pe, tag)

        def norm_mean(pe, tag):
            for p in range(2):
                pe.wait_ge(S("norm_sq"), nth(tag, p))
                nc.tensor.matmul(bank(4 + p), W("mean"), half(sq, p), start=True, stop=True).then_inc(S("norm_var"), 1)

        def norm_scalar(act, tag, eps=None, src=None, root=False):
            for p in range(2):
                if src is None:
                    act.wait_ge(S("norm_d"), nd(tag, p))
                nc.scalar.activation(half(sq, p), bank(2 + p) if src is None else half(src, p),
                                     ACT.Square).then_inc(S("norm_sq"), 1)
            for p in range(2):
                act.wait_ge(S("norm_var"), nth(tag, p))
                if root:
                    nc.scalar.activation(half(rstd, p), bank(4 + p), ACT.Sqrt, bias=eps5).then_inc(S("norm_root"), 1)
                    act.wait_ge(S("norm_root"), p + 1)
                    nc.scalar.activation(half(rstd, p), half(rstd, p), ACT.Ln).then_inc(S("norm_ln"), 1)
                    act.wait_ge(S("norm_ln"), nth(tag, p))
                    nc.scalar.activation(half(rstd, p), half(rstd, p), ACT.Exp, scale=-1.0).then_inc(S("norm_rstd"), 1)
                    continue
                nc.scalar.activation(half(rstd, p), bank(4 + p), ACT.Ln, bias=eps5 if eps is None else eps).then_inc(S("norm_ln"), 1)
                act.wait_ge(S("norm_ln"), nth(tag, p))
                nc.scalar.activation(half(rstd, p), half(rstd, p), ACT.Exp, scale=-0.5).then_inc(S("norm_rstd"), 1)

        def nd(tag, p):
            n = NORMS.index(tag)
            return 2 * (n - sum(NORMS.index(r) < n for r in ("rms1", "rms2"))) + p + 1

        def residual_norm_tensor(pe, l):
            def ready(p):
                pe.wait_ge(S("sum_ready"), 2 * l + p + 1)
            norm_tensor(pe, str(l), hsum, ready)

        def residual_norm_vector(dve, l, bias=None, res=None):
            for p in range(2):
                dve.wait_ge(S("y_ready"), 2 * l + p + 1)
                nc.vector.scalar_tensor_tensor(out=half(hsum, p), in0=bank(p), scalar=0.0 if bias is None else bias,
                                               in1=half(xT if res is None else res, p),
                                               op0=ALU.add, op1=ALU.add).then_inc(S("sum_ready"), 1)
            for p in range(2):
                dve.wait_ge(S("norm_rstd"), nth(str(l), p))
                nc.vector.tensor_tensor(half(xT, p), bank(2 + p), half(rstd, p), ALU.mult).then_inc(S("x_ready"), 1)

        x_q = A(0, XH, T)
        x_kv = A(8192, B, 2, P)
        x_kvt = A(10240, B, 2, P)
        x_m = A(12288, XH, P)
        x_u = A(13312, XH, P)
        x_c = A(14336, XH)
        x_qs = A(14400, 2, XH, P)
        x_kvs = A(16448, 2, 2, P)
        x_kvts = A(16960, 2, 2, P)
        x_p = A(17472, 2, 4, 2 * P)
        x_pt = A(19520, 2, 2, 512)
        x_nm = A(21568, 2, 4)
        x_sum = A(21576, 2, 4)
        x_rec = A(21584, 2, 4)
        x_bo = A(21592, 1)

        a_q = A(0, NG, T)
        a_k = A(4096, NG, T)
        a_v = A(8192, B, NH, VA)
        a_vflat = A(8192, B * NH * VA)
        a_qs = A(9344, 2, NG, P)
        a_ks = A(10368, 2, NG, P)
        a_p = A(11392, 2, NH // 2, P)
        a_pt = A(13440, 2, NH // 2, P)
        a_cn = A(15488, 2, P)
        a_oT = A(15744, T)
        a_mx = A(16768, 2, NH // 2)
        a_rec = A(16784, 2, NH)
        a_t1 = A(16816, 2, HALF)
        a_t2 = A(17840, 2, HALF)
        f_h = A(18864, T)
        f_x2 = A(6528, T)
        f_res = A(19888, T)

        m_lg = A(0, B, E)
        m_e = A(64, B, E)
        m_mx = A(128, B)
        m_gt = A(192, B, E, E)
        m_eq = A(704, B, E, E)
        m_rank = A(1216, B, E)
        m_w = A(1280, B, E)
        m_s = A(1344, B)
        m_z = A(1352, B)
        m_d = A(1360, B)
        m_parts = A(1408, B * P // 2).bitcast(BF16).rearrange("p (b c) -> p b c", b=B)
        m_wT = A(1920, T // 2).bitcast(BF16)
        m_xw = A(2432, 2, T)
        m_sg = A(4480, 2, HALF)
        m_hid = A(5504, 2, HALF)
        zeros = sb("zeros", [P, HALF], BF16)
        m_x2 = A(20912, T)

        g_c = small[:, 8:11]
        g_s = small[:, 11:14]
        g_n = small[:, 14:17]
        g_n2 = small[:, 17:20]
        g_a = small[:, 20:21]
        g_b = small[:, 21:22]
        g_rot = A(0, 3, P)
        g_t = A(384, 3, P)
        g_q = A(768, T)
        g_k = A(1792, T)
        g_v = A(2816, B, P)
        g_z = A(3840, B, P)
        g_pt = A(4864, B, P)
        g_av = A(5888, B, P)
        g_sq = A(6912, B, P)
        g_mx = A(7936, B)
        g_sm = A(7944, B)
        g_rc = A(7952, B)
        g_in = A(7960, B)

        q_ab = A(0, 36)
        q_sc = A(36, 36)
        q_inv = A(72, 36)
        q_w = A(128, 36, 32)
        q_wT = A(1280, 9, P)
        q_x = A(2432, T)
        q_up = A(3456, 3 * T)
        q_gate = A(6528, 3 * T)
        q_sig = A(9600, 3 * T)
        q_col = small[:, 24:29]
        q_s = small[:, 32:37]
        q_i = small[:, 40:45]
        ones1 = sb("ones1", [1, P])
        q_top = sb("q_top", [1, 8])

        r_prev = A(0, B, P)
        r_diff = A(1024, T)
        r_k = A(2048, T)
        r_v = A(3072, T)
        r_r = A(4096, T)
        r_ek = A(5120, T)
        r_ekv = A(6144, T)
        r_sa = A(7168, B, P + 1)
        r_sb = A(8200, B, P + 1)
        r_den = A(9232, T)
        r_sig = A(10256, T)
        r_dec = small[:, 48:49]
        r_u = small[:, 49:50]
        r_e = small[:, 50:51]

        s_sig = A(0, T)
        s_u = A(1024, T)
        s_st = A(2048, T)
        s_h = A(3072, T)
        s_hn = A(4096, T)
        s_a = small[:, 51:52]

        d_r = A(0, T)
        d_s = A(1024, T)
        d_w = small[:, 52:53]
        d_e = small[:, 53:54]

        e_a = A(0, T)

        t_p = A(0, B, NE)
        t_rep = A(1280, B, NE)
        t_top = A(2560, B, TOPK)
        t_s = A(2624, B)
        t_w = A(2688, B, NE)
        t_r1 = A(3968, B, NE)
        t_parts = A(5248, B * SETS * P // 2).bitcast(BF16).rearrange("p (b s c) -> p b s c", b=B, s=SETS)
        t_combT = A(7296, SETS * T // 2).bitcast(BF16).rearrange("p (s t) -> p s t", s=SETS)
        t_sg = A(9344, 2, HALF)
        t_hid = A(10368, 2, HALF)
        t_sh = A(11392, T)

        def bankb(n):
            return ps[:, n, :].bitcast(BF16)

        CREDIT = {"a_z", "a_ptA", "a_ptB", "a_oT", "a_turned", "m_hid"}

        def credited(eng, *names):
            for name in names:
                eng.sem_inc(S(name), 1)

        WAVES, UNITS = 2 * B, (E * 2 * M0_CH, E * 2 * M2_CH)
        LEFT = {"a_proj": 8, "a_q_ready": 8, "a_k_ready": 8, "a_vproj": 1, "a_v_ready": 1, "a_ones": 1, "a_slices": 2 * B,
                "a_scores": WAVES, "a_mx": WAVES, "a_z": WAVES, "a_p": WAVES, "a_turned": WAVES, "a_ptA": WAVES, "a_ptB": WAVES,
                "a_weighed": WAVES, "a_rec": B, "a_cn": B, "a_oturned": B, "a_oT": B,
                "a_rope_used": 0, "a_rope_part": 0, "a_rope_sum": 0,
                "m_logits": 1, "m_lg": 1, "m_e": 1, "m_pad": 1, "m_parts": 3, "m_wturned": 1, "m_wT": 1, "m_spread": 2 * E, "m_xw": 2 * E,
                "m_gate": UNITS, "m_silu": UNITS, "m_up": UNITS, "m_hid": UNITS, "m_down": (UNITS[0] - 2, UNITS[1] - 2),
                "m_load0": 16 * E, "m_load1": 16 * E}
        RUN = {"x1": ("a", 0), "x2": ("a", 1), "f2": ("a", 2), "m0": ("m", 0), "m2": ("m", 1), "m3": ("m", 2)}

        def R(t, name):
            return S(RUN[t][0] + name)

        def waits(eng, t):
            kind, run = RUN[t]

            def before(name):
                left = LEFT[kind + name]
                return sum(left[0:run]) if isinstance(left, tuple) else run * left
            return lambda name, v: eng.wait_ge(S(kind + name), v + before(name) + (kind + name in CREDIT))

        def credited_once(eng, t, *names):
            if RUN[t][1] == 0:
                credited(eng, *(RUN[t][0] + name for name in names))


        def narrow_tensor(pe, t, qsrc, ksrc, rope, mask, wo, done="y_ready"):
            wait = waits(pe, t)
            mm = nc.tensor.matmul
            credited_once(pe, t, "_turned")
            for m in range(2 * NG):
                g, p = m // 2, m % 2
                cols = slice(g * P, (g + 1) * P)
                if rope:
                    if m >= 2:
                        wait("_rope_used", m - 1)
                    for k, name in enumerate(("_wq", "_wqr", "_wk", "_wkr")):
                        ins = mm(bank((4 * m + k) % 8), W(t + name)[:, cols], half(qsrc, p), start=True, stop=True)
                    ins.then_inc(R(t, "_proj"), 1)
                else:
                    if m >= 4:
                        wait("_q_ready", m - 3)
                        wait("_k_ready", m - 3)
                    mm(bank((2 * m) % 8), W(t + "_wq")[:, cols], half(qsrc, p), start=True, stop=True)
                    mm(bank((2 * m + 1) % 8), W(t + "_wk")[:, cols], half(ksrc, p), start=True, stop=True).then_inc(R(t, "_proj"), 1)
            if rope:
                wait("_rope_used", 2 * NG)
            else:
                wait("_q_ready", 2 * NG)
                wait("_k_ready", 2 * NG)
            for b in range(B):
                ins = mm(ps[:, b // HB, (b % HB) * P:(b % HB + 1) * P], ksrc[:, b * P:(b + 1) * P], W(t + "_wv"), start=True, stop=True)
            ins.then_inc(R(t, "_vproj"), 1)
            wait("_v_ready", 1)

            def scores(b, v, w, slot):
                if v == 0:
                    wait("_slices", 2 * b + 2)
                wait("_z", w - 1) if not isinstance(w, int) or w >= 2 else None
                for jj in range(2):
                    j = 2 * v + jj
                    sbank = 2 * v + jj
                    if mask is not None:
                        rows = mask if mask is caus else mask[:, bass.ds(b * P, P)]
                        mm(bank(sbank), identb[:, :], (rows[:, :] if mask is caus else rows).unsqueeze(1).to_broadcast([P, NG, P]),
                           start=True, stop=False, skip_group_check=True)
                    for g in range(NG):
                        ins = mm(ps[:, sbank, g * P:(g + 1) * P], a_qs[32 * j:32 * j + 32, slot, g, :],
                                 a_ks[32 * j:32 * j + 32, slot, g, :], start=mask is None, stop=True, skip_group_check=True)
                ins.then_inc(R(t, "_scores"), 1)

            def turn(b, v, w):
                wait("_p", w + 1)
                wait("_ptA", w)
                wait("_ptB", w)
                for n in range(NH // 2):
                    ins = nc.tensor.transpose(ps[:, 4 + n // 4, (n % 4) * P:(n % 4 + 1) * P], a_p[:, v, n, :], ident)
                ins.then_inc(R(t, "_turned"), 1)

            def weigh(b, v, w, slot):
                wait("_ptA", w + 1)
                wait("_ptB", w + 1)
                for n in range(NH // 2):
                    h = NH // 2 * v + n
                    ins = mm(ps[:, 6, slot * 256 + h * VA:slot * 256 + (h + 1) * VA], a_pt[:, v, n, :],
                             a_vflat[:, bass.ds(b * (NH * VA) + h * VA, VA)], start=True, stop=True, skip_group_check=True)
                ins.then_inc(R(t, "_weighed"), 1)

            def turn_out(b, slot):
                wait("_cn", b + 1)
                wait("_oT", b)
                nc.tensor.transpose(ps[:, 7, slot * P:(slot + 1) * P], a_cn[:, slot, :], ident).then_inc(R(t, "_oturned"), 1)

            def body(i, final):
                for k in range(4):
                    b, v, w = 2 * i + k // 2, k % 2, 4 * i + k
                    if not (final and k == 3):
                        scores(2 * i + (k + 1) // 2, (k + 1) % 2, w + 1, (k + 1) // 2 % 2)
                    turn(b, v, w)
                    weigh(b, v, w, k // 2)
                    if k == 2:
                        turn_out(2 * i, 0)
                turn_out(2 * i + 1, 1)

            scores(0, 0, 0, 0)
            with pe.Fori(0, B // 2 - 1) as i:
                body(i, False)
            body(B // 2 - 1, True)
            for p in range(2):
                wait("_oT", B)
                mm(bank(p), wo, half(a_oT, p), start=True, stop=True).then_inc(S(done), 1)

        def narrow_scalar(act, t, rope, bv, scale, bq=None):
            wait = waits(act, t)
            credited_once(act, t, "_ptA", "_oT")
            if not rope:
                for m in range(2 * NG):
                    g, p = m // 2, m % 2
                    wait("_proj", m + 1)
                    nc.scalar.activation(half(a_q[:, g, :], p), bank((2 * m) % 8), ACT.Identity,
                                         bias=bq[:, g:g + 1]).then_inc(R(t, "_q_ready"), 1)

            def exps(v, w):
                wait("_z", w + 1)
                nc.scalar.activation(a_p[:, v], a_p[:, v], ACT.Exp, scale=scale).then_inc(R(t, "_p"), 1)

            def copies(v, w):
                wait("_turned", w + 1)
                nc.scalar.activation(a_pt[:, v, 0:4, :], ps[:, 4, :].rearrange("p (n q) -> p n q", n=4), ACT.Copy).then_inc(R(t, "_ptA"), 1)

            def out(b, slot):
                wait("_oturned", b + 1)
                if bv is None:
                    nc.scalar.activation(a_oT[:, bass.ds(b * P, P)], ps[:, 7, slot * P:(slot + 1) * P], ACT.Copy).then_inc(R(t, "_oT"), 1)
                else:
                    nc.scalar.activation(a_oT[:, bass.ds(b * P, P)], ps[:, 7, slot * P:(slot + 1) * P], ACT.Identity,
                                         bias=bv).then_inc(R(t, "_oT"), 1)

            def body(i, final):
                for k in range(4):
                    w = 4 * i + k
                    if not (final and k == 3):
                        exps((k + 1) % 2, w + 1)
                    copies(k % 2, w)
                    if k == 2:
                        out(2 * i, 0)
                out(2 * i + 1, 1)

            exps(0, 0)
            with act.Fori(0, B // 2 - 1) as i:
                body(i, False)
            body(B // 2 - 1, True)

        def narrow_vector(dve, t, rope, bk=None):
            wait = waits(dve, t)
            credited_once(dve, t, "_z", "_ptB")
            for m in range(2 * NG):
                g, p = m // 2, m % 2
                wait("_proj", m + 1)
                if rope:
                    if m >= 1:
                        wait("_rope_sum", 2 * m)
                    for k, (tab, dst) in enumerate((("cos", a_t1[:, 0]), ("sin", a_t1[:, 1]), ("cos", a_t2[:, 0]), ("sin", a_t2[:, 1]))):
                        nc.vector.tensor_tensor(dst.rearrange("p (b t) -> p b t", b=HB),
                                                bank((4 * m + k) % 8).rearrange("p (b t) -> p b t", b=HB),
                                                W(tab).unsqueeze(1).to_broadcast([P, HB, P]), ALU.mult).then_inc(R(t, "_rope_used" if k == 3 else "_rope_part"), 1)
                else:
                    nc.vector.tensor_scalar(half(a_k[:, g, :], p), bank((2 * m + 1) % 8), bk[:, g:g + 1], None,
                                            ALU.add).then_inc(R(t, "_k_ready"), 1)
            wait("_vproj", 1)
            wait("_ones", 1)
            for p in range(2):
                ins = nc.vector.tensor_copy(a_v[:, HB * p:HB * (p + 1), :, 0:HD].rearrange("p b h d -> p (b h) d"),
                                            bank(p).rearrange("p (n d) -> p n d", d=HD))
            ins.then_inc(R(t, "_v_ready"), 1)

            def maxima(v, w):
                wait("_scores", w + 1)
                sc = ps[:, 2 * v:2 * v + 2, :].rearrange("p a (g k) -> p (a g) k", g=NG)
                nc.vector.tensor_reduce(a_mx[:, v], sc, AX.X, ALU.max).then_inc(R(t, "_mx"), 1)
                wait("_mx", w + 1)
                wait("_turned", w - 1) if not isinstance(w, int) or w >= 2 else None
                nc.vector.tensor_tensor(a_p[:, v], sc, a_mx[:, v].unsqueeze(2).to_broadcast([P, NH // 2, P]),
                                        ALU.subtract).then_inc(R(t, "_z"), 1)

            def copies(v, w):
                wait("_turned", w + 1)
                nc.vector.tensor_copy(a_pt[:, v, 4:8, :], ps[:, 5, :].rearrange("p (n q) -> p n q", n=4)).then_inc(R(t, "_ptB"), 1)

            def outputs(b, slot):
                wait("_weighed", 2 * b + 2)
                o = ps[:, 6, slot * 256:slot * 256 + NH * VA].rearrange("p (h d) -> p h d", d=VA)
                nc.vector.reciprocal(a_rec[:, slot], o[:, :, HD]).then_inc(R(t, "_rec"), 1)
                wait("_rec", b + 1)
                nc.vector.tensor_tensor(a_cn[:, slot].rearrange("p (h d) -> p h d", d=HD), o[:, :, 0:HD],
                                        a_rec[:, slot].unsqueeze(2).to_broadcast([P, NH, HD]), ALU.mult).then_inc(R(t, "_cn"), 1)

            def body(i, final):
                for k in range(4):
                    w = 4 * i + k
                    if not (final and k == 3):
                        maxima((k + 1) % 2, w + 1)
                    copies(k % 2, w)
                    if k % 2 == 1:
                        outputs(2 * i + k // 2, k // 2)

            maxima(0, 0)
            with dve.Fori(0, B // 2 - 1) as i:
                body(i, False)
            body(B // 2 - 1, True)

        def narrow_gpsimd(pool, t, rope, before):
            wait = waits(pool, t)
            before()
            nc.gpsimd.memset(a_v[:, :, :, HD], 1.0).then_inc(R(t, "_ones"), 1)
            if rope:
                for m in range(2 * NG):
                    g, p = m // 2, m % 2
                    wait("_rope_used", m + 1)
                    wait("_rope_part", 3 * m + 3)
                    nc.gpsimd.tensor_tensor(half(a_q[:, g, :], p), a_t1[:, 0], a_t1[:, 1], ALU.add).then_inc(R(t, "_rope_sum"), 1)
                    nc.gpsimd.tensor_tensor(half(a_k[:, g, :], p), a_t2[:, 0], a_t2[:, 1], ALU.add).then_inc(R(t, "_rope_sum"), 1)
                wait("_rope_sum", 4 * NG)
            else:
                wait("_q_ready", 2 * NG)
                wait("_k_ready", 2 * NG)

            def slices(b, slot):
                nc.gpsimd.tensor_copy(a_qs[:, slot], a_q[:, :, bass.ds(b * P, P)]).then_inc(R(t, "_slices"), 1)
                nc.gpsimd.tensor_copy(a_ks[:, slot], a_k[:, :, bass.ds(b * P, P)]).then_inc(R(t, "_slices"), 1)

            slices(0, 0)
            slices(1, 1)
            with pool.Fori(1, B // 2) as i:
                for slot in range(2):
                    wait("_scores", 4 * i + 2 * slot - 2)
                    slices(2 * i + slot, slot)


        def route_tensor(pe, t, src):
            for b in range(B):
                ins = nc.tensor.matmul(ps[:, 2, b * E:(b + 1) * E], src[:, b * P:(b + 1) * P], W(t + "_router"),
                                       start=True, stop=True, skip_group_check=True)
            ins.then_inc(R(t, "_logits"), 1)
            waits(pe, t)("_parts", 3)
            waits(pe, t)("_pad", 1)
            for b in range(B):
                ins = nc.tensor.transpose(bankb(3)[:, b * P:(b + 1) * P], m_parts[:, b, :], identb[:, :])
            ins.then_inc(R(t, "_wturned"), 1)

        def route_scalar(act, t):
            waits(act, t)("_lg", 1)
            nc.scalar.activation(m_e[:, :, :], m_lg[:, :, :], ACT.Exp).then_inc(R(t, "_e"), 1)

        def route_vector(dve, t, zterm, link):
            V = nc.vector
            piece(dve, "before")
            waits(dve, t)("_logits", 1)
            lg = ps[:, 2, 0:B * E].rearrange("p (b e) -> p b e", b=B)
            link(V.tensor_reduce(m_mx, lg, AX.X, ALU.max))
            V.tensor_tensor(m_lg, lg, m_mx.unsqueeze(2).to_broadcast([P, B, E]), ALU.subtract).then_inc(R(t, "_lg"), 1)
            waits(dve, t)("_e", 1)
            mine = m_e.unsqueeze(3).to_broadcast([P, B, E, E])
            other = m_e.unsqueeze(2).to_broadcast([P, B, E, E])
            before = W("before").rearrange("p (a c) -> p a c", a=E).unsqueeze(1).to_broadcast([P, B, E, E])
            link(V.tensor_tensor(m_eq, other, mine, ALU.is_equal))
            link(V.tensor_tensor(m_eq, m_eq, before, ALU.mult))
            link(V.tensor_tensor(m_gt, other, mine, ALU.is_gt))
            link(V.tensor_tensor(m_gt, m_gt, m_eq, ALU.add))
            link(V.tensor_reduce(m_rank, m_gt, AX.X, ALU.add))
            if zterm:
                link(V.tensor_reduce(m_z, m_e, AX.X, ALU.add))
            link(V.scalar_tensor_tensor(out=m_w, in0=m_rank, scalar=1.5, in1=m_e, op0=ALU.is_lt, op1=ALU.mult))
            link(V.tensor_reduce(m_s, m_w, AX.X, ALU.add))
            if zterm:
                link(V.scalar_tensor_tensor(out=m_s, in0=m_z, scalar=zterm, in1=m_s, op0=ALU.mult, op1=ALU.add))
            link(V.reciprocal(m_d, m_s))
            link(V.tensor_tensor(m_w, m_w, m_d.unsqueeze(2).to_broadcast([P, B, E]), ALU.mult))
            waits(dve, t)("_pad", 1)
            for k in range(3):
                part = m_parts[:, :, k:3 * E:3]
                ins = V.tensor_copy(part, m_w)
                ins.then_inc(R(t, "_parts"), 1)
                if k < 2:
                    waits(dve, t)("_parts", k + 1)
                    link(V.tensor_tensor(m_w, m_w, part, ALU.subtract))
            waits(dve, t)("_wturned", 1)
            V.tensor_copy(m_wT, bankb(3)).then_inc(R(t, "_wT"), 1)

        def mix_tensor(pe, t, src, CH, ROWS, l):
            wait = waits(pe, t)
            mm = nc.tensor.matmul
            UPE = 2 * CH
            wait("_wT", 1)
            pe.wait_ge(S("filled"), 4)
            for p in range(2):
                mm(bank(p), zeros[:, 0:P], zeros[:, :], start=True, stop=False, skip_group_check=True)

            def spread(e):
                for p in range(2):
                    wait("_xw", 2 * e + p - 1) if not isinstance(e, int) or e >= 1 else None
                    mm(bank(6 + p), sel8[:, bass.ds(e * P, P)], half(m_wT, p), start=True, stop=True).then_inc(R(t, "_spread"), 1)

            def up(e, slot, c, p, n):
                if c == 0 and p == 0:
                    wait(f"_load{slot}", 32 * ((e - slot) // 2 + 1) if isinstance(e, int) else 16 * (e - slot) + 32)
                wait("_hid", n - 1) if not isinstance(n, int) or n >= 2 else None
                mm(ps[0:ROWS, 2 + p, :], ring[:, slot, c * ROWS:(c + 1) * ROWS], half(src, p), start=True, stop=True).then_inc(R(t, "_gate"), 1)
                wait("_xw", 2 * e + p + 1)
                mm(ps[0:ROWS, 4 + p, :], ring[:, slot, (CH + c) * ROWS:(CH + c + 1) * ROWS], half(m_xw[:, slot], p),
                   start=True, stop=True).then_inc(R(t, "_up"), 1)

            def down(slot, c, p, n, final):
                wait("_hid", n + 1)
                at = 2 * CH * ROWS + c * P
                ins = mm(bank(p), ring[0:ROWS, slot, at:at + P], m_hid[0:ROWS, p], start=False, stop=final, skip_group_check=True)
                ins.then_inc(S("y_ready") if final else R(t, "_down"), 1)

            def body(i, last_pair):
                for slot in range(2):
                    e = 2 * i + slot
                    last_expert = last_pair and slot == 1
                    for u in range(UPE):
                        n = UPE * e + u
                        if u == UPE // 2 and not last_expert:
                            spread(e + 1)
                        if u < UPE - 1:
                            up(e, slot, (u + 1) // 2, (u + 1) % 2, n + 1)
                        elif not last_expert:
                            up(e + 1, 1 - slot, 0, 0, n + 1)
                        down(slot, u // 2, u % 2, n, last_expert and u >= UPE - 2)

            spread(0)
            up(0, 0, 0, 0, 0)
            with pe.Fori(0, E // 2 - 1) as i:
                body(i, False)
            body(E // 2 - 1, True)

        def mix_scalar(act, t, CH, ROWS):
            def unit(n, p):
                waits(act, t)("_gate", n + 1)
                nc.scalar.activation(m_sg[0:ROWS, p], ps[0:ROWS, 2 + p, :], ACT.Silu).then_inc(R(t, "_silu"), 1)
            with act.Fori(0, E * CH) as i:
                for p in range(2):
                    unit(2 * i + p, p)

        def mix_vector(dve, t, src, CH, ROWS):
            wait = waits(dve, t)
            UPE = 2 * CH
            credited_once(dve, t, "_hid")

            def weigh(e, slot):
                for p in range(2):
                    wait("_spread", 2 * e + p + 1)
                    nc.vector.tensor_tensor(half(m_xw[:, slot], p), half(src, p), bank(6 + p), ALU.mult).then_inc(R(t, "_xw"), 1)

            def hidden(n, p):
                wait("_silu", n + 1)
                wait("_up", n + 1)
                nc.vector.tensor_tensor(m_hid[0:ROWS, p], m_sg[0:ROWS, p], ps[0:ROWS, 4 + p, :], ALU.mult).then_inc(R(t, "_hid"), 1)

            def body(i, last_pair):
                for slot in range(2):
                    e = 2 * i + slot
                    for u in range(UPE):
                        hidden(UPE * e + u, u % 2)
                        if u == UPE // 2 and not (last_pair and slot == 1):
                            weigh(e + 1, 1 - slot)

            weigh(0, 0)
            with dve.Fori(0, E // 2 - 1) as i:
                body(i, False)
            body(E // 2 - 1, True)

        def mix_load(sp, t, up_in, down_in, CH, ROWS):
            UPE = 2 * CH

            def load(e, slot):
                sp.dma_start(ring[:, slot, 0:2 * CH * ROWS], up_in[bass.ds(e, 1), :, :].rearrange("e p n -> p (e n)")).then_inc(R(t, f"_load{slot}"), 16)
                sp.dma_start(ring[0:ROWS, slot, 2 * CH * ROWS:2 * CH * ROWS + CH * P],
                             down_in[bass.ds(e, 1), :, :].rearrange("e p n -> p (e n)")).then_inc(R(t, f"_load{slot}"), 16)

            load(0, 0)
            load(1, 1)
            with sp.Fori(1, E // 2) as i:
                for slot in range(2):
                    waits(sp, t)("_down", UPE * (2 * i + slot - 1))
                    load(2 * i + slot, slot)

        SCALE8 = HD ** -0.5

        @block.sync
        def _(sp):
            def load_piece(n):
                lo = PIECE_ENDS[n - 1] if n else 0
                sp.dma_start(pack[:, lo:PIECE_ENDS[n]], pack_in[:, lo:PIECE_ENDS[n]]).then_inc(S(f"pack_{n}"), 16)
            sp.dma_start(ctxT[:, :], ctxT_in).then_inc(S("ctx_loaded"), 16)
            load_piece(0)
            sp.dma_start(xT[:, :], xT_in).then_inc(S("x_loaded"), 16)
            load_piece(1)
            load_piece(2)
            sp.dma_start(identb[:, :], identb_in).then_inc(S("consts"), 16)
            sp.dma_start(sel8[:, :], sel8_in).then_inc(S("consts"), 16)
            sp.dma_start(caus[:, :], caus_in).then_inc(S("consts"), 16)
            sp.dma_start(sel160[:, :], sel160_in).then_inc(S("consts"), 16)
            load_piece(3)
            sp.dma_start(mask8[:, :], mask_in).then_inc(S("mask_loaded"), 16)
            for n in range(4, len(PIECES)):
                load_piece(n)
            sp.dma_start(ctx_tm[:, :], ctx_in).then_inc(S("ctxtm_loaded"), 16)
            mix_load(sp, "m0", m0_up_in, m0_down_in, M0_CH, M0_ROWS)
            sp.wait_ge(S("y_ready"), 6)
            mix_load(sp, "m2", m2_up_in, m2_down_in, M2_CH, M2_ROWS)
            sp.wait_ge(S("y_ready"), 18)

            def load(n, slot):
                sp.dma_start(ring[:, slot, 0:1024], m3_in[bass.ds(n, 1), :, :].rearrange("e p n -> p (e n)")).then_inc(R("m3", f"_load{slot}"), 16)
            load(0, 0)
            load(1, 1)
            with sp.Fori(1, GROUPS) as i:
                for slot in range(2):
                    waits(sp, "m3")("_down", 16 * i + 8 * slot - 8)
                    load(2 * i + slot, slot)
            for p in range(2):
                sp.wait_ge(S("x_ready"), 2 * (LAYERS - 1) + p + 1)
                sp.dma_start(half(out, p), half(xT, p)).then_inc(S("stored"), 16)
            sp.wait_ge(S("stored"), 32)

        @block.tensor
        def _(pe):
            mm = nc.tensor.matmul
            pe.wait_ge(S("pack_0"), 16)

            def ctx_ready(p):
                pe.wait_ge(S("ctx_loaded"), 16)
            norm_tensor(pe, "ctx", ctxT, ctx_ready)
            piece(pe, "l0_wk")
            wait_x(pe, 0)
            pe.wait_ge(S("norm_out"), 2)
            for p in range(2):
                mm(bank(2 + p), W("l0_wk"), half(xT, p), start=True, stop=True).then_inc(S("l0_k"), 1)
                mm(bank(4 + p), W("l0_wr"), half(xT, p), start=True, stop=True).then_inc(S("l0_r"), 1)
            piece(pe, "x0_wq")
            for h in range(XH):
                ins = mm(ps[:, 6 + h // 4, (h % 4) * P:(h % 4 + 1) * P], W("x0_wq", h * P, P), W("x0_wk", h * P, P),
                         start=True, stop=True, skip_group_check=True)
            ins.then_inc(S("x0_mw"), 1)
            pe.wait_ge(S("x0_m"), 1)
            for h in range(XH):
                ins = mm(ps[:, 6 + h // 4, (h % 4) * P:(h % 4 + 1) * P], W("x0_wv", h * P, P), W("x0_wo", h * P, P),
                         start=True, stop=True, skip_group_check=True)
            ins.then_inc(S("x0_uw"), 1)
            pe.wait_ge(S("x0_u"), 1)
            for h in range(XH):
                ins = mm(ps[:, 6, h:h + 1], W("x0_wk", h * P, P), W("x0_bq", h, 1), start=True, stop=True, skip_group_check=True)
            for h in range(XH):
                ins = mm(ps[:, 7, 0:1], W("x0_wo", h * P, P), W("x0_bv", h, 1), start=(h == 0), stop=(h == XH - 1), skip_group_check=True)
            ins.then_inc(S("x0_bw"), 1)
            for p in range(2):
                pe.wait_ge(S("l0_gated"), p + 1)
                mm(bank(p), W("l0_wv"), half(d_s, p), start=True, stop=True).then_inc(S("y_ready"), 1)
            residual_norm_tensor(pe, 0)

            norm_tensor(pe, "lat", xT, lambda p: wait_x(pe, 1, p))
            pe.wait_ge(S("norm_out"), 4)
            pe.wait_ge(S("x0_bvec"), 1)
            for b in range(B):
                for s in range(2):
                    ins = nc.tensor.transpose(ps[:, b // 2, (b % 2 * 2 + s) * P:(b % 2 * 2 + s + 1) * P], x_kv[:, b, s, :], ident)
                ins.then_inc(S("x0_kvt"), 1)
            for h in range(XH):
                for p in range(2):
                    n = 2 * h + p
                    if n >= 4:
                        pe.wait_ge(S("x0_q"), n - 3)
                    mm(bank(4 + n % 4), x_m[:, h, :], x_kv[:, HB * p:HB * (p + 1), 1, :], start=True, stop=True).then_inc(S("x0_qmm"), 1)
            pe.wait_ge(S("x0_q"), 16)
            pe.wait_ge(S("x0_kvt_sb"), 4)

            def x_scores(b, v, w, slot):
                if v == 0:
                    pe.wait_ge(S("x0_slices"), 3 * b + 3)
                if not isinstance(w, int) or w >= 2:
                    pe.wait_ge(S("x0_p"), 4 * (w - 1) + 1)
                for i in range(4):
                    ins = mm(ps[:, 2 * v + i // 2, (i % 2) * 256:(i % 2 + 1) * 256], x_qs[:, slot, 4 * v + i, :],
                             x_kvs[:, slot].rearrange("p s k -> p (s k)"), start=True, stop=True, skip_group_check=True)
                ins.then_inc(S("x0_scores"), 1)

            def x_turn(v, w):
                pe.wait_ge(S("x0_pn"), 4 * (w + 1))
                pe.wait_ge(S("x0_ptA"), w + 1)
                pe.wait_ge(S("x0_ptB"), w + 1)
                for s in range(2):
                    for i in range(4):
                        ins = nc.tensor.transpose(ps[:, 4 + s, i * P:(i + 1) * P], x_p[:, v, i, s * P:(s + 1) * P], ident)
                ins.then_inc(S("x0_turned"), 1)

            def x_weigh(v, w, slot, first):
                pe.wait_ge(S("x0_ptA"), w + 2)
                pe.wait_ge(S("x0_ptB"), w + 2)
                pe.wait_ge(S("x0_o"), first + 1)
                for s in range(2):
                    ins = mm(bank(6 + v), x_kvts[:, slot, s, :], x_pt[:, v, s, :], start=(s == 0), stop=(s == 1))
                ins.then_inc(S("x0_weighed"), 1)

            def x_body(i, final):
                for k in range(4):
                    w = 4 * i + k
                    if not (final and k == 3):
                        x_scores(2 * i + (k + 1) // 2, (k + 1) % 2, w + 1, (k + 1) // 2 % 2)
                    x_turn(k % 2, w)
                    x_weigh(k % 2, w, k // 2, w if k == 0 else w - 1)

            credited(pe, "x0_turned")
            x_scores(0, 0, 0, 0)
            with pe.Fori(0, B // 2 - 1) as i:
                x_body(i, False)
            x_body(B // 2 - 1, True)
            pe.wait_ge(S("x0_o"), 2 * B + 1)
            for p in range(2):
                for h in range(XH):
                    ins = mm(bank(p), x_u[:, h, :], half(x_q[:, h, :], p), start=(h == 0), stop=(h == XH - 1))
                ins.then_inc(S("y_ready"), 1)
            residual_norm_tensor(pe, 1)

            piece(pe, "m0_router")
            pe.wait_ge(S("consts"), 64)
            wait_x(pe, 2)
            route_tensor(pe, "m0", xT)
            mix_tensor(pe, "m0", xT, M0_CH, M0_ROWS, 2)
            residual_norm_tensor(pe, 2)

            pe.wait_ge(S("l1_rot"), 1)
            wait_x(pe, 3)
            for p in range(2):
                mm(bank(p), g_rot[:, 0, :], half(xT, p), start=True, stop=True).then_inc(S("l1_qmm"), 1)
                mm(bank(2 + p), g_rot[:, 1, :], half(xT, p), start=True, stop=True).then_inc(S("l1_kmm"), 1)
                for b in range(HB * p, HB * (p + 1)):
                    ins = mm(ps[:, 4 + p, (b % HB) * P:(b % HB + 1) * P], xT[:, b * P:(b + 1) * P], g_rot[:, 2, :],
                             start=True, stop=True, skip_group_check=True)
                ins.then_inc(S("l1_vmm"), 1)
            for p in range(2):
                pe.wait_ge(S("l1_q"), p + 1)
                pe.wait_ge(S("l1_k"), p + 1)
                for b in range(HB * p, HB * (p + 1)):
                    ins = mm(ps[:, 6 + p, (b % HB) * P:(b % HB + 1) * P], g_q[:, b * P:(b + 1) * P], g_k[:, b * P:(b + 1) * P],
                             start=True, stop=True, skip_group_check=True)
                ins.then_inc(S("l1_scores"), 1)
            for p in range(2):
                pe.wait_ge(S("l1_e"), p + 1)
                for b in range(HB * p, HB * (p + 1)):
                    ins = nc.tensor.transpose(ps[:, p, (b % HB) * P:(b % HB + 1) * P], g_z[:, b, :], ident)
                ins.then_inc(S("l1_turned"), 1)
            for p in range(2):
                pe.wait_ge(S("l1_pt"), p + 1)
                pe.wait_ge(S("l1_v"), p + 1)
                for b in range(HB * p, HB * (p + 1)):
                    ins = mm(ps[:, 2 + p, (b % HB) * P:(b % HB + 1) * P], g_pt[:, b, :], g_v[:, b, :],
                             start=True, stop=True, skip_group_check=True)
                ins.then_inc(S("l1_weighed"), 1)
            for p in range(2):
                pe.wait_ge(S("l1_out"), p + 1)
                for b in range(HB * p, HB * (p + 1)):
                    ins = nc.tensor.transpose(ps[:, p, (b % HB) * P:(b % HB + 1) * P], g_av[:, b, :], ident)
                ins.then_inc(S("y_ready"), 1)
            residual_norm_tensor(pe, 3)

            piece(pe, "x1_wq")
            pe.wait_ge(S("ctx_loaded"), 16)
            pe.wait_ge(S("maskb"), 1)
            wait_x(pe, 4)
            narrow_tensor(pe, "x1", xT, ctxT, False, maskb, W("x1_wo"))
            residual_norm_tensor(pe, 4)

            pe.wait_ge(S("f1_wq"), 1)
            wait_x(pe, 5)
            for n in range(9):
                ins = nc.tensor.transpose(ps[:, 5 + n // 4, (n % 4) * P:(n % 4 + 1) * P],
                                          q_w[:, 4 * n:4 * n + 4, :].rearrange("p a k -> p (a k)"), ident)
            ins.then_inc(S("f1_wturned"), 1)

            def largest(n):
                pe.wait_ge(S("f1_col"), n + 1)
                nc.tensor.transpose(ps[0:1, 0, 0:P], q_col[:, n:n + 1], ident).then_inc(S("f1_colT"), 1)
                pe.wait_ge(S("f1_top"), n + 1)
                mm(ps[:, 1, 0:1], ones1[:, :], q_top[:, n:n + 1], start=True, stop=True).then_inc(S("f1_topB"), 1)

            pe.wait_ge(S("filled"), 4)
            largest(0)
            pe.wait_ge(S("f1_wT"), 1)
            pe.wait_ge(S("f1_xq"), 1)
            for k in range(2):
                for c in range(3):
                    for p in range(2):
                        if k:
                            pe.wait_ge(S("f1_up"), 2 * c + p + 1)
                        mm(bank(2 + 2 * c + p), q_wT[:, 3 * (1 - k) + c, :], half(q_x, p), start=True, stop=True).then_inc(S("f1_mm"), 1)
            for n in range(1, 5):
                largest(n)
            pe.wait_ge(S("f1_o"), 1)
            for p in range(2):
                for c in range(3):
                    ins = mm(bank(p), q_wT[:, 6 + c, :], q_up[:, c * T + p * HALF:c * T + (p + 1) * HALF], start=(c == 0), stop=(c == 2))
                ins.then_inc(S("y_ready"), 1)
            residual_norm_tensor(pe, 5)

            piece(pe, "l2_wk")
            for p in range(2):
                for k, (name, src) in enumerate((("l2_wk", r_k), ("l2_wv", r_v), ("l2_wr", r_r))):
                    pe.wait_ge(S("l2_mix"), 3 * p + k + 1)
                    mm(bank(2 * k + p), W(name), half(src, p), start=True, stop=True).then_inc(S(f"{name}_mm"), 1)
            for p in range(2):
                pe.wait_ge(S("l2_ek"), p + 1)
                mm(bank(6 + p), W("headsum"), half(r_ek, p), start=True, stop=True).then_inc(S("l2_bsum"), 1)
            for p in range(2):
                pe.wait_ge(S("l2_out"), p + 1)
                mm(bank(p), W("l2_wo"), half(r_k, p), start=True, stop=True).then_inc(S("y_ready"), 1)
            residual_norm_tensor(pe, 6)

            piece(pe, "x2_wq")
            wait_x(pe, 7)
            narrow_tensor(pe, "x2", xT, ctxT, False, None, W("x2_wo"))
            residual_norm_tensor(pe, 7)

            norm_mean(pe, "rms1")
            pe.wait_ge(S("f2_h"), 2)
            piece(pe, "f2_wq")
            narrow_tensor(pe, "f2", f_h, f_h, True, caus, W("f2_wo"), "f2_attn")
            norm_mean(pe, "rms2")
            pe.wait_ge(S("f2_h"), 4)
            route_tensor(pe, "m2", m_x2)
            mix_tensor(pe, "m2", m_x2, M2_CH, M2_ROWS, 8)
            residual_norm_tensor(pe, 8)

            for p in range(2):
                wait_x(pe, 9, 1)
                mm(ps[0:64, 2 + p, :], W("l3_wg"), half(xT, p), start=True, stop=True).then_inc(S("l3_gmm"), 1)
                mm(ps[0:64, 4 + p, :], W("l3_wb"), half(xT, p), start=True, stop=True).then_inc(S("l3_bmm"), 1)
            for p in range(2):
                pe.wait_ge(S("l3_state"), 4 * p + 4)
                mm(bank(6 + p), W("l3_wc")[0:64, :], half(s_st, p)[0:64, :], start=True, stop=True).then_inc(S("l3_ymm"), 1)

            def inner_ready(p):
                pe.wait_ge(S("l3_h"), p + 1)
            norm_tensor(pe, "inner", s_h, inner_ready)
            for p in range(2):
                pe.wait_ge(S("l3_hn"), p + 1)
                mm(bank(p), W("l3_wout"), half(s_hn, p), start=True, stop=True).then_inc(S("y_ready"), 1)
            residual_norm_tensor(pe, 9)

            pe.wait_ge(S("ctxtm_loaded"), 16)
            for p in range(2):
                wait_x(pe, 10, 1)
                for b in range(HB * p, HB * (p + 1)):
                    ins = mm(ps[:, 6 + p, (b % HB) * P:(b % HB + 1) * P], ctxT[:, b * P:(b + 1) * P], xT[:, b * P:(b + 1) * P],
                             start=True, stop=True, skip_group_check=True)
                ins.then_inc(S("e_up"), 1)
            for p in range(2):
                pe.wait_ge(S("e_act"), p + 1)
                for b in range(HB * p, HB * (p + 1)):
                    ins = mm(ps[:, p, (b % HB) * P:(b % HB + 1) * P], ctx_tm[:, b * P:(b + 1) * P], e_a[:, b * P:(b + 1) * P],
                             start=True, stop=True, skip_group_check=True)
                ins.then_inc(S("y_ready"), 1)
            residual_norm_tensor(pe, 10)

            wait_x(pe, 11)
            for b in range(B):
                ins = mm(ps[:, 2 + b // 3, (b % 3) * NE:(b % 3 + 1) * NE], xT[:, b * P:(b + 1) * P], W("m3_router"),
                         start=True, stop=True, skip_group_check=True)
            ins.then_inc(R("m3", "_logits"), 1)
            for p in range(2):
                mm(ps[0:64, 6 + p, :], W("m3_sgate"), half(xT, p), start=True, stop=True).then_inc(S("m3_shared"), 1)
            for p in range(2):
                pe.wait_ge(S("m3_sact"), p + 1)
                mm(bank(p), W("m3_sdown")[0:64, :], half(t_sh, p)[0:64, :], start=True, stop=False, skip_group_check=True)
            waits(pe, "m3")("_parts", 3)
            for s in range(SETS):
                for b in range(B):
                    ins = nc.tensor.transpose(bankb(2 + s)[:, b * P:(b + 1) * P], t_parts[:, b, s, :], identb[:, :])
                ins.then_inc(R("m3", "_wturned"), 1)
            waits(pe, "m3")("_wT", SETS)

            def up(i, j, p, n):
                if j % 4 == 0 and p == 0:
                    waits(pe, "m3")(f"_load{j // 4}", 16 * i + 16)
                if not isinstance(n, int) or n >= 2:
                    waits(pe, "m3")("_hid", n - 1)
                at = (j % 4) * 2 * P
                mm(bank(2 + p), ring[:, j // 4, at:at + P], half(xT, p), start=True, stop=True).then_inc(R("m3", "_gate"), 1)
                mm(bank(4 + p), sel160[:, bass.ds((10 * (j % 2) + i) * P, P)], half(t_combT[:, j // 2, :], p),
                   start=True, stop=True).then_inc(R("m3", "_spread"), 1)

            def down(j, p, n, final):
                waits(pe, "m3")("_hid", n + 1)
                at = (j % 4) * 2 * P + P
                mm(bank(p), ring[:, j // 4, at:at + P], t_hid[:, p], start=False, stop=final,
                   skip_group_check=True).then_inc(S("y_ready") if final else R("m3", "_down"), 1)

            def body(i, final):
                for u in range(2 * CHUNKS):
                    n = 2 * CHUNKS * i + u
                    if u < 2 * CHUNKS - 1:
                        up(i, (u + 1) // 2, (u + 1) % 2, n + 1)
                    elif not final:
                        up(i + 1, 0, 0, n + 1)
                    down(u // 2, u % 2, n, final and u >= 2 * CHUNKS - 2)

            up(0, 0, 0, 0)
            with pe.Fori(0, GROUPS - 1) as i:
                body(i, False)
            body(GROUPS - 1, True)
            residual_norm_tensor(pe, 11)

        @block.scalar
        def _(act):
            A_ = nc.scalar.activation
            act.wait_ge(S("filled"), 2)
            norm_scalar(act, "ctx")
            piece(act, "l0_td")
            A_(d_e, W("l0_td"), ACT.Exp).then_inc(S("l0_e"), 1)
            for p in range(2):
                act.wait_ge(S("l0_r"), p + 1)
                A_(bank(4 + p), bank(4 + p), ACT.Sigmoid).then_inc(S("l0_sig"), 1)
            act.wait_ge(S("x0_mw"), 1)
            A_(x_m.rearrange("p h d -> p (h d)"), ps[:, 6:8, :].rearrange("p a c -> p (a c)"), ACT.Copy,
               scale=P ** -0.5).then_inc(S("x0_m"), 1)
            act.wait_ge(S("x0_bw"), 1)
            A_(x_c, ps[:, 6, 0:XH], ACT.Copy, scale=P ** -0.5).then_inc(S("x0_cvec"), 1)
            norm_scalar(act, "0", root=True)

            norm_scalar(act, "lat")
            act.wait_ge(S("x0_cvec"), 1)
            for h in range(XH):
                for p in range(2):
                    act.wait_ge(S("x0_qmm"), 2 * h + p + 1)
                    A_(half(x_q[:, h, :], p), bank(4 + (2 * h + p) % 4), ACT.Identity, bias=x_c[:, h:h + 1]).then_inc(S("x0_q"), 1)

            def x_exps(v, w):
                act.wait_ge(S("x0_nm"), w + 1)
                if not isinstance(w, int) or w >= 2:
                    act.wait_ge(S("x0_turned"), w)
                for i in range(4):
                    A_(x_p[:, v, i, :], ps[:, 2 * v + i // 2, (i % 2) * 256:(i % 2 + 1) * 256], ACT.Exp,
                       bias=x_nm[:, v, i:i + 1], accum_out=x_sum[:, v, i:i + 1]).then_inc(S("x0_p"), 1)

            def x_copies(b, v, w):
                act.wait_ge(S("x0_turned"), w + 2)
                A_(x_pt[:, v, 0, :], bank(4), ACT.Copy).then_inc(S("x0_ptA"), 1)
                act.wait_ge(S("x0_weighed"), w + 1)
                A_(x_q[:, 4 * v:4 * v + 4, bass.ds(b * P, P)], bank(6 + v).rearrange("p (h t) -> p h t", h=4),
                   ACT.Copy).then_inc(S("x0_o"), 1)

            def x_body(i, final):
                for k in range(4):
                    w = 4 * i + k
                    if not (final and k == 3):
                        x_exps((k + 1) % 2, w + 1)
                    x_copies(2 * i + k // 2, k % 2, w)

            credited(act, "x0_p", "x0_ptA", "x0_o")
            x_exps(0, 0)
            with act.Fori(0, B // 2 - 1) as i:
                x_body(i, False)
            x_body(B // 2 - 1, True)
            norm_scalar(act, "1")

            route_scalar(act, "m0")
            mix_scalar(act, "m0", M0_CH, M0_ROWS)
            norm_scalar(act, "2")

            act.wait_ge(S("l1_norm"), 1)
            A_(g_n2, g_n, ACT.Ln).then_inc(S("l1_log"), 1)
            act.wait_ge(S("l1_log"), 1)
            A_(g_n, g_n2, ACT.Exp, scale=-0.5).then_inc(S("l1_root"), 1)
            for p in range(2):
                act.wait_ge(S("l1_qmm"), p + 1)
                A_(half(g_q, p), bank(p), ACT.Copy).then_inc(S("l1_q"), 1)
                act.wait_ge(S("l1_vmm"), p + 1)
                A_(g_v[:, HB * p:HB * (p + 1), :], bank(4 + p).rearrange("p (b d) -> p b d", b=HB), ACT.Copy).then_inc(S("l1_v"), 1)
            for p in range(2):
                act.wait_ge(S("l1_z"), p + 1)
                A_(g_z[:, HB * p:HB * (p + 1), :], g_z[:, HB * p:HB * (p + 1), :], ACT.Exp).then_inc(S("l1_e"), 1)
            for p in range(2):
                act.wait_ge(S("l1_turned"), p + 1)
                A_(g_pt[:, HB * p:HB * (p + 1), :], bank(p).rearrange("p (b d) -> p b d", b=HB), ACT.Copy).then_inc(S("l1_pt"), 1)
            for p in range(2):
                act.wait_ge(S("l1_in"), p + 1)
                A_(g_in[:, HB * p:HB * (p + 1)], g_in[:, HB * p:HB * (p + 1)], ACT.Ln).then_inc(S("l1_log"), 1)
                act.wait_ge(S("l1_log"), p + 2)
                A_(g_in[:, HB * p:HB * (p + 1)], g_in[:, HB * p:HB * (p + 1)], ACT.Exp, scale=-0.5).then_inc(S("l1_root"), 1)
            norm_scalar(act, "3")

            piece(act, "x1_bq")
            narrow_scalar(act, "x1", False, W("x1_bv"), SCALE8, W("x1_bq"))
            norm_scalar(act, "4")

            act.wait_ge(S("f1_wturned"), 1)
            A_(q_wT.rearrange("p a k -> p (a k)"), ps[:, 5:8, :].rearrange("p a c -> p (a c)")[:, 0:9 * P], ACT.Copy).then_inc(S("f1_wT"), 1)
            for k, dst in enumerate((q_up, q_gate)):
                for n in range(6):
                    act.wait_ge(S("f1_mm"), 6 * k + n + 1)
                    A_(dst[:, n * HALF:(n + 1) * HALF], bank(2 + n), ACT.Copy).then_inc(S("f1_gate" if k else "f1_up"), 1)
            act.wait_ge(S("f1_gq"), 1)
            A_(q_sig, q_gate, ACT.Sigmoid).then_inc(S("f1_sig"), 1)
            norm_scalar(act, "5")

            piece(act, "l2_td")
            A_(r_e, W("l2_td"), ACT.Exp).then_inc(S("l2_decay"), 1)
            A_(r_u, W("l2_tf"), ACT.Exp).then_inc(S("l2_decay"), 1)
            act.wait_ge(S("l2_decay"), 2)
            A_(r_dec, r_e, ACT.Exp, scale=-1.0).then_inc(S("l2_decay"), 1)
            for p in range(2):
                act.wait_ge(S("l2_wk_mm"), p + 1)
                A_(half(r_ek, p), bank(p), ACT.Exp).then_inc(S("l2_ek"), 1)
            for p in range(2):
                act.wait_ge(S("l2_wr_mm"), p + 1)
                A_(half(r_sig, p), bank(4 + p), ACT.Sigmoid).then_inc(S("l2_sig"), 1)
            norm_scalar(act, "6")

            piece(act, "x2_bq")
            narrow_scalar(act, "x2", False, W("x2_bv"), SCALE8, W("x2_bq"))
            norm_scalar(act, "7")

            wait_x(act, 8)
            norm_scalar(act, "rms1", eps6, xT)
            narrow_scalar(act, "f2", True, None, SCALE8)
            act.wait_ge(S("f2_x2"), 2)
            norm_scalar(act, "rms2", eps6, f_x2)
            route_scalar(act, "m2")
            mix_scalar(act, "m2", M2_CH, M2_ROWS)
            norm_scalar(act, "8")

            A_(s_a, W("l3_alog"), ACT.Exp).then_inc(S("l3_a"), 1)
            for p in range(2):
                act.wait_ge(S("l3_gmm"), p + 1)
                A_(half(s_sig, p)[0:64, :], ps[0:64, 2 + p, :], ACT.Sigmoid, bias=W("l3_bg")[0:64, :]).then_inc(S("l3_sig"), 1)
            norm_scalar(act, "inner")
            norm_scalar(act, "9")

            for p in range(2):
                act.wait_ge(S("e_up"), p + 1)
                A_(half(e_a, p), bank(6 + p), ACT.Gelu_apprx_tanh).then_inc(S("e_act"), 1)
            norm_scalar(act, "10")

            act.wait_ge(S("m3_biased"), 3)
            A_(t_p[:, :, :], t_p[:, :, :], ACT.Sigmoid).then_inc(S("m3_prob"), 1)
            for p in range(2):
                act.wait_ge(S("m3_shared"), p + 1)
                A_(half(t_sh, p)[0:64, :], ps[0:64, 6 + p, :], ACT.Silu).then_inc(S("m3_sact"), 1)
            with act.Fori(0, GROUPS * CHUNKS) as i:
                for p in range(2):
                    waits(act, "m3")("_gate", 2 * i + p + 1)
                    A_(t_sg[:, p], bank(2 + p), ACT.Silu).then_inc(R("m3", "_silu"), 1)
            norm_scalar(act, "11")

        @block.vector
        def _(dve):
            V = nc.vector
            link = linked(dve, "dve_step")

            def affine_norm(tag, s, g, b):
                for p in range(2):
                    dst = x_kv[:, HB * p:HB * (p + 1), s, :]
                    dve.wait_ge(S("norm_rstd"), nth(tag, p))
                    link(V.tensor_tensor(dst, bank(2 + p).rearrange("p (b t) -> p b t", b=HB),
                                         half(rstd, p).rearrange("p (b t) -> p b t", b=HB), ALU.mult))
                    V.tensor_scalar(dst, dst, W(g), W(b), ALU.mult, ALU.add).then_inc(S("norm_out"), 1)

            piece(dve, "x0_gm")
            affine_norm("ctx", 0, "x0_gm", "x0_bm")
            dve.wait_ge(S("l0_e"), 1)
            link(V.tensor_scalar(d_w, d_e, -1.0, None, ALU.mult))
            for p in range(2):
                dve.wait_ge(S("l0_k"), p + 1)
                for b in range(HB * p, HB * (p + 1)):
                    ins = V.tensor_tensor_scan(d_s[:, b * P:(b + 1) * P], d_w.to_broadcast([P, P]),
                                               ps[:, 2 + p, (b % HB) * P:(b % HB + 1) * P], 0.0, ALU.mult, ALU.add)
                    link(ins)
                dve.wait_ge(S("l0_sig"), p + 1)
                V.tensor_tensor(half(d_s, p), half(d_s, p), bank(4 + p), ALU.mult).then_inc(S("l0_gated"), 1)
            dve.wait_ge(S("x0_uw"), 1)
            V.tensor_copy(x_u.rearrange("p h d -> p (h d)"), ps[:, 6:8, :].rearrange("p a c -> p (a c)")).then_inc(S("x0_u"), 1)
            dve.wait_ge(S("x0_bw"), 1)
            V.tensor_tensor(x_bo, ps[:, 7, 0:1], W("x0_bo"), ALU.add).then_inc(S("x0_bvec"), 1)
            residual_norm_vector(dve, 0)

            affine_norm("lat", 1, "x0_gl", "x0_bl")
            for n in range(4):
                dve.wait_ge(S("x0_kvt"), 2 * n + 2)
                V.tensor_copy(x_kvt[:, 2 * n:2 * n + 2].rearrange("p b s d -> p (b s d)"), bank(n)).then_inc(S("x0_kvt_sb"), 1)

            def x_maxima(v, w):
                dve.wait_ge(S("x0_scores"), w + 1)
                V.tensor_reduce(x_nm[:, v], ps[:, 2 * v:2 * v + 2, :].rearrange("p a (h k) -> p (a h) k", h=2), AX.X, ALU.max,
                                negate=True).then_inc(S("x0_nm"), 1)

            def x_copies(v, w):
                dve.wait_ge(S("x0_turned"), w + 2)
                V.tensor_copy(x_pt[:, v, 1, :], bank(5)).then_inc(S("x0_ptB"), 1)

            def x_normalise(v, w):
                dve.wait_ge(S("x0_p"), 4 * (w + 1) + 1)
                V.reciprocal(x_rec[:, v], x_sum[:, v]).then_inc(S("x0_rec"), 1)
                dve.wait_ge(S("x0_rec"), w + 1)
                for i in range(4):
                    V.tensor_scalar(x_p[:, v, i, :], x_p[:, v, i, :], x_rec[:, v, i:i + 1], None, ALU.mult).then_inc(S("x0_pn"), 1)

            def x_body(i, final):
                for k in range(4):
                    w = 4 * i + k
                    if not (final and k == 3):
                        x_maxima((k + 1) % 2, w + 1)
                    x_copies(k % 2, w)
                    if not (final and k == 3):
                        x_normalise((k + 1) % 2, w + 1)

            credited(dve, "x0_ptB")
            x_maxima(0, 0)
            x_normalise(0, 0)
            with dve.Fori(0, B // 2 - 1) as i:
                x_body(i, False)
            x_body(B // 2 - 1, True)
            residual_norm_vector(dve, 1, x_bo)

            route_vector(dve, "m0", 1e-6, link)
            mix_vector(dve, "m0", xT, M0_CH, M0_ROWS)
            residual_norm_vector(dve, 2)

            wait_x(dve, 3)
            link(V.tensor_tensor(g_n, W("l1_rc"), W("l1_rc"), ALU.mult))
            link(V.tensor_tensor(g_n2, W("l1_rs"), W("l1_rs"), ALU.mult))
            V.tensor_tensor(g_n, g_n, g_n2, ALU.add).then_inc(S("l1_norm"), 1)
            link(V.reciprocal(g_a, W("l1_scale")))
            link(V.tensor_scalar(g_a, g_a, 2.0, None, ALU.mult))
            link(V.tensor_tensor(g_b, g_a, W("l1_bias"), ALU.add))
            dve.wait_ge(S("l1_root"), 1)
            link(V.tensor_tensor(g_c, W("l1_rc"), g_n, ALU.mult))
            link(V.tensor_tensor(g_s, W("l1_rs"), g_n, ALU.mult))
            for k in range(3):
                link(V.tensor_scalar(g_t[:, k], W("swap"), g_s[:, k:k + 1], None, ALU.mult))
                ins = V.scalar_tensor_tensor(out=g_rot[:, k], in0=ident, scalar=g_c[:, k:k + 1], in1=g_t[:, k], op0=ALU.mult, op1=ALU.add)
            ins.then_inc(S("l1_rot"), 1)
            for p in range(2):
                dve.wait_ge(S("l1_kmm"), p + 1)
                V.tensor_copy(half(g_k, p), bank(2 + p)).then_inc(S("l1_k"), 1)
            for p in range(2):
                z = g_z[:, HB * p:HB * (p + 1), :]
                mx = g_mx[:, HB * p:HB * (p + 1)]
                dve.wait_ge(S("l1_scores"), p + 1)
                link(V.tensor_scalar(z, bank(6 + p).rearrange("p (b k) -> p b k", b=HB), g_a, g_b, ALU.mult, ALU.add))
                link(V.tensor_reduce(mx, z, AX.X, ALU.max))
                V.tensor_tensor(z, z, mx.unsqueeze(2).to_broadcast([P, HB, P]), ALU.subtract).then_inc(S("l1_z"), 1)
            for p in range(2):
                dve.wait_ge(S("l1_e"), p + 1)
                link(V.tensor_reduce(g_sm[:, HB * p:HB * (p + 1)], g_z[:, HB * p:HB * (p + 1), :], AX.X, ALU.add))
                link(V.reciprocal(g_rc[:, HB * p:HB * (p + 1)], g_sm[:, HB * p:HB * (p + 1)]))
            for p in range(2):
                av = g_av[:, HB * p:HB * (p + 1), :]
                s2 = g_sq[:, HB * p:HB * (p + 1), :]
                dve.wait_ge(S("l1_weighed"), p + 1)
                link(V.tensor_tensor(av, bank(2 + p).rearrange("p (b d) -> p b d", b=HB),
                                     g_rc[:, HB * p:HB * (p + 1)].unsqueeze(2).to_broadcast([P, HB, P]), ALU.mult))
                link(V.tensor_tensor(s2, av, av, ALU.mult))
                link(V.tensor_reduce(g_in[:, HB * p:HB * (p + 1)], s2, AX.X, ALU.add))
                V.tensor_scalar(g_in[:, HB * p:HB * (p + 1)], g_in[:, HB * p:HB * (p + 1)], 1e-8, None, ALU.max).then_inc(S("l1_in"), 1)
            for p in range(2):
                av = g_av[:, HB * p:HB * (p + 1), :]
                dve.wait_ge(S("l1_root"), p + 2)
                V.tensor_tensor(av, av, g_in[:, HB * p:HB * (p + 1)].unsqueeze(2).to_broadcast([P, HB, P]), ALU.mult).then_inc(S("l1_out"), 1)
            dve.wait_ge(S("mask_loaded"), 16)
            V.tensor_scalar(maskb[:, :], mask8[:, :], NEG, None, ALU.mult).then_inc(S("maskb"), 1)
            residual_norm_vector(dve, 3)

            piece(dve, "x1_bk")
            narrow_vector(dve, "x1", False, W("x1_bk"))
            residual_norm_vector(dve, 4, W("x1_bo"))

            wait_x(dve, 5)
            at = PACK_AT["f1_gate"][0]
            wts = pack[:, at:at + 9 * P].rearrange("p (a k) -> p a k", k=32)
            link(V.tensor_reduce(q_ab, wts, AX.X, ALU.max, apply_absolute_value=True))
            link(V.tensor_scalar(q_sc, q_ab, 1.0 / 7.0, 1e-12, ALU.mult, ALU.max))
            link(V.reciprocal(q_inv, q_sc))
            link(V.tensor_tensor(q_w, wts, q_inv.unsqueeze(2).to_broadcast([P, 36, 32]), ALU.mult))
            link(V.tensor_scalar(q_w, q_w, ROUND, ROUND, ALU.add, ALU.subtract))
            V.tensor_tensor(q_w, q_w, q_sc.unsqueeze(2).to_broadcast([P, 36, 32]), ALU.mult).then_inc(S("f1_wq"), 1)

            def largest(n, src):
                V.tensor_reduce(q_col[:, n:n + 1], src, AX.X, ALU.max, apply_absolute_value=True).then_inc(S("f1_col"), 1)
                dve.wait_ge(S("f1_colT"), n + 1)
                V.tensor_reduce(q_top[:, n:n + 1], ps[0:1, 0, 0:P], AX.X, ALU.max).then_inc(S("f1_top"), 1)
                dve.wait_ge(S("f1_topB"), n + 1)
                link(V.tensor_scalar(q_s[:, n:n + 1], ps[:, 1, 0:1], 1.0 / QMAX, 1e-12, ALU.mult, ALU.max))
                link(V.reciprocal(q_i[:, n:n + 1], q_s[:, n:n + 1]))

            def quantise(n, dst, src):
                link(V.tensor_scalar(dst, src, q_i[:, n:n + 1], ROUND, ALU.mult, ALU.add))
                return V.tensor_scalar(dst, dst, ROUND, q_s[:, n:n + 1], ALU.subtract, ALU.mult)

            largest(0, xT[:, :])
            quantise(0, q_x, xT[:, :]).then_inc(S("f1_xq"), 1)
            dve.wait_ge(S("f1_up"), 6)
            largest(1, q_up)
            link(quantise(1, q_up, q_up))
            dve.wait_ge(S("f1_gate"), 6)
            largest(2, q_gate)
            quantise(2, q_gate, q_gate).then_inc(S("f1_gq"), 1)
            dve.wait_ge(S("f1_sig"), 1)
            link(V.tensor_scalar(q_sig, q_sig, 65536.0, ROUND, ALU.mult, ALU.add))
            link(V.tensor_scalar(q_sig, q_sig, ROUND, 65535.0, ALU.subtract, ALU.min))
            link(V.scalar_tensor_tensor(out=q_gate, in0=q_sig, scalar=1.0 / 65536.0, in1=q_gate, op0=ALU.mult, op1=ALU.mult))
            largest(3, q_gate)
            link(quantise(3, q_gate, q_gate))
            link(V.tensor_tensor(q_up, q_gate, q_up, ALU.mult))
            largest(4, q_up)
            quantise(4, q_up, q_up).then_inc(S("f1_o"), 1)
            residual_norm_vector(dve, 5)

            piece(dve, "l2_mk")
            for p in range(2):
                dve.wait_ge(S("l2_prev"), p + 1)
                prev = r_prev[:, HB * p:HB * (p + 1), :].rearrange("p b t -> p (b t)")
                link(V.tensor_tensor(half(r_diff, p), half(xT, p), prev, ALU.subtract))
                for name, dst in (("l2_mk", r_k), ("l2_mv", r_v), ("l2_mr", r_r)):
                    V.scalar_tensor_tensor(out=half(dst, p), in0=half(r_diff, p), scalar=W(name), in1=prev,
                                           op0=ALU.mult, op1=ALU.add).then_inc(S("l2_mix"), 1)
            dve.wait_ge(S("l2_decay"), 3)
            dve.wait_ge(S("l2_zero"), 3)
            for p in range(2):
                seqs = range(HB * p, HB * (p + 1))
                dve.wait_ge(S("l2_ek"), p + 1)
                dve.wait_ge(S("l2_wv_mm"), p + 1)
                link(V.tensor_tensor(half(r_ekv, p), half(r_ek, p), bank(2 + p), ALU.mult))
                dve.wait_ge(S("l2_bsum"), p + 1)
                for b in seqs:
                    ins = V.tensor_tensor_scan(r_sa[:, b, 1:P + 1], r_dec.to_broadcast([P, P]), r_ekv[:, b * P:(b + 1) * P],
                                               0.0, ALU.mult, ALU.add)
                    ins = V.tensor_tensor_scan(r_sb[:, b, 1:P + 1], r_dec.to_broadcast([P, P]),
                                               ps[:, 6 + p, (b % HB) * P:(b % HB + 1) * P], 0.0, ALU.mult, ALU.add)
                link(ins)
                ha = r_sa[:, HB * p:HB * (p + 1), 0:P]
                hb = r_sb[:, HB * p:HB * (p + 1), 0:P]
                den = half(r_den, p).rearrange("p (b t) -> p b t", b=HB)
                num = half(r_ekv, p).rearrange("p (b t) -> p b t", b=HB)
                link(V.scalar_tensor_tensor(out=num, in0=num, scalar=r_u, in1=ha, op0=ALU.mult, op1=ALU.add))
                link(V.scalar_tensor_tensor(out=den, in0=bank(6 + p).rearrange("p (b t) -> p b t", b=HB), scalar=r_u, in1=hb,
                                            op0=ALU.mult, op1=ALU.add))
                link(V.tensor_scalar(half(r_den, p), half(r_den, p), 1e-6, None, ALU.max))
                link(V.reciprocal(half(r_den, p), half(r_den, p)))
                link(V.tensor_tensor(half(r_den, p), half(r_den, p), half(r_ekv, p), ALU.mult))
                dve.wait_ge(S("l2_sig"), p + 1)
                V.tensor_tensor(half(r_k, p), half(r_den, p), half(r_sig, p), ALU.mult).then_inc(S("l2_out"), 1)
            residual_norm_vector(dve, 6)

            piece(dve, "x2_bk")
            narrow_vector(dve, "x2", False, W("x2_bk"))
            residual_norm_vector(dve, 7, W("x2_bo"))

            piece(dve, "f2_ln1")
            for p in range(2):
                dve.wait_ge(S("norm_rstd"), nth("rms1", p))
                V.scalar_tensor_tensor(out=half(f_h, p), in0=half(xT, p), scalar=W("f2_ln1"), in1=half(rstd, p),
                                       op0=ALU.mult, op1=ALU.mult).then_inc(S("f2_h"), 1)
            narrow_vector(dve, "f2", True)
            for p in range(2):
                dve.wait_ge(S("f2_attn"), p + 1)
                V.tensor_tensor(half(f_x2, p), bank(p), half(xT, p), ALU.add).then_inc(S("f2_x2"), 1)
            dve.wait_ge(S("f2_x2"), 2)
            link(V.tensor_tensor(f_res, f_x2, xT[:, :], ALU.add))
            for p in range(2):
                dve.wait_ge(S("norm_rstd"), nth("rms2", p))
                V.scalar_tensor_tensor(out=half(m_x2, p), in0=half(f_x2, p), scalar=W("f2_ln2"), in1=half(rstd, p),
                                       op0=ALU.mult, op1=ALU.mult).then_inc(S("f2_h"), 1)
            route_vector(dve, "m2", 0.0, link)
            mix_vector(dve, "m2", m_x2, M2_CH, M2_ROWS)
            residual_norm_vector(dve, 8, None, f_res)

            dve.wait_ge(S("l3_a"), 1)
            for p in range(2):
                dve.wait_ge(S("l3_sig"), p + 1)
                dve.wait_ge(S("l3_bmm"), p + 1)
                link(V.tensor_tensor(half(s_u, p)[0:64, :], half(s_sig, p)[0:64, :], ps[0:64, 4 + p, :], ALU.mult))
                for b in range(HB * p, HB * (p + 1)):
                    V.tensor_tensor_scan(s_st[0:64, b * P:(b + 1) * P], s_a[0:64, :].to_broadcast([64, P]),
                                         s_u[0:64, b * P:(b + 1) * P], 0.0, ALU.mult, ALU.add).then_inc(S("l3_state"), 1)
            for p in range(2):
                dve.wait_ge(S("l3_ymm"), p + 1)
                link(V.scalar_tensor_tensor(out=half(s_h, p), in0=half(xT, p), scalar=W("l3_d"), in1=bank(6 + p),
                                            op0=ALU.mult, op1=ALU.add))
                V.tensor_tensor(half(s_h, p), half(s_h, p), half(xT, p), ALU.add).then_inc(S("l3_h"), 1)
            for p in range(2):
                dve.wait_ge(S("norm_rstd"), nth("inner", p))
                link(V.tensor_tensor(half(s_hn, p), bank(2 + p), half(rstd, p), ALU.mult))
                V.tensor_scalar(half(s_hn, p), half(s_hn, p), W("l3_gamma"), W("l3_beta"), ALU.mult, ALU.add).then_inc(S("l3_hn"), 1)
            residual_norm_vector(dve, 9, W("l3_bout"))

            residual_norm_vector(dve, 10)

            waits(dve, "m3")("_logits", 1)
            for k in range(3):
                b0, b1 = 3 * k, min(3 * k + 3, B)
                V.tensor_tensor(t_p[:, b0:b1, :], ps[:, 2 + k, 0:(b1 - b0) * NE].rearrange("p (b e) -> p b e", e=NE),
                                W("m3_bias").unsqueeze(1).to_broadcast([P, b1 - b0, NE]), ALU.add).then_inc(S("m3_biased"), 1)
            dve.wait_ge(S("m3_prob"), 1)
            for b in range(B):
                ins = V.max(t_top[:, b, :], t_p[:, b, :])
            link(ins)
            for b in range(B):
                ins = V.match_replace(t_rep[:, b, :], t_top[:, b, :], t_p[:, b, :], 0.0)
            link(ins)
            link(V.tensor_tensor(t_w, t_p, t_rep, ALU.subtract))
            link(V.tensor_reduce(t_s, t_top, AX.X, ALU.add))
            link(V.tensor_scalar(t_s, t_s, 1e-9, None, ALU.add))
            link(V.reciprocal(t_s, t_s))
            link(V.tensor_scalar(t_s, t_s, 2.5, None, ALU.mult))
            link(V.tensor_tensor(t_w, t_w, t_s.unsqueeze(2).to_broadcast([P, B, NE]), ALU.mult))
            waits(dve, "m3")("_pad", 1)
            w4 = t_w.rearrange("p b (s e) -> p b s e", s=SETS)
            for k in range(3):
                part = t_parts[:, :, :, k:3 * SETE:3]
                V.tensor_copy(part, w4).then_inc(R("m3", "_parts"), 1)
                if k < 2:
                    waits(dve, "m3")("_parts", k + 1)
                    link(V.tensor_tensor(w4, w4, part, ALU.subtract))
            for s in range(SETS):
                waits(dve, "m3")("_wturned", s + 1)
                V.tensor_copy(t_combT[:, s, :], bankb(2 + s)).then_inc(R("m3", "_wT"), 1)
            with dve.Fori(0, GROUPS * CHUNKS) as i:
                for p in range(2):
                    waits(dve, "m3")("_silu", 2 * i + p + 1)
                    waits(dve, "m3")("_spread", 2 * i + p + 1)
                    V.tensor_tensor(t_hid[:, p], t_sg[:, p], bank(4 + p), ALU.mult).then_inc(R("m3", "_hid"), 1)
            residual_norm_vector(dve, 11)

        @block.gpsimd
        def _(pool):
            G = nc.gpsimd
            G.memset(eps5, EPS).then_inc(S("filled"), 1)
            G.memset(eps6, 1e-6).then_inc(S("filled"), 1)
            G.memset(ones1[:, :], 1.0).then_inc(S("filled"), 1)
            G.memset(zeros[:, :], 0.0).then_inc(S("filled"), 1)
            def x_slices(b, slot):
                G.tensor_copy(x_qs[:, slot], x_q[:, :, bass.ds(b * P, P)]).then_inc(S("x0_slices"), 1)
                G.tensor_copy(x_kvs[:, slot], x_kv[:, bass.ds(b, 1), :, :].rearrange("p o s d -> p (o s) d")).then_inc(S("x0_slices"), 1)
                G.tensor_copy(x_kvts[:, slot], x_kvt[:, bass.ds(b, 1), :, :].rearrange("p o s d -> p (o s) d")).then_inc(S("x0_slices"), 1)
            pool.wait_ge(S("norm_out"), 4)
            pool.wait_ge(S("x0_kvt_sb"), 4)
            pool.wait_ge(S("x0_q"), 2 * XH)
            x_slices(0, 0)
            x_slices(1, 1)
            with pool.Fori(1, B // 2) as i:
                for slot in range(2):
                    pool.wait_ge(S("x0_weighed"), 4 * i + 2 * slot - 2)
                    x_slices(2 * i + slot, slot)

            def padding(t, ready):
                ready()
                G.memset(m_parts[:, :, :], 0.0).then_inc(R(t, "_pad"), 1)

            padding("m0", lambda: wait_x(pool, 2))
            narrow_gpsimd(pool, "x1", False, lambda: wait_x(pool, 4))
            wait_x(pool, 6)
            G.memset(r_sa[:, :, 0], 0.0).then_inc(S("l2_zero"), 1)
            G.memset(r_sb[:, :, 0], 0.0).then_inc(S("l2_zero"), 1)
            G.memset(r_prev[:, :, 0], 0.0).then_inc(S("l2_zero"), 1)
            pool.wait_ge(S("l2_zero"), 3)
            for p in range(2):
                G.tensor_copy(r_prev[:, HB * p:HB * (p + 1), 1:P],
                              half(xT, p).rearrange("p (b t) -> p b t", b=HB)[:, :, 0:P - 1]).then_inc(S("l2_prev"), 1)
            narrow_gpsimd(pool, "x2", False, lambda: wait_x(pool, 7))
            narrow_gpsimd(pool, "f2", True, lambda: wait_x(pool, 8))
            padding("m2", lambda: pool.wait_ge(S("f2_x2"), 2))
            wait_x(pool, 11)
            G.memset(t_parts[:, :, :, :], 0.0).then_inc(R("m3", "_pad"), 1)


def _pack(i):
    import numpy as np
    f = np.float32

    def heads_rows(w):
        out = np.zeros((w.shape[0], NG, 4, 32), f)
        out[:, :, :, 0:HD] = w.reshape(w.shape[0], 4, NG, HD).transpose(0, 2, 1, 3)
        return out.reshape(w.shape[0], NG * P)

    def heads_bias(b):
        out = np.zeros((4, 32, NG), f)
        out[:, 0:HD, :] = b.reshape(4, NG, HD).transpose(0, 2, 1)
        return out.reshape(P, NG)

    def rows(w):
        out = np.zeros((P, w.shape[1]), f)
        out[0:w.shape[0]] = w
        return out

    def col(v):
        return rows(v.reshape(-1, 1))

    def doubled(w):
        return np.repeat(w.reshape(P, 8, HD), 2, axis=1).reshape(P, P)

    def swapped(w):
        return w.reshape(P, NH, 2, HD // 2)[:, :, ::-1, :].reshape(P, P)

    by_head = lambda w: w.reshape(P, XH, P)
    turned = lambda w: by_head(w).transpose(2, 1, 0).reshape(P, XH * P)
    n = np.arange(P)
    swap = np.zeros((P, P), f)
    swap[n[0::2], n[1::2]] = 1
    swap[n[1::2], n[0::2]] = -1
    inv_freq = (1.0 / np.power(f(10000.0), np.arange(0, HD, 2, dtype=f) / f(HD), dtype=f)).astype(f)
    ang = np.arange(P, dtype=f)[:, None] * inv_freq[None, :]
    cos, sin = np.zeros((4, 32, P), f), np.zeros((4, 32, P), f)
    cos[:, 0:HD] = np.concatenate([np.cos(ang), np.cos(ang)], 1).T
    sin[:, 0:HD] = np.concatenate([-np.sin(ang), np.sin(ang)], 1).T
    before = (n[:E, None] > n[None, :E]).astype(f).reshape(1, E * E)
    kv = i["L0_xattn_Wkv"]
    rot = i["L1_attn_rot_w"].reshape(3, P // 2, 2)
    natural = lambda w: w.reshape(3, P, P).transpose(1, 0, 2).reshape(P, 3 * P)
    wk2, wv2 = doubled(i["L2_ffn_wk"]), doubled(i["L2_ffn_wv"])
    parts = {
        "center": np.eye(P, dtype=f) - f(1 / P), "mean": np.full((P, P), 1 / P, f), "ident": np.eye(P, dtype=f),
        "l0_wk": i["L0_attn_Wk"].T, "l0_wr": i["L0_attn_Wr"].T, "l0_wv": i["L0_attn_Wv"].T, "l0_td": col(i["L0_attn_time_decay"]),
        "x0_wq": turned(i["L0_xattn_Wq"]), "x0_wk": turned(kv[:, :XH * P]), "x0_wv": turned(kv[:, XH * P:]),
        "x0_wo": i["L0_xattn_Wo"].reshape(XH, P, P).transpose(1, 0, 2).reshape(P, XH * P),
        "x0_bq": i["L0_xattn_bq"].reshape(XH, P).T, "x0_bv": i["L0_xattn_bkv"][XH * P:].reshape(XH, P).T,
        "x0_bo": col(i["L0_xattn_bo"]), "x0_gm": col(i["L0_xattn_gamma_media"]), "x0_bm": col(i["L0_xattn_beta_media"]),
        "x0_gl": col(i["L0_xattn_gamma_lat"]), "x0_bl": col(i["L0_xattn_beta_lat"]),
        "m0_router": i["L0_ffn_router_w"].T, "before": np.broadcast_to(before, (P, E * E)),
        "l1_rc": np.repeat(rot[:, :, 0], 2, axis=1).T, "l1_rs": np.repeat(rot[:, :, 1], 2, axis=1).T,
        "l1_scale": np.broadcast_to(i["L1_attn_scale"].reshape(1, 1), (P, 1)),
        "l1_bias": np.broadcast_to(i["L1_attn_bias"].reshape(1, 1), (P, 1)), "swap": swap,
        "x1_wq": heads_rows(i["L1_xattn_Wq"]), "x1_wk": heads_rows(i["L1_xattn_Wk"]), "x1_wv": i["L1_xattn_Wv"], "x1_wo": i["L1_xattn_Wo"],
        "x1_bq": heads_bias(i["L1_xattn_bq"]), "x1_bk": heads_bias(i["L1_xattn_bk"]), "x1_bv": col(i["L1_xattn_bv"]), "x1_bo": col(i["L1_xattn_bo"]),
        "f1_gate": natural(i["L1_ffn_w_gate"]), "f1_up": natural(i["L1_ffn_w_up"]), "f1_down": i["L1_ffn_w_down"],
        "l2_mk": col(i["L2_attn_mix_k"]), "l2_mv": col(i["L2_attn_mix_v"]), "l2_mr": col(i["L2_attn_mix_r"]),
        "l2_td": col(np.repeat(i["L2_attn_time_decay"], HD)), "l2_tf": col(np.repeat(i["L2_attn_time_first"], HD)),
        "l2_wk": i["L2_attn_W_key"].T, "l2_wv": i["L2_attn_W_value"].T, "l2_wr": i["L2_attn_W_receptance"].T, "l2_wo": i["L2_attn_W_output"].T,
        "headsum": (n[:, None] // HD == n[None, :] // HD).astype(f),
        "x2_wq": heads_rows(i["L2_xattn_wq"].T), "x2_wk": heads_rows(i["L2_xattn_wk"].T), "x2_wv": i["L2_xattn_wv"].T, "x2_wo": i["L2_xattn_wo"].T,
        "x2_bq": heads_bias(i["L2_xattn_bq"]), "x2_bk": heads_bias(i["L2_xattn_bk"]), "x2_bv": col(i["L2_xattn_bv"]), "x2_bo": col(i["L2_xattn_bo"]),
        "f2_ln1": col(i["L2_ffn_ln1_w"]), "f2_ln2": col(i["L2_ffn_ln2_w"]),
        "f2_wq": heads_rows(i["L2_ffn_wq"]), "f2_wqr": heads_rows(swapped(i["L2_ffn_wq"])),
        "f2_wk": heads_rows(wk2), "f2_wkr": heads_rows(swapped(wk2)), "f2_wv": wv2, "f2_wo": i["L2_ffn_wo"],
        "m2_router": i["L2_ffn_router_w"], "cos": cos.reshape(P, P), "sin": sin.reshape(P, P),
        "l3_alog": col(i["L3_attn_A_log"]), "l3_bg": col(i["L3_attn_bg"]), "l3_d": col(i["L3_attn_D"]), "l3_bout": col(i["L3_attn_bout"]),
        "l3_gamma": col(i["L3_attn_gamma"]), "l3_beta": col(i["L3_attn_beta"]),
        "l3_wb": i["L3_attn_WB"].T, "l3_wg": i["L3_attn_Wg"].T, "l3_wc": rows(i["L3_attn_WC"].T), "l3_wout": i["L3_attn_Wout"].T,
        "m3_router": i["L3_ffn_router_w"].T, "m3_sgate": i["L3_ffn_w_gate_shared"].T, "m3_sdown": rows(i["L3_ffn_w_down_shared"].T),
        "m3_bias": np.broadcast_to(i["L3_ffn_expert_bias"].reshape(1, NE), (P, NE)),
    }
    return np.concatenate([np.asarray(parts[name], f).reshape(P, cols) for name, cols in PACK], axis=1)


def kernel(**inputs):
    import ml_dtypes
    import numpy as np
    import concourse.bacc as bacc
    from concourse.bass_utils import run_bass_kernel_spmd

    i = {k: np.asarray(v) for k, v in inputs.items()}
    bf = ml_dtypes.bfloat16
    feature_major = lambda a: np.ascontiguousarray(a.transpose(2, 0, 1).reshape(P, T))
    token_major = lambda a: np.ascontiguousarray(a.transpose(1, 0, 2).reshape(P, T))

    sel8 = np.zeros((P, E, P), np.float32)
    for e in range(E):
        sel8[3 * e:3 * e + 3, e, :] = 1
    sel160 = np.zeros((P, 20, 2, 64), np.float32)
    for q in range(20):
        for el in range(2):
            sel160[(2 * q + el) * 3:(2 * q + el) * 3 + 3, q, el, :] = 1
    pairs = np.array([[20 * (j // 2) + 10 * (j % 2) + g for j in range(CHUNKS)] for g in range(GROUPS)])
    gate = i["L3_ffn_w_gate"].reshape(NE // 2, P, P).transpose(0, 2, 1)
    down = i["L3_ffn_w_down"].transpose(0, 2, 1).reshape(NE // 2, P, P)
    m3 = np.stack([gate[pairs], down[pairs]], axis=2).reshape(2 * GROUPS, 4, 2, P, P)
    m3 = m3.transpose(0, 3, 1, 2, 4).reshape(2 * GROUPS, P, 1024)
    w13, w2 = i["L0_ffn_w13"], i["L0_ffn_w2"]
    chunked = lambda w, ch, rows: w.reshape(E, ch, rows, P).transpose(0, 2, 1, 3).reshape(E, rows, ch * P)
    arrays = {
        "xT_in": feature_major(i["x"]), "ctxT_in": feature_major(i["ctx_1024"]), "ctx_in": token_major(i["ctx_1024"]),
        "mask_in": i["mask_Bx1xSxS2_bk1"].reshape(B, P, P).transpose(1, 0, 2).reshape(P, T),
        "pack_in": _pack(i),
        "sel8_in": sel8.reshape(P, E * P).astype(bf), "sel160_in": sel160.reshape(P, 20 * P).astype(bf),
        "caus_in": np.where(np.tril(np.ones((P, P), bool)), 0.0, -1e30).astype(bf), "identb_in": np.eye(P).astype(bf),
        "m0_up_in": w13, "m0_down_in": chunked(w2, M0_CH, M0_ROWS),
        "m2_up_in": np.concatenate([i["L2_ffn_w_gate"], i["L2_ffn_w_up"]], axis=2), "m2_down_in": chunked(i["L2_ffn_w_down"], M2_CH, M2_ROWS),
        "m3_in": m3,
    }
    nc = bacc.Bacc("TRN2", target_bir_lowering=False, num_devices=1)
    args = []
    for name, a in arrays.items():
        arrays[name] = a = np.ascontiguousarray(a)
        args.append(nc.dram_tensor(name, a.shape, mybir.dt.from_np(a.dtype), kind="ExternalInput").ap())
    args.append(nc.dram_tensor("out", (P, T), F32, kind="ExternalOutput").ap())
    program(nc, *args)
    r = run_bass_kernel_spmd(nc, [arrays], core_ids=[0])
    return np.ascontiguousarray(r.results[0]["out"].reshape(P, B, P).transpose(1, 2, 0))
```

```python
from contextlib import ExitStack

import concourse.bass as bass
from concourse import mybir

F32 = mybir.dt.float32
BF16 = mybir.dt.bfloat16
U8 = mybir.dt.uint8
ALU = mybir.AluOpType
ACT = mybir.ActivationFunctionType
AX = mybir.AxisListType

P = 128
B = 8
T = B * P
HALF = T // 2
HB = B // 2
NH, HD = 16, 8
VA = HD + 1
XH = 8
E = 8
NE, TOPK = 160, 8
GROUPS, CHUNKS = 10, 8
SETS = 4
SETE = NE // SETS
EPS = 1e-5
ROUND = 1.5 * 2.0 ** 23
QMAX = 32767.0
NEG = -1e15

PACK = [
    ("center", P), ("mean", P), ("ident", P),
    ("l0_wk", P), ("l0_wr", P), ("l0_wv", P), ("l0_td", 1),
    ("x0_wq", XH * P), ("x0_wk", XH * P), ("x0_wv", XH * P), ("x0_wo", XH * P),
    ("x0_bq", XH), ("x0_bv", XH), ("x0_bo", 1), ("x0_gm", 1), ("x0_bm", 1), ("x0_gl", 1), ("x0_bl", 1),
    ("m0_router", E), ("before", E * E),
    ("l1_rc", 3), ("l1_rs", 3), ("l1_scale", 1), ("l1_bias", 1), ("swap", P),
    ("headmask", NH), ("x1_wq", P), ("x1_wk", P), ("x1_wv", P), ("x1_wo", P),
    ("x1_bq", 1), ("x1_bk", 1), ("x1_bv", 1), ("x1_bo", 1),
    ("f1_gate", 3 * P), ("f1_up", 3 * P), ("f1_down", 3 * P),
    ("l2_mk", 1), ("l2_mv", 1), ("l2_mr", 1), ("l2_td", 1), ("l2_tf", 1),
    ("l2_wk", P), ("l2_wv", P), ("l2_wr", P), ("l2_wo", P), ("headsum", P),
    ("x2_wq", P), ("x2_wk", P), ("x2_wv", P), ("x2_wo", P),
    ("x2_bq", 1), ("x2_bk", 1), ("x2_bv", 1), ("x2_bo", 1),
    ("f2_ln1", 1), ("f2_ln2", 1), ("f2_wq", P), ("f2_wqr", P), ("f2_wk", P), ("f2_wkr", P),
    ("f2_wv", P), ("f2_wo", P), ("m2_router", E), ("cos", P), ("sin", P),
    ("l3_alog", 1), ("l3_bg", 1), ("l3_d", 1), ("l3_bout", 1), ("l3_gamma", 1), ("l3_beta", 1),
    ("l3_wb", 64), ("l3_wg", 64), ("l3_wc", P), ("l3_wout", P),
    ("m3_router", NE), ("m3_sgate", 64), ("m3_sdown", P), ("m3_bias", NE),
]
PACK_AT = {}
PACK_COLS = 0
for _name, _cols in PACK:
    PACK_AT[_name] = (PACK_COLS, _cols)
    PACK_COLS += _cols
PIECES = ["l0_wk", "x0_wq", "m0_router", "headmask", "l2_mk", "f2_ln1", None]
PIECE_ENDS = [PACK_AT[n][0] if n else PACK_COLS for n in PIECES]

M0_CH, M0_ROWS = 2, 128
M2_CH, M2_ROWS = 4, 112
LAYERS = 12


def program(nc, xT_in, ctxT_in, ctx_in, mask_in, pack_in, sel8_in, sel160_in, caus_in, identb_in,
            m0_up_in, m0_down_in, m2_up_in, m2_down_in, m3_in, out):
    ctx = ExitStack()
    with ctx:
        def sb(name, shape, dt=F32):
            return ctx.enter_context(nc.sbuf_tensor(name, shape, dt))

        sems = {}

        def S(name):
            if name not in sems:
                sems[name] = ctx.enter_context(nc.semaphore(name))
            return sems[name]

        ps = ctx.enter_context(nc.psum_tensor("ps", [P, 8, 512], F32))

        pack = sb("pack", [P, PACK_COLS])

        def W(name, lo=0, n=None):
            at, cols = PACK_AT[name]
            return pack[:, at + lo:at + (cols if n is None else lo + n)]

        xT = sb("xT", [P, T])
        ctxT = sb("ctxT", [P, T])
        ctx_tm = sb("ctx_tm", [P, T])
        mask8 = sb("mask8", [P, T], U8)
        maskb = sb("maskb", [P, T], BF16)
        caus = sb("caus", [P, P], BF16)
        identb = sb("identb", [P, P], BF16)
        sel8 = sb("sel8", [P, E * P], BF16)
        sel160 = sb("sel160", [P, 20 * P], BF16)
        hsum = sb("hsum", [P, T])
        sq = sb("sq", [P, T])
        rstd = sb("rstd", [P, T])
        small = sb("small", [P, 64])
        eps5 = small[:, 0:1]
        eps6 = small[:, 1:2]
        ring = sb("ring", [P, 2, 1408])
        arena = sb("arena", [P, 26048])

        def A(lo, *shape):
            n = 1
            for s in shape:
                n *= s
            v = arena[:, lo:lo + n]
            if len(shape) == 2:
                v = v.rearrange("p (a b) -> p a b", a=shape[0])
            elif len(shape) == 3:
                v = v.rearrange("p (a b c) -> p a b c", a=shape[0], b=shape[1])
            elif len(shape) == 4:
                v = v.rearrange("p (a b c d) -> p a b c d", a=shape[0], b=shape[1], c=shape[2])
            return v

        def half(buf, p):
            return buf[:, p * HALF:(p + 1) * HALF]

        def bank(n):
            return ps[:, n, :]

        ident = W("ident")

        def linked(eng, name):
            count = [0]

            def link(ins):
                count[0] += 1
                ins.then_inc(S(name), 1)
                eng.wait_ge(S(name), count[0])
            return link

        def piece(eng, name):
            n = next(i for i, e in enumerate(PIECE_ENDS) if PACK_AT[name][0] < e)
            eng.wait_ge(S(f"pack_{n}"), 16)

        block = ctx.enter_context(nc.Block())

        NORMS = ["ctx", "0", "lat", "1", "2", "3", "4", "5", "6", "7", "rms1", "rms2", "8", "inner", "9", "10", "11"]

        def nth(tag, p):
            return 2 * NORMS.index(tag) + p + 1

        def wait_x(eng, l, p=1):
            if l == 0:
                eng.wait_ge(S("x_loaded"), 16)
            else:
                eng.wait_ge(S("x_ready"), 2 * (l - 1) + p + 1)


        def norm_tensor(pe, tag, src, ready):
            for p in range(2):
                ready(p)
                nc.tensor.matmul(bank(2 + p), W("center"), half(src, p), start=True, stop=True).then_inc(S("norm_d"), 1)
            norm_mean(pe, tag)

        def norm_mean(pe, tag):
            for p in range(2):
                pe.wait_ge(S("norm_sq"), nth(tag, p))
                nc.tensor.matmul(bank(4 + p), W("mean"), half(sq, p), start=True, stop=True).then_inc(S("norm_var"), 1)

        def log_tables():
            nc.scalar.preload_act_table_set("natural_log_exp_and_others")

        def norm_scalar(act, tag, eps=None, src=None, root=False):
            for p in range(2):
                if src is None:
                    act.wait_ge(S("norm_d"), nd(tag, p))
                nc.scalar.activation(half(sq, p), bank(2 + p) if src is None else half(src, p),
                                     ACT.Square).then_inc(S("norm_sq"), 1)
            if root:
                for p in range(2):
                    act.wait_ge(S("norm_var"), nth(tag, p))
                    nc.scalar.activation(half(rstd, p), bank(4 + p), ACT.Sqrt, bias=eps5).then_inc(S("norm_root"), 1)
                log_tables()
            for p in range(2):
                if root:
                    act.wait_ge(S("norm_root"), p + 1)
                else:
                    act.wait_ge(S("norm_var"), nth(tag, p))
                nc.scalar.activation(half(rstd, p), half(rstd, p) if root else bank(4 + p), ACT.Ln,
                                     bias=0.0 if root else eps5 if eps is None else eps).then_inc(S("norm_ln"), 1)
            for p in range(2):
                act.wait_ge(S("norm_ln"), nth(tag, p))
                nc.scalar.activation(half(rstd, p), half(rstd, p), ACT.Exp, scale=-1.0 if root else -0.5).then_inc(S("norm_rstd"), 1)

        def nd(tag, p):
            n = NORMS.index(tag)
            return 2 * (n - sum(NORMS.index(r) < n for r in ("rms1", "rms2"))) + p + 1

        def residual_norm_tensor(pe, l):
            def ready(p):
                pe.wait_ge(S("sum_ready"), 2 * l + p + 1)
            norm_tensor(pe, str(l), hsum, ready)

        def residual_norm_vector(dve, l, bias=None, res=None, meanwhile=None):
            for p in range(2):
                dve.wait_ge(S("y_ready"), 2 * l + p + 1)
                nc.vector.scalar_tensor_tensor(out=half(hsum, p), in0=bank(p), scalar=0.0 if bias is None else bias,
                                               in1=half(xT if res is None else res, p),
                                               op0=ALU.add, op1=ALU.add).then_inc(S("sum_ready"), 1)
            if meanwhile:
                meanwhile()
            for p in range(2):
                dve.wait_ge(S("norm_rstd"), nth(str(l), p))
                nc.vector.tensor_tensor(half(xT, p), bank(2 + p), half(rstd, p), ALU.mult).then_inc(S("x_ready"), 1)

        x_q = A(0, XH, T)
        x_kv = A(8192, B, 2, P)
        x_kvt = A(10240, B, 2, P)
        x_m = A(12288, XH, P)
        x_u = A(13312, XH, P)
        x_c = A(14336, XH)
        x_qs = A(14400, 2, XH, P)
        x_kvs = A(16448, 2, 2, P)
        x_kvts = A(16960, 2, 2, P)
        x_p = A(17472, 2, 4, 2 * P)
        x_pt = A(19520, 2, 2, 512)
        x_nm = A(21568, 2, 4)
        x_sum = A(21576, 2, 4)
        x_rec = A(21584, 2, 4)
        x_bo = A(21592, 1)

        a_kb = A(0, NH, T)
        a_q = A(16384, T)
        a_k = A(17408, T)
        a_v = A(18432, B, NH, VA)
        a_vflat = A(18432, B * NH * VA)
        a_qs = A(19584, 2, P)
        a_p = A(19840, 2, NH // 2, P)
        a_pt = A(21888, 2, NH // 2, P)
        a_rope = A(19840, 2, 2, 2, HALF)
        a_cn = A(23936, B, P)
        a_oT = a_q
        a_mx = A(24960, 2, NH // 2)
        a_rec = A(24976, 2, NH)
        f_h = A(25024, T)
        f_x2 = A(6528, T)
        f_res = A(7552, T)

        m_lg = A(0, B, E)
        m_e = A(64, B, E)
        m_mx = A(128, B)
        m_gt = A(192, B, E, E)
        m_eq = A(704, B, E, E)
        m_rank = A(1216, B, E)
        m_w = A(1280, B, E)
        m_s = A(1344, B)
        m_z = A(1352, B)
        m_d = A(1360, B)
        m_parts = A(1408, B * P // 2).bitcast(BF16).rearrange("p (b c) -> p b c", b=B)
        m_wT = A(1920, T // 2).bitcast(BF16)
        m_xw = A(2432, 2, T)
        m_sg = A(4480, 2, HALF)
        m_hid = A(5504, 2, HALF)
        zeros = sb("zeros", [P, HALF], BF16)
        m_x2 = A(8576, T)

        g_c = small[:, 8:11]
        g_s = small[:, 11:14]
        g_n = small[:, 14:17]
        g_n2 = small[:, 17:20]
        g_a = small[:, 20:21]
        g_b = small[:, 21:22]
        g_rot = A(0, 3, P)
        g_t = A(384, 3, P)
        g_q = A(768, T)
        g_k = A(1792, T)
        g_v = A(2816, B, P)
        g_z = A(3840, B, P)
        g_pt = A(4864, B, P)
        g_av = A(5888, B, P)
        g_sq = A(6912, B, P)
        g_mx = A(7936, B)
        g_sm = A(7944, B)
        g_rc = A(7952, B)
        g_in = A(7960, B)

        q_ab = A(0, 36)
        q_sc = A(36, 36)
        q_inv = A(72, 36)
        q_w = A(128, 36, 32)
        q_wT = A(1280, 9, P)
        q_x = A(2432, T)
        q_up = A(3456, 3 * T)
        q_gate = A(6528, 3 * T)
        q_sig = A(9600, 3 * T)
        q_col = small[:, 24:29]
        q_s = small[:, 32:37]
        q_i = small[:, 40:45]
        ones1 = sb("ones1", [1, P])
        q_top = sb("q_top", [1, 8])

        r_prev = A(0, B, P)
        r_diff = A(1024, T)
        r_k = A(2048, T)
        r_v = A(3072, T)
        r_r = A(4096, T)
        r_ek = A(5120, T)
        r_ekv = A(6144, T)
        r_sa = A(7168, B, P + 1)
        r_sb = A(8200, B, P + 1)
        r_den = A(9232, T)
        r_sig = A(10256, T)
        r_dec = small[:, 48:49]
        r_u = small[:, 49:50]
        r_e = small[:, 50:51]

        s_sig = A(0, T)
        s_u = A(1024, T)
        s_st = A(2048, T)
        s_h = A(3072, T)
        s_hn = A(4096, T)
        s_a = small[:, 51:52]

        d_r = A(0, T)
        d_s = A(1024, T)
        d_w = small[:, 52:53]
        d_e = small[:, 53:54]

        e_a = A(0, T)

        t_p = A(0, B, NE)
        t_rep = A(1280, B, NE)
        t_top = A(2560, B, TOPK)
        t_s = A(2624, B)
        t_w = A(2688, B, NE)
        t_r1 = A(3968, B, NE)
        t_parts = A(5248, B * SETS * P // 2).bitcast(BF16).rearrange("p (b s c) -> p b s c", b=B, s=SETS)
        t_combT = A(7296, SETS * T // 2).bitcast(BF16).rearrange("p (s t) -> p s t", s=SETS)
        t_sg = A(9344, 2, HALF)
        t_hid = A(10368, 2, HALF)
        t_sh = A(11392, T)

        def bankb(n):
            return ps[:, n, :].bitcast(BF16)

        CREDIT = {"a_pt": 1, "a_cn": 2, "m_hid": 1}

        def credited(eng, *names):
            for name in names:
                eng.sem_inc(S(name), CREDIT.get(name, 1))

        WAVES, UNITS = 2 * B, (E * 2 * M0_CH, E * 2 * M2_CH)
        LEFT = {"a_kproj": 2, "a_qproj": 2, "a_q_ready": 2, "a_k_ready": 2, "a_kb0": NH, "a_kb1": NH, "a_vproj": 1, "a_v_ready": 1,
                "a_ones": 1, "a_slices": B, "a_scores": WAVES, "a_mx": WAVES, "a_z": WAVES, "a_p": WAVES, "a_turned": WAVES,
                "a_pt": WAVES, "a_weighed": WAVES, "a_rec": B, "a_cn": B, "a_oturned": 2, "a_oT": 2, "a_rope_k": 0, "a_rope_q": 0,
                "m_logits": 1, "m_lg": 1, "m_e": 1, "m_pad": 1, "m_parts": 3, "m_wturned": 1, "m_wT": 1, "m_spread": 2 * E, "m_xw": 2 * E,
                "m_gate": UNITS, "m_silu": UNITS, "m_up": UNITS, "m_hid": UNITS, "m_down": (UNITS[0] - 2, UNITS[1] - 2),
                "m_load0": 16 * E, "m_load1": 16 * E}
        RUN = {"x1": ("a", 0), "x2": ("a", 1), "f2": ("a", 2), "m0": ("m", 0), "m2": ("m", 1), "m3": ("m", 2)}

        def R(t, name):
            return S(RUN[t][0] + name)

        def waits(eng, t):
            kind, run = RUN[t]

            def before(name):
                left = LEFT[kind + name]
                return sum(left[0:run]) if isinstance(left, tuple) else run * left
            return lambda name, v: eng.wait_ge(S(kind + name), v + before(name) + CREDIT.get(kind + name, 0))

        def credited_once(eng, t, *names):
            if RUN[t][1] == 0:
                credited(eng, *(RUN[t][0] + name for name in names))


        def narrow_keys_tensor(pe, t):
            for p in range(2):
                nc.tensor.matmul(bank(6 + p), W(t + "_wk"), half(ctxT, p), start=True, stop=True).then_inc(R(t, "_kproj"), 1)

        def narrow_tensor(pe, t, qsrc, ksrc, rope, mask, wo, done="y_ready"):
            wait = waits(pe, t)
            mm = nc.tensor.matmul
            if rope:
                for first, names, signal in ((4, ("_wk", "_wkr"), "_kproj"), (0, ("_wq", "_wqr"), "_qproj")):
                    for p in range(2):
                        for k, name in enumerate(names):
                            ins = mm(bank(first + 2 * k + p), W(t + name), half(qsrc, p), start=True, stop=True)
                        ins.then_inc(R(t, signal), 1)
                wait("_rope_k", 4)
            else:
                for p in range(2):
                    mm(bank(p), W(t + "_wq"), half(qsrc, p), start=True, stop=True).then_inc(R(t, "_qproj"), 1)
                wait("_k_ready", 2)
            for b in range(B):
                ins = mm(ps[:, 6 + b // HB, (b % HB) * P:(b % HB + 1) * P], ksrc[:, b * P:(b + 1) * P], W(t + "_wv"), start=True, stop=True)
            ins.then_inc(R(t, "_vproj"), 1)
            wait("_q_ready", 2)

            def scores(b, v, slot):
                if v == 0:
                    wait("_slices", b + 1)
                for jj in range(2):
                    sbank = 2 * v + jj
                    if mask is not None:
                        rows = mask if mask is caus else mask[:, bass.ds(b * P, P)]
                        mm(bank(sbank), identb[:, :], (rows[:, :] if mask is caus else rows).unsqueeze(1).to_broadcast([P, 4, P]),
                           start=True, stop=False, skip_group_check=True)
                    ins = mm(bank(sbank), a_qs[:, slot, :], a_kb[:, 4 * sbank:4 * sbank + 4, bass.ds(b * P, P)],
                             start=mask is None, stop=True, skip_group_check=True)
                ins.then_inc(R(t, "_scores"), 1)

            def turn(v, w):
                wait("_p", w + 1)
                wait("_pt", w)
                for n in range(NH // 2):
                    ins = nc.tensor.transpose(ps[:, 4 + n // 4, (n % 4) * P:(n % 4 + 1) * P], a_p[:, v, n, :], ident)
                ins.then_inc(R(t, "_turned"), 1)

            def weigh(b, v, w, slot):
                if v == 0:
                    wait("_cn", b - 1)
                wait("_pt", w + 1)
                for n in range(NH // 2):
                    h = NH // 2 * v + n
                    ins = mm(ps[:, 6 + slot, h * VA:(h + 1) * VA], a_pt[:, v, n, :],
                             a_vflat[:, bass.ds(b * (NH * VA) + h * VA, VA)], start=True, stop=True, skip_group_check=True)
                ins.then_inc(R(t, "_weighed"), 1)

            def body(i, final):
                for k in range(4):
                    b, v, w = 2 * i + k // 2, k % 2, 4 * i + k
                    turn(v, w)
                    if not (final and k >= 2):
                        scores(2 * i + k // 2 + 1, v, (k // 2 + 1) % 2)
                    weigh(b, v, w, k // 2)

            wait("_kb0", NH)
            scores(0, 0, 0)
            scores(0, 1, 0)
            wait("_kb1", NH)
            wait("_v_ready", 1)
            with pe.Fori(0, B // 2 - 1) as i:
                body(i, False)
            body(B // 2 - 1, True)
            for p in range(2):
                wait("_cn", HB * (p + 1))
                for b in range(HB):
                    ins = nc.tensor.transpose(ps[:, 2 + p, b * P:(b + 1) * P], a_cn[:, HB * p + b, :], ident)
                ins.then_inc(R(t, "_oturned"), 1)
            for p in range(2):
                wait("_oT", p + 1)
                mm(bank(p), wo, half(a_oT, p), start=True, stop=True).then_inc(S(done), 1)

        def spread_keys(t, heads, scaled):
            for p in range(2):
                for h in heads:
                    scaled(half(a_kb[:, h, :], p), half(a_k, p), W("headmask")[:, h:h + 1]).then_inc(R(t, f"_kb{p}"), 1)

        def narrow_scalar(act, t, rope, bv, scale, heads, bq=None):
            wait = waits(act, t)
            credited_once(act, t, "_pt")
            if not rope:
                for p in range(2):
                    wait("_qproj", p + 1)
                    nc.scalar.activation(half(a_q, p), bank(p), ACT.Identity, bias=bq).then_inc(R(t, "_q_ready"), 1)
            wait("_k_ready", 2)
            spread_keys(t, heads, lambda dst, src, col: nc.scalar.activation(dst, src, ACT.Copy, scale=col))

            def exps(v, w):
                wait("_z", w + 1)
                nc.scalar.activation(a_p[:, v], a_p[:, v], ACT.Exp, scale=scale).then_inc(R(t, "_p"), 1)

            def copies(v, w):
                wait("_turned", w + 1)
                nc.scalar.activation(a_pt[:, v], ps[:, 4:6, :].rearrange("p a (n q) -> p (a n) q", n=4), ACT.Copy).then_inc(R(t, "_pt"), 1)

            def body(i, final):
                for k in range(4):
                    w = 4 * i + k
                    copies(k % 2, w)
                    if not (final and k >= 2):
                        exps(k % 2, w + 2)

            exps(0, 0)
            exps(1, 1)
            with act.Fori(0, B // 2 - 1) as i:
                body(i, False)
            body(B // 2 - 1, True)
            for p in range(2):
                wait("_oturned", p + 1)
                nc.scalar.activation(half(a_oT, p), bank(2 + p), ACT.Identity, bias=0.0 if bv is None else bv).then_inc(R(t, "_oT"), 1)

        def narrow_keys_vector(dve, t, heads, bk):
            for p in range(2):
                waits(dve, t)("_kproj", p + 1)
                nc.vector.tensor_scalar(half(a_k, p), bank(6 + p), bk, None, ALU.add).then_inc(R(t, "_k_ready"), 1)
            narrow_spread_vector(dve, t, heads)

        def narrow_spread_vector(dve, t, heads):
            waits(dve, t)("_k_ready", 2)
            spread_keys(t, heads, lambda dst, src, col: nc.vector.tensor_scalar(dst, src, col, None, ALU.mult))

        def narrow_rope_vector(dve, t):
            wait = waits(dve, t)
            for k, (first, proj, part) in enumerate(((4, "_kproj", "_rope_k"), (0, "_qproj", "_rope_q"))):
                for p in range(2):
                    wait(proj, p + 1)
                    for m, tab in enumerate(("cos", "sin")):
                        nc.vector.tensor_tensor(a_rope[:, k, m, p].rearrange("p (b t) -> p b t", b=HB),
                                                bank(first + 2 * m + p).rearrange("p (b t) -> p b t", b=HB),
                                                W(tab).unsqueeze(1).to_broadcast([P, HB, P]), ALU.mult).then_inc(R(t, part), 1)
            for p in range(2):
                wait("_rope_k", 2 * p + 2)
                nc.vector.tensor_tensor(half(a_k, p), a_rope[:, 0, 0, p], a_rope[:, 0, 1, p], ALU.add).then_inc(R(t, "_k_ready"), 1)

        def narrow_vector(dve, t):
            wait = waits(dve, t)
            credited_once(dve, t, "_cn")
            wait("_vproj", 1)
            wait("_ones", 1)
            for p in range(2):
                ins = nc.vector.tensor_copy(a_v[:, HB * p:HB * (p + 1), :, 0:HD].rearrange("p b h d -> p (b h) d"),
                                            bank(6 + p).rearrange("p (n d) -> p n d", d=HD))
            ins.then_inc(R(t, "_v_ready"), 1)

            def maxima(v, w, first=False):
                wait("_scores", w + 1)
                sc = ps[:, 2 * v:2 * v + 2, :].rearrange("p a (g k) -> p (a g) k", g=4)
                nc.vector.tensor_reduce(a_mx[:, v], sc, AX.X, ALU.max).then_inc(R(t, "_mx"), 1)
                wait("_mx", w + 1)
                if not first:
                    wait("_turned", w - 1)
                nc.vector.tensor_tensor(a_p[:, v], sc, a_mx[:, v].unsqueeze(2).to_broadcast([P, NH // 2, P]),
                                        ALU.subtract).then_inc(R(t, "_z"), 1)

            def outputs(b, slot):
                wait("_weighed", 2 * b + 2)
                o = ps[:, 6 + slot, 0:NH * VA].rearrange("p (h d) -> p h d", d=VA)
                nc.vector.reciprocal(a_rec[:, slot], o[:, :, HD]).then_inc(R(t, "_rec"), 1)
                wait("_rec", b + 1)
                nc.vector.tensor_tensor(a_cn[:, bass.ds(b, 1), :].rearrange("p o (h d) -> p (o h) d", d=HD), o[:, :, 0:HD],
                                        a_rec[:, slot].unsqueeze(2).to_broadcast([P, NH, HD]), ALU.mult).then_inc(R(t, "_cn"), 1)

            def body(i, final):
                for k in range(4):
                    if not (final and k >= 2):
                        maxima(k % 2, 4 * i + k + 2)
                    if k % 2 == 1:
                        outputs(2 * i + k // 2, k // 2)

            maxima(0, 0, True)
            maxima(1, 1, True)
            with dve.Fori(0, B // 2 - 1) as i:
                body(i, False)
            body(B // 2 - 1, True)

        def narrow_gpsimd(pool, t, rope, before):
            wait = waits(pool, t)
            before()
            nc.gpsimd.memset(a_v[:, :, :, HD], 1.0).then_inc(R(t, "_ones"), 1)
            if rope:
                for p in range(2):
                    wait("_rope_q", 2 * p + 2)
                    nc.gpsimd.tensor_tensor(half(a_q, p), a_rope[:, 1, 0, p], a_rope[:, 1, 1, p], ALU.add).then_inc(R(t, "_q_ready"), 1)
            wait("_q_ready", 2)

            def slices(b, slot):
                nc.gpsimd.tensor_copy(a_qs[:, slot], a_q[:, bass.ds(b * P, P)]).then_inc(R(t, "_slices"), 1)

            slices(0, 0)
            slices(1, 1)
            with pool.Fori(1, B // 2) as i:
                for slot in range(2):
                    wait("_scores", 4 * i + 2 * slot - 2)
                    slices(2 * i + slot, slot)


        def route_tensor(pe, t, src):
            for b in range(B):
                ins = nc.tensor.matmul(ps[:, 2, b * E:(b + 1) * E], src[:, b * P:(b + 1) * P], W(t + "_router"),
                                       start=True, stop=True, skip_group_check=True)
            ins.then_inc(R(t, "_logits"), 1)
            waits(pe, t)("_parts", 3)
            waits(pe, t)("_pad", 1)
            for b in range(B):
                ins = nc.tensor.transpose(bankb(3)[:, b * P:(b + 1) * P], m_parts[:, b, :], identb[:, :])
            ins.then_inc(R(t, "_wturned"), 1)

        def route_scalar(act, t):
            waits(act, t)("_lg", 1)
            nc.scalar.activation(m_e[:, :, :], m_lg[:, :, :], ACT.Exp).then_inc(R(t, "_e"), 1)

        def route_vector(dve, t, zterm, link):
            V = nc.vector
            piece(dve, "before")
            waits(dve, t)("_logits", 1)
            lg = ps[:, 2, 0:B * E].rearrange("p (b e) -> p b e", b=B)
            link(V.tensor_reduce(m_mx, lg, AX.X, ALU.max))
            V.tensor_tensor(m_lg, lg, m_mx.unsqueeze(2).to_broadcast([P, B, E]), ALU.subtract).then_inc(R(t, "_lg"), 1)
            waits(dve, t)("_e", 1)
            mine = m_e.unsqueeze(3).to_broadcast([P, B, E, E])
            other = m_e.unsqueeze(2).to_broadcast([P, B, E, E])
            before = W("before").rearrange("p (a c) -> p a c", a=E).unsqueeze(1).to_broadcast([P, B, E, E])
            link(V.tensor_tensor(m_eq, other, mine, ALU.is_equal))
            link(V.tensor_tensor(m_eq, m_eq, before, ALU.mult))
            link(V.tensor_tensor(m_gt, other, mine, ALU.is_gt))
            link(V.tensor_tensor(m_gt, m_gt, m_eq, ALU.add))
            link(V.tensor_reduce(m_rank, m_gt, AX.X, ALU.add))
            if zterm:
                link(V.tensor_reduce(m_z, m_e, AX.X, ALU.add))
            link(V.scalar_tensor_tensor(out=m_w, in0=m_rank, scalar=1.5, in1=m_e, op0=ALU.is_lt, op1=ALU.mult))
            link(V.tensor_reduce(m_s, m_w, AX.X, ALU.add))
            if zterm:
                link(V.scalar_tensor_tensor(out=m_s, in0=m_z, scalar=zterm, in1=m_s, op0=ALU.mult, op1=ALU.add))
            link(V.reciprocal(m_d, m_s))
            link(V.tensor_tensor(m_w, m_w, m_d.unsqueeze(2).to_broadcast([P, B, E]), ALU.mult))
            waits(dve, t)("_pad", 1)
            for k in range(3):
                part = m_parts[:, :, k:3 * E:3]
                ins = V.tensor_copy(part, m_w)
                ins.then_inc(R(t, "_parts"), 1)
                if k < 2:
                    waits(dve, t)("_parts", k + 1)
                    link(V.tensor_tensor(m_w, m_w, part, ALU.subtract))
            waits(dve, t)("_wturned", 1)
            V.tensor_copy(m_wT, bankb(3)).then_inc(R(t, "_wT"), 1)

        def mix_tensor(pe, t, src, CH, ROWS, l):
            wait = waits(pe, t)
            mm = nc.tensor.matmul
            UPE = 2 * CH
            wait("_wT", 1)
            pe.wait_ge(S("filled"), 4)
            for p in range(2):
                mm(bank(p), zeros[:, 0:P], zeros[:, :], start=True, stop=False, skip_group_check=True)

            def spread(e):
                for p in range(2):
                    wait("_xw", 2 * e + p - 1) if not isinstance(e, int) or e >= 1 else None
                    mm(bank(6 + p), sel8[:, bass.ds(e * P, P)], half(m_wT, p), start=True, stop=True).then_inc(R(t, "_spread"), 1)

            def up(e, slot, c, p, n):
                if c == 0 and p == 0:
                    wait(f"_load{slot}", 32 * ((e - slot) // 2 + 1) if isinstance(e, int) else 16 * (e - slot) + 32)
                wait("_hid", n - 1) if not isinstance(n, int) or n >= 2 else None
                mm(ps[0:ROWS, 2 + p, :], ring[:, slot, c * ROWS:(c + 1) * ROWS], half(src, p), start=True, stop=True).then_inc(R(t, "_gate"), 1)
                wait("_xw", 2 * e + p + 1)
                mm(ps[0:ROWS, 4 + p, :], ring[:, slot, (CH + c) * ROWS:(CH + c + 1) * ROWS], half(m_xw[:, slot], p),
                   start=True, stop=True).then_inc(R(t, "_up"), 1)

            def down(slot, c, p, n, final):
                wait("_hid", n + 1)
                at = 2 * CH * ROWS + c * P
                ins = mm(bank(p), ring[0:ROWS, slot, at:at + P], m_hid[0:ROWS, p], start=False, stop=final, skip_group_check=True)
                ins.then_inc(S("y_ready") if final else R(t, "_down"), 1)

            def body(i, last_pair):
                for slot in range(2):
                    e = 2 * i + slot
                    last_expert = last_pair and slot == 1
                    for u in range(UPE):
                        n = UPE * e + u
                        if u == UPE // 2 and not last_expert:
                            spread(e + 1)
                        if u < UPE - 1:
                            up(e, slot, (u + 1) // 2, (u + 1) % 2, n + 1)
                        elif not last_expert:
                            up(e + 1, 1 - slot, 0, 0, n + 1)
                        down(slot, u // 2, u % 2, n, last_expert and u >= UPE - 2)

            spread(0)
            up(0, 0, 0, 0, 0)
            with pe.Fori(0, E // 2 - 1) as i:
                body(i, False)
            body(E // 2 - 1, True)

        def mix_scalar(act, t, CH, ROWS):
            def unit(n, p):
                waits(act, t)("_gate", n + 1)
                nc.scalar.activation(m_sg[0:ROWS, p], ps[0:ROWS, 2 + p, :], ACT.Silu).then_inc(R(t, "_silu"), 1)
            nc.scalar.preload_act_table(ACT.Silu)
            with act.Fori(0, E * CH) as i:
                for p in range(2):
                    unit(2 * i + p, p)
            log_tables()

        def mix_vector(dve, t, src, CH, ROWS):
            wait = waits(dve, t)
            UPE = 2 * CH
            credited_once(dve, t, "_hid")

            def weigh(e, slot):
                for p in range(2):
                    wait("_spread", 2 * e + p + 1)
                    nc.vector.tensor_tensor(half(m_xw[:, slot], p), half(src, p), bank(6 + p), ALU.mult).then_inc(R(t, "_xw"), 1)

            def hidden(n, p):
                wait("_silu", n + 1)
                wait("_up", n + 1)
                nc.vector.tensor_tensor(m_hid[0:ROWS, p], m_sg[0:ROWS, p], ps[0:ROWS, 4 + p, :], ALU.mult).then_inc(R(t, "_hid"), 1)

            def body(i, last_pair):
                for slot in range(2):
                    e = 2 * i + slot
                    for u in range(UPE):
                        hidden(UPE * e + u, u % 2)
                        if u == UPE // 2 and not (last_pair and slot == 1):
                            weigh(e + 1, 1 - slot)

            weigh(0, 0)
            with dve.Fori(0, E // 2 - 1) as i:
                body(i, False)
            body(E // 2 - 1, True)

        def mix_load(sp, t, up_in, down_in, CH, ROWS):
            UPE = 2 * CH

            def load(e, slot):
                sp.dma_start(ring[:, slot, 0:2 * CH * ROWS], up_in[bass.ds(e, 1), :, :].rearrange("e p n -> p (e n)")).then_inc(R(t, f"_load{slot}"), 16)
                sp.dma_start(ring[0:ROWS, slot, 2 * CH * ROWS:2 * CH * ROWS + CH * P],
                             down_in[bass.ds(e, 1), :, :].rearrange("e p n -> p (e n)")).then_inc(R(t, f"_load{slot}"), 16)

            load(0, 0)
            load(1, 1)
            with sp.Fori(1, E // 2) as i:
                for slot in range(2):
                    waits(sp, t)("_down", UPE * (2 * i + slot - 1))
                    load(2 * i + slot, slot)

        SCALE8 = HD ** -0.5

        @block.sync
        def _(sp):
            def load_piece(n):
                lo = PIECE_ENDS[n - 1] if n else 0
                sp.dma_start(pack[:, lo:PIECE_ENDS[n]], pack_in[:, lo:PIECE_ENDS[n]]).then_inc(S(f"pack_{n}"), 16)
            sp.dma_start(ctxT[:, :], ctxT_in).then_inc(S("ctx_loaded"), 16)
            load_piece(0)
            sp.dma_start(xT[:, :], xT_in).then_inc(S("x_loaded"), 16)
            load_piece(1)
            load_piece(2)
            sp.dma_start(identb[:, :], identb_in).then_inc(S("consts"), 16)
            sp.dma_start(sel8[:, :], sel8_in).then_inc(S("consts"), 16)
            sp.dma_start(caus[:, :], caus_in).then_inc(S("consts"), 16)
            sp.dma_start(sel160[:, :], sel160_in).then_inc(S("consts"), 16)
            load_piece(3)
            sp.dma_start(mask8[:, :], mask_in).then_inc(S("mask_loaded"), 16)
            for n in range(4, len(PIECES)):
                load_piece(n)
            sp.dma_start(ctx_tm[:, :], ctx_in).then_inc(S("ctxtm_loaded"), 16)
            mix_load(sp, "m0", m0_up_in, m0_down_in, M0_CH, M0_ROWS)
            sp.wait_ge(S("y_ready"), 6)
            mix_load(sp, "m2", m2_up_in, m2_down_in, M2_CH, M2_ROWS)
            sp.wait_ge(S("y_ready"), 18)

            def load(n, slot):
                sp.dma_start(ring[:, slot, 0:1024], m3_in[bass.ds(n, 1), :, :].rearrange("e p n -> p (e n)")).then_inc(R("m3", f"_load{slot}"), 16)
            load(0, 0)
            load(1, 1)
            with sp.Fori(1, GROUPS) as i:
                for slot in range(2):
                    waits(sp, "m3")("_down", 16 * i + 8 * slot - 8)
                    load(2 * i + slot, slot)
            for p in range(2):
                sp.wait_ge(S("x_ready"), 2 * (LAYERS - 1) + p + 1)
                sp.dma_start(half(out, p), half(xT, p)).then_inc(S("stored"), 16)
            sp.wait_ge(S("stored"), 32)

        @block.tensor
        def _(pe):
            mm = nc.tensor.matmul
            pe.wait_ge(S("pack_0"), 16)

            def ctx_ready(p):
                pe.wait_ge(S("ctx_loaded"), 16)
            norm_tensor(pe, "ctx", ctxT, ctx_ready)
            piece(pe, "l0_wk")
            wait_x(pe, 0)
            pe.wait_ge(S("norm_out"), 2)
            for p in range(2):
                mm(bank(2 + p), W("l0_wk"), half(xT, p), start=True, stop=True).then_inc(S("l0_k"), 1)
                mm(bank(4 + p), W("l0_wr"), half(xT, p), start=True, stop=True).then_inc(S("l0_r"), 1)
            piece(pe, "x0_wq")
            for h in range(XH):
                ins = mm(ps[:, 6 + h // 4, (h % 4) * P:(h % 4 + 1) * P], W("x0_wq", h * P, P), W("x0_wk", h * P, P),
                         start=True, stop=True, skip_group_check=True)
            ins.then_inc(S("x0_mw"), 1)
            pe.wait_ge(S("x0_m"), 1)
            for h in range(XH):
                ins = mm(ps[:, 6 + h // 4, (h % 4) * P:(h % 4 + 1) * P], W("x0_wv", h * P, P), W("x0_wo", h * P, P),
                         start=True, stop=True, skip_group_check=True)
            ins.then_inc(S("x0_uw"), 1)
            pe.wait_ge(S("x0_u"), 1)
            for h in range(XH):
                ins = mm(ps[:, 6, h:h + 1], W("x0_wk", h * P, P), W("x0_bq", h, 1), start=True, stop=True, skip_group_check=True)
            for h in range(XH):
                ins = mm(ps[:, 7, 0:1], W("x0_wo", h * P, P), W("x0_bv", h, 1), start=(h == 0), stop=(h == XH - 1), skip_group_check=True)
            ins.then_inc(S("x0_bw"), 1)
            for p in range(2):
                pe.wait_ge(S("l0_gated"), p + 1)
                mm(bank(p), W("l0_wv"), half(d_s, p), start=True, stop=True).then_inc(S("y_ready"), 1)
            residual_norm_tensor(pe, 0)

            norm_tensor(pe, "lat", xT, lambda p: wait_x(pe, 1, p))
            pe.wait_ge(S("norm_out"), 4)
            pe.wait_ge(S("x0_bvec"), 1)
            for b in range(B):
                for s in range(2):
                    ins = nc.tensor.transpose(ps[:, b // 2, (b % 2 * 2 + s) * P:(b % 2 * 2 + s + 1) * P], x_kv[:, b, s, :], ident)
                ins.then_inc(S("x0_kvt"), 1)
            for h in range(XH):
                for p in range(2):
                    n = 2 * h + p
                    if n >= 4:
                        pe.wait_ge(S("x0_q"), n - 3)
                    mm(bank(4 + n % 4), x_m[:, h, :], x_kv[:, HB * p:HB * (p + 1), 1, :], start=True, stop=True).then_inc(S("x0_qmm"), 1)
            pe.wait_ge(S("x0_q"), 16)
            pe.wait_ge(S("x0_kvt_sb"), 4)

            def x_scores(b, v, w, slot):
                if v == 0:
                    pe.wait_ge(S("x0_slices"), 3 * b + 3)
                if not isinstance(w, int) or w >= 2:
                    pe.wait_ge(S("x0_p"), 4 * (w - 1) + 1)
                for i in range(4):
                    ins = mm(ps[:, 2 * v + i // 2, (i % 2) * 256:(i % 2 + 1) * 256], x_qs[:, slot, 4 * v + i, :],
                             x_kvs[:, slot].rearrange("p s k -> p (s k)"), start=True, stop=True, skip_group_check=True)
                ins.then_inc(S("x0_scores"), 1)

            def x_turn(v, w):
                pe.wait_ge(S("x0_pn"), 4 * (w + 1))
                pe.wait_ge(S("x0_ptA"), w + 1)
                pe.wait_ge(S("x0_ptB"), w + 1)
                for s in range(2):
                    for i in range(4):
                        ins = nc.tensor.transpose(ps[:, 4 + s, i * P:(i + 1) * P], x_p[:, v, i, s * P:(s + 1) * P], ident)
                ins.then_inc(S("x0_turned"), 1)

            def x_weigh(v, w, slot, first):
                pe.wait_ge(S("x0_ptA"), w + 2)
                pe.wait_ge(S("x0_ptB"), w + 2)
                pe.wait_ge(S("x0_o"), first + 1)
                for s in range(2):
                    ins = mm(bank(6 + v), x_kvts[:, slot, s, :], x_pt[:, v, s, :], start=(s == 0), stop=(s == 1))
                ins.then_inc(S("x0_weighed"), 1)

            def x_body(i, final):
                for k in range(4):
                    w = 4 * i + k
                    if not (final and k == 3):
                        x_scores(2 * i + (k + 1) // 2, (k + 1) % 2, w + 1, (k + 1) // 2 % 2)
                    x_turn(k % 2, w)
                    x_weigh(k % 2, w, k // 2, w if k == 0 else w - 1)

            credited(pe, "x0_turned")
            x_scores(0, 0, 0, 0)
            with pe.Fori(0, B // 2 - 1) as i:
                x_body(i, False)
            x_body(B // 2 - 1, True)
            pe.wait_ge(S("x0_o"), 2 * B + 1)
            for p in range(2):
                for h in range(XH):
                    ins = mm(bank(p), x_u[:, h, :], half(x_q[:, h, :], p), start=(h == 0), stop=(h == XH - 1))
                ins.then_inc(S("y_ready"), 1)
            residual_norm_tensor(pe, 1)

            piece(pe, "m0_router")
            pe.wait_ge(S("consts"), 64)
            wait_x(pe, 2)
            route_tensor(pe, "m0", xT)
            mix_tensor(pe, "m0", xT, M0_CH, M0_ROWS, 2)
            residual_norm_tensor(pe, 2)

            pe.wait_ge(S("l1_rot"), 1)
            wait_x(pe, 3)
            for p in range(2):
                mm(bank(p), g_rot[:, 0, :], half(xT, p), start=True, stop=True).then_inc(S("l1_qmm"), 1)
                mm(bank(2 + p), g_rot[:, 1, :], half(xT, p), start=True, stop=True).then_inc(S("l1_kmm"), 1)
                for b in range(HB * p, HB * (p + 1)):
                    ins = mm(ps[:, 4 + p, (b % HB) * P:(b % HB + 1) * P], xT[:, b * P:(b + 1) * P], g_rot[:, 2, :],
                             start=True, stop=True, skip_group_check=True)
                ins.then_inc(S("l1_vmm"), 1)
            for p in range(2):
                pe.wait_ge(S("l1_q"), p + 1)
                pe.wait_ge(S("l1_k"), p + 1)
                for b in range(HB * p, HB * (p + 1)):
                    ins = mm(ps[:, 6 + p, (b % HB) * P:(b % HB + 1) * P], g_q[:, b * P:(b + 1) * P], g_k[:, b * P:(b + 1) * P],
                             start=True, stop=True, skip_group_check=True)
                ins.then_inc(S("l1_scores"), 1)
            for p in range(2):
                pe.wait_ge(S("l1_e"), p + 1)
                for b in range(HB * p, HB * (p + 1)):
                    ins = nc.tensor.transpose(ps[:, p, (b % HB) * P:(b % HB + 1) * P], g_z[:, b, :], ident)
                ins.then_inc(S("l1_turned"), 1)
            for p in range(2):
                pe.wait_ge(S("l1_pt"), p + 1)
                pe.wait_ge(S("l1_v"), p + 1)
                for b in range(HB * p, HB * (p + 1)):
                    ins = mm(ps[:, 2 + p, (b % HB) * P:(b % HB + 1) * P], g_pt[:, b, :], g_v[:, b, :],
                             start=True, stop=True, skip_group_check=True)
                ins.then_inc(S("l1_weighed"), 1)
            for p in range(2):
                pe.wait_ge(S("l1_out"), p + 1)
                for b in range(HB * p, HB * (p + 1)):
                    ins = nc.tensor.transpose(ps[:, p, (b % HB) * P:(b % HB + 1) * P], g_av[:, b, :], ident)
                ins.then_inc(S("y_ready"), 1)
            residual_norm_tensor(pe, 3)

            piece(pe, "x1_wk")
            pe.wait_ge(S("ctx_loaded"), 16)
            narrow_keys_tensor(pe, "x1")
            pe.wait_ge(S("maskb"), 1)
            wait_x(pe, 4)
            narrow_tensor(pe, "x1", xT, ctxT, False, maskb, W("x1_wo"))
            residual_norm_tensor(pe, 4)

            pe.wait_ge(S("f1_wq"), 1)
            wait_x(pe, 5)
            for n in range(9):
                ins = nc.tensor.transpose(ps[:, 5 + n // 4, (n % 4) * P:(n % 4 + 1) * P],
                                          q_w[:, 4 * n:4 * n + 4, :].rearrange("p a k -> p (a k)"), ident)
            ins.then_inc(S("f1_wturned"), 1)

            def largest(n):
                pe.wait_ge(S("f1_col"), n + 1)
                nc.tensor.transpose(ps[0:1, 0, 0:P], q_col[:, n:n + 1], ident).then_inc(S("f1_colT"), 1)
                pe.wait_ge(S("f1_top"), n + 1)
                mm(ps[:, 1, 0:1], ones1[:, :], q_top[:, n:n + 1], start=True, stop=True).then_inc(S("f1_topB"), 1)

            pe.wait_ge(S("filled"), 4)
            largest(0)
            pe.wait_ge(S("f1_wT"), 1)
            pe.wait_ge(S("f1_xq"), 1)
            for k in range(2):
                for c in range(3):
                    for p in range(2):
                        if k:
                            pe.wait_ge(S("f1_up"), 2 * c + p + 1)
                        mm(bank(2 + 2 * c + p), q_wT[:, 3 * (1 - k) + c, :], half(q_x, p), start=True, stop=True).then_inc(S("f1_mm"), 1)
            for n in range(1, 5):
                largest(n)
            pe.wait_ge(S("f1_o"), 1)
            for p in range(2):
                for c in range(3):
                    ins = mm(bank(p), q_wT[:, 6 + c, :], q_up[:, c * T + p * HALF:c * T + (p + 1) * HALF], start=(c == 0), stop=(c == 2))
                ins.then_inc(S("y_ready"), 1)
            residual_norm_tensor(pe, 5)

            piece(pe, "l2_wk")
            for p in range(2):
                for k, (name, src) in enumerate((("l2_wk", r_k), ("l2_wv", r_v), ("l2_wr", r_r))):
                    pe.wait_ge(S("l2_mix"), 3 * p + k + 1)
                    mm(bank(2 * k + p), W(name), half(src, p), start=True, stop=True).then_inc(S(f"{name}_mm"), 1)
            for p in range(2):
                pe.wait_ge(S("l2_ek"), p + 1)
                mm(bank(6 + p), W("headsum"), half(r_ek, p), start=True, stop=True).then_inc(S("l2_bsum"), 1)
            for p in range(2):
                pe.wait_ge(S("l2_out"), p + 1)
                mm(bank(p), W("l2_wo"), half(r_k, p), start=True, stop=True).then_inc(S("y_ready"), 1)
            residual_norm_tensor(pe, 6)

            piece(pe, "x2_wk")
            narrow_keys_tensor(pe, "x2")
            wait_x(pe, 7)
            narrow_tensor(pe, "x2", xT, ctxT, False, None, W("x2_wo"))
            residual_norm_tensor(pe, 7)

            norm_mean(pe, "rms1")
            pe.wait_ge(S("f2_h"), 2)
            piece(pe, "f2_wq")
            narrow_tensor(pe, "f2", f_h, f_h, True, caus, W("f2_wo"), "f2_attn")
            norm_mean(pe, "rms2")
            pe.wait_ge(S("f2_h"), 4)
            route_tensor(pe, "m2", m_x2)
            mix_tensor(pe, "m2", m_x2, M2_CH, M2_ROWS, 8)
            residual_norm_tensor(pe, 8)

            for p in range(2):
                wait_x(pe, 9, 1)
                mm(ps[0:64, 2 + p, :], W("l3_wg"), half(xT, p), start=True, stop=True).then_inc(S("l3_gmm"), 1)
                mm(ps[0:64, 4 + p, :], W("l3_wb"), half(xT, p), start=True, stop=True).then_inc(S("l3_bmm"), 1)
            for p in range(2):
                pe.wait_ge(S("l3_state"), 4 * p + 4)
                mm(bank(6 + p), W("l3_wc")[0:64, :], half(s_st, p)[0:64, :], start=True, stop=True).then_inc(S("l3_ymm"), 1)

            def inner_ready(p):
                pe.wait_ge(S("l3_h"), p + 1)
            norm_tensor(pe, "inner", s_h, inner_ready)
            for p in range(2):
                pe.wait_ge(S("l3_hn"), p + 1)
                mm(bank(p), W("l3_wout"), half(s_hn, p), start=True, stop=True).then_inc(S("y_ready"), 1)
            residual_norm_tensor(pe, 9)

            pe.wait_ge(S("ctxtm_loaded"), 16)
            for p in range(2):
                wait_x(pe, 10, 1)
                for b in range(HB * p, HB * (p + 1)):
                    ins = mm(ps[:, 6 + p, (b % HB) * P:(b % HB + 1) * P], ctxT[:, b * P:(b + 1) * P], xT[:, b * P:(b + 1) * P],
                             start=True, stop=True, skip_group_check=True)
                ins.then_inc(S("e_up"), 1)
            for p in range(2):
                pe.wait_ge(S("e_act"), p + 1)
                for b in range(HB * p, HB * (p + 1)):
                    ins = mm(ps[:, p, (b % HB) * P:(b % HB + 1) * P], ctx_tm[:, b * P:(b + 1) * P], e_a[:, b * P:(b + 1) * P],
                             start=True, stop=True, skip_group_check=True)
                ins.then_inc(S("y_ready"), 1)
            residual_norm_tensor(pe, 10)

            wait_x(pe, 11)
            for b in range(B):
                ins = mm(ps[:, 2 + b // 3, (b % 3) * NE:(b % 3 + 1) * NE], xT[:, b * P:(b + 1) * P], W("m3_router"),
                         start=True, stop=True, skip_group_check=True)
            ins.then_inc(R("m3", "_logits"), 1)
            for p in range(2):
                mm(ps[0:64, 6 + p, :], W("m3_sgate"), half(xT, p), start=True, stop=True).then_inc(S("m3_shared"), 1)
            for p in range(2):
                pe.wait_ge(S("m3_sact"), p + 1)
                mm(bank(p), W("m3_sdown")[0:64, :], half(t_sh, p)[0:64, :], start=True, stop=False, skip_group_check=True)
            waits(pe, "m3")("_parts", 3)
            for s in range(SETS):
                for b in range(B):
                    ins = nc.tensor.transpose(bankb(2 + s)[:, b * P:(b + 1) * P], t_parts[:, b, s, :], identb[:, :])
                ins.then_inc(R("m3", "_wturned"), 1)
            waits(pe, "m3")("_wT", SETS)

            def up(i, j, p, n):
                if j % 4 == 0 and p == 0:
                    waits(pe, "m3")(f"_load{j // 4}", 16 * i + 16)
                if not isinstance(n, int) or n >= 2:
                    waits(pe, "m3")("_hid", n - 1)
                at = (j % 4) * 2 * P
                mm(bank(2 + p), ring[:, j // 4, at:at + P], half(xT, p), start=True, stop=True).then_inc(R("m3", "_gate"), 1)
                mm(bank(4 + p), sel160[:, bass.ds((10 * (j % 2) + i) * P, P)], half(t_combT[:, j // 2, :], p),
                   start=True, stop=True).then_inc(R("m3", "_spread"), 1)

            def down(j, p, n, final):
                waits(pe, "m3")("_hid", n + 1)
                at = (j % 4) * 2 * P + P
                mm(bank(p), ring[:, j // 4, at:at + P], t_hid[:, p], start=False, stop=final,
                   skip_group_check=True).then_inc(S("y_ready") if final else R("m3", "_down"), 1)

            def body(i, final):
                for u in range(2 * CHUNKS):
                    n = 2 * CHUNKS * i + u
                    if u < 2 * CHUNKS - 1:
                        up(i, (u + 1) // 2, (u + 1) % 2, n + 1)
                    elif not final:
                        up(i + 1, 0, 0, n + 1)
                    down(u // 2, u % 2, n, final and u >= 2 * CHUNKS - 2)

            up(0, 0, 0, 0)
            with pe.Fori(0, GROUPS - 1) as i:
                body(i, False)
            body(GROUPS - 1, True)
            residual_norm_tensor(pe, 11)

        @block.scalar
        def _(act):
            A_ = nc.scalar.activation
            log_tables()
            act.wait_ge(S("filled"), 2)
            norm_scalar(act, "ctx")
            piece(act, "l0_td")
            A_(d_e, W("l0_td"), ACT.Exp).then_inc(S("l0_e"), 1)
            for p in range(2):
                act.wait_ge(S("l0_r"), p + 1)
                A_(bank(4 + p), bank(4 + p), ACT.Sigmoid).then_inc(S("l0_sig"), 1)
            act.wait_ge(S("x0_mw"), 1)
            A_(x_m.rearrange("p h d -> p (h d)"), ps[:, 6:8, :].rearrange("p a c -> p (a c)"), ACT.Copy,
               scale=P ** -0.5).then_inc(S("x0_m"), 1)
            act.wait_ge(S("x0_bw"), 1)
            A_(x_c, ps[:, 6, 0:XH], ACT.Copy, scale=P ** -0.5).then_inc(S("x0_cvec"), 1)
            norm_scalar(act, "0", root=True)

            norm_scalar(act, "lat")
            act.wait_ge(S("x0_cvec"), 1)
            for h in range(XH):
                for p in range(2):
                    act.wait_ge(S("x0_qmm"), 2 * h + p + 1)
                    A_(half(x_q[:, h, :], p), bank(4 + (2 * h + p) % 4), ACT.Identity, bias=x_c[:, h:h + 1]).then_inc(S("x0_q"), 1)

            def x_exps(v, w):
                act.wait_ge(S("x0_nm"), w + 1)
                if not isinstance(w, int) or w >= 2:
                    act.wait_ge(S("x0_turned"), w)
                for i in range(4):
                    A_(x_p[:, v, i, :], ps[:, 2 * v + i // 2, (i % 2) * 256:(i % 2 + 1) * 256], ACT.Exp,
                       bias=x_nm[:, v, i:i + 1], accum_out=x_sum[:, v, i:i + 1]).then_inc(S("x0_p"), 1)

            def x_copies(b, v, w):
                act.wait_ge(S("x0_turned"), w + 2)
                A_(x_pt[:, v, 0, :], bank(4), ACT.Copy).then_inc(S("x0_ptA"), 1)
                act.wait_ge(S("x0_weighed"), w + 1)
                A_(x_q[:, 4 * v:4 * v + 4, bass.ds(b * P, P)], bank(6 + v).rearrange("p (h t) -> p h t", h=4),
                   ACT.Copy).then_inc(S("x0_o"), 1)

            def x_body(i, final):
                for k in range(4):
                    w = 4 * i + k
                    if not (final and k == 3):
                        x_exps((k + 1) % 2, w + 1)
                    x_copies(2 * i + k // 2, k % 2, w)

            credited(act, "x0_p", "x0_ptA", "x0_o")
            x_exps(0, 0)
            with act.Fori(0, B // 2 - 1) as i:
                x_body(i, False)
            x_body(B // 2 - 1, True)
            norm_scalar(act, "1")

            route_scalar(act, "m0")
            mix_scalar(act, "m0", M0_CH, M0_ROWS)
            norm_scalar(act, "2")

            act.wait_ge(S("l1_norm"), 1)
            A_(g_n2, g_n, ACT.Ln).then_inc(S("l1_log"), 1)
            act.wait_ge(S("l1_log"), 1)
            A_(g_n, g_n2, ACT.Exp, scale=-0.5).then_inc(S("l1_root"), 1)
            for p in range(2):
                act.wait_ge(S("l1_qmm"), p + 1)
                A_(half(g_q, p), bank(p), ACT.Copy).then_inc(S("l1_q"), 1)
                act.wait_ge(S("l1_vmm"), p + 1)
                A_(g_v[:, HB * p:HB * (p + 1), :], bank(4 + p).rearrange("p (b d) -> p b d", b=HB), ACT.Copy).then_inc(S("l1_v"), 1)
            for p in range(2):
                act.wait_ge(S("l1_z"), p + 1)
                A_(g_z[:, HB * p:HB * (p + 1), :], g_z[:, HB * p:HB * (p + 1), :], ACT.Exp).then_inc(S("l1_e"), 1)
            for p in range(2):
                act.wait_ge(S("l1_turned"), p + 1)
                A_(g_pt[:, HB * p:HB * (p + 1), :], bank(p).rearrange("p (b d) -> p b d", b=HB), ACT.Copy).then_inc(S("l1_pt"), 1)
            for p in range(2):
                act.wait_ge(S("l1_in"), p + 1)
                A_(g_in[:, HB * p:HB * (p + 1)], g_in[:, HB * p:HB * (p + 1)], ACT.Ln).then_inc(S("l1_log"), 1)
                act.wait_ge(S("l1_log"), p + 2)
                A_(g_in[:, HB * p:HB * (p + 1)], g_in[:, HB * p:HB * (p + 1)], ACT.Exp, scale=-0.5).then_inc(S("l1_root"), 1)
            norm_scalar(act, "3")

            piece(act, "x1_bq")
            narrow_scalar(act, "x1", False, W("x1_bv"), SCALE8, range(10, NH), W("x1_bq"))
            norm_scalar(act, "4")

            act.wait_ge(S("f1_wturned"), 1)
            A_(q_wT.rearrange("p a k -> p (a k)"), ps[:, 5:8, :].rearrange("p a c -> p (a c)")[:, 0:9 * P], ACT.Copy).then_inc(S("f1_wT"), 1)
            for k, dst in enumerate((q_up, q_gate)):
                for n in range(6):
                    act.wait_ge(S("f1_mm"), 6 * k + n + 1)
                    A_(dst[:, n * HALF:(n + 1) * HALF], bank(2 + n), ACT.Copy).then_inc(S("f1_gate" if k else "f1_up"), 1)
            act.wait_ge(S("f1_gq"), 1)
            A_(q_sig, q_gate, ACT.Sigmoid).then_inc(S("f1_sig"), 1)
            log_tables()
            norm_scalar(act, "5")

            piece(act, "l2_td")
            A_(r_e, W("l2_td"), ACT.Exp).then_inc(S("l2_decay"), 1)
            A_(r_u, W("l2_tf"), ACT.Exp).then_inc(S("l2_decay"), 1)
            act.wait_ge(S("l2_decay"), 2)
            A_(r_dec, r_e, ACT.Exp, scale=-1.0).then_inc(S("l2_decay"), 1)
            for p in range(2):
                act.wait_ge(S("l2_wk_mm"), p + 1)
                A_(half(r_ek, p), bank(p), ACT.Exp).then_inc(S("l2_ek"), 1)
            for p in range(2):
                act.wait_ge(S("l2_wr_mm"), p + 1)
                A_(half(r_sig, p), bank(4 + p), ACT.Sigmoid).then_inc(S("l2_sig"), 1)
            log_tables()
            norm_scalar(act, "6")

            piece(act, "x2_bq")
            narrow_scalar(act, "x2", False, W("x2_bv"), SCALE8, range(10, NH), W("x2_bq"))
            norm_scalar(act, "7")

            wait_x(act, 8)
            norm_scalar(act, "rms1", eps6, xT)
            narrow_scalar(act, "f2", True, None, SCALE8, range(8, NH))
            act.wait_ge(S("f2_x2"), 2)
            norm_scalar(act, "rms2", eps6, f_x2)
            route_scalar(act, "m2")
            mix_scalar(act, "m2", M2_CH, M2_ROWS)
            norm_scalar(act, "8")

            A_(s_a, W("l3_alog"), ACT.Exp).then_inc(S("l3_a"), 1)
            for p in range(2):
                act.wait_ge(S("l3_gmm"), p + 1)
                A_(half(s_sig, p)[0:64, :], ps[0:64, 2 + p, :], ACT.Sigmoid, bias=W("l3_bg")[0:64, :]).then_inc(S("l3_sig"), 1)
            log_tables()
            norm_scalar(act, "inner")
            norm_scalar(act, "9")

            for p in range(2):
                act.wait_ge(S("e_up"), p + 1)
                A_(half(e_a, p), bank(6 + p), ACT.Gelu_apprx_tanh).then_inc(S("e_act"), 1)
            log_tables()
            norm_scalar(act, "10")

            act.wait_ge(S("m3_biased"), 3)
            A_(t_p[:, :, :], t_p[:, :, :], ACT.Sigmoid).then_inc(S("m3_prob"), 1)
            for p in range(2):
                act.wait_ge(S("m3_shared"), p + 1)
                A_(half(t_sh, p)[0:64, :], ps[0:64, 6 + p, :], ACT.Silu).then_inc(S("m3_sact"), 1)
            with act.Fori(0, GROUPS * CHUNKS) as i:
                for p in range(2):
                    waits(act, "m3")("_gate", 2 * i + p + 1)
                    A_(t_sg[:, p], bank(2 + p), ACT.Silu).then_inc(R("m3", "_silu"), 1)
            log_tables()
            norm_scalar(act, "11")

        @block.vector
        def _(dve):
            V = nc.vector
            link = linked(dve, "dve_step")

            def affine_norm(tag, s, g, b):
                for p in range(2):
                    dst = x_kv[:, HB * p:HB * (p + 1), s, :]
                    dve.wait_ge(S("norm_rstd"), nth(tag, p))
                    link(V.tensor_tensor(dst, bank(2 + p).rearrange("p (b t) -> p b t", b=HB),
                                         half(rstd, p).rearrange("p (b t) -> p b t", b=HB), ALU.mult))
                    V.tensor_scalar(dst, dst, W(g), W(b), ALU.mult, ALU.add).then_inc(S("norm_out"), 1)

            piece(dve, "x0_gm")
            affine_norm("ctx", 0, "x0_gm", "x0_bm")
            dve.wait_ge(S("l0_e"), 1)
            link(V.tensor_scalar(d_w, d_e, -1.0, None, ALU.mult))
            for p in range(2):
                dve.wait_ge(S("l0_k"), p + 1)
                for b in range(HB * p, HB * (p + 1)):
                    ins = V.tensor_tensor_scan(d_s[:, b * P:(b + 1) * P], d_w.to_broadcast([P, P]),
                                               ps[:, 2 + p, (b % HB) * P:(b % HB + 1) * P], 0.0, ALU.mult, ALU.add)
                    link(ins)
                dve.wait_ge(S("l0_sig"), p + 1)
                V.tensor_tensor(half(d_s, p), half(d_s, p), bank(4 + p), ALU.mult).then_inc(S("l0_gated"), 1)
            dve.wait_ge(S("x0_uw"), 1)
            V.tensor_copy(x_u.rearrange("p h d -> p (h d)"), ps[:, 6:8, :].rearrange("p a c -> p (a c)")).then_inc(S("x0_u"), 1)
            dve.wait_ge(S("x0_bw"), 1)
            V.tensor_tensor(x_bo, ps[:, 7, 0:1], W("x0_bo"), ALU.add).then_inc(S("x0_bvec"), 1)
            residual_norm_vector(dve, 0)

            affine_norm("lat", 1, "x0_gl", "x0_bl")
            for n in range(4):
                dve.wait_ge(S("x0_kvt"), 2 * n + 2)
                V.tensor_copy(x_kvt[:, 2 * n:2 * n + 2].rearrange("p b s d -> p (b s d)"), bank(n)).then_inc(S("x0_kvt_sb"), 1)

            def x_maxima(v, w):
                dve.wait_ge(S("x0_scores"), w + 1)
                V.tensor_reduce(x_nm[:, v], ps[:, 2 * v:2 * v + 2, :].rearrange("p a (h k) -> p (a h) k", h=2), AX.X, ALU.max,
                                negate=True).then_inc(S("x0_nm"), 1)

            def x_copies(v, w):
                dve.wait_ge(S("x0_turned"), w + 2)
                V.tensor_copy(x_pt[:, v, 1, :], bank(5)).then_inc(S("x0_ptB"), 1)

            def x_normalise(v, w):
                dve.wait_ge(S("x0_p"), 4 * (w + 1) + 1)
                V.reciprocal(x_rec[:, v], x_sum[:, v]).then_inc(S("x0_rec"), 1)
                dve.wait_ge(S("x0_rec"), w + 1)
                for i in range(4):
                    V.tensor_scalar(x_p[:, v, i, :], x_p[:, v, i, :], x_rec[:, v, i:i + 1], None, ALU.mult).then_inc(S("x0_pn"), 1)

            def x_body(i, final):
                for k in range(4):
                    w = 4 * i + k
                    if not (final and k == 3):
                        x_maxima((k + 1) % 2, w + 1)
                    x_copies(k % 2, w)
                    if not (final and k == 3):
                        x_normalise((k + 1) % 2, w + 1)

            credited(dve, "x0_ptB")
            x_maxima(0, 0)
            x_normalise(0, 0)
            with dve.Fori(0, B // 2 - 1) as i:
                x_body(i, False)
            x_body(B // 2 - 1, True)
            residual_norm_vector(dve, 1, x_bo)

            route_vector(dve, "m0", 1e-6, link)
            mix_vector(dve, "m0", xT, M0_CH, M0_ROWS)
            residual_norm_vector(dve, 2)

            wait_x(dve, 3)
            link(V.tensor_tensor(g_n, W("l1_rc"), W("l1_rc"), ALU.mult))
            link(V.tensor_tensor(g_n2, W("l1_rs"), W("l1_rs"), ALU.mult))
            V.tensor_tensor(g_n, g_n, g_n2, ALU.add).then_inc(S("l1_norm"), 1)
            link(V.reciprocal(g_a, W("l1_scale")))
            link(V.tensor_scalar(g_a, g_a, 2.0, None, ALU.mult))
            link(V.tensor_tensor(g_b, g_a, W("l1_bias"), ALU.add))
            dve.wait_ge(S("l1_root"), 1)
            link(V.tensor_tensor(g_c, W("l1_rc"), g_n, ALU.mult))
            link(V.tensor_tensor(g_s, W("l1_rs"), g_n, ALU.mult))
            for k in range(3):
                link(V.tensor_scalar(g_t[:, k], W("swap"), g_s[:, k:k + 1], None, ALU.mult))
                ins = V.scalar_tensor_tensor(out=g_rot[:, k], in0=ident, scalar=g_c[:, k:k + 1], in1=g_t[:, k], op0=ALU.mult, op1=ALU.add)
            ins.then_inc(S("l1_rot"), 1)
            for p in range(2):
                dve.wait_ge(S("l1_kmm"), p + 1)
                V.tensor_copy(half(g_k, p), bank(2 + p)).then_inc(S("l1_k"), 1)
            for p in range(2):
                z = g_z[:, HB * p:HB * (p + 1), :]
                mx = g_mx[:, HB * p:HB * (p + 1)]
                dve.wait_ge(S("l1_scores"), p + 1)
                link(V.tensor_scalar(z, bank(6 + p).rearrange("p (b k) -> p b k", b=HB), g_a, g_b, ALU.mult, ALU.add))
                link(V.tensor_reduce(mx, z, AX.X, ALU.max))
                V.tensor_tensor(z, z, mx.unsqueeze(2).to_broadcast([P, HB, P]), ALU.subtract).then_inc(S("l1_z"), 1)
            for p in range(2):
                dve.wait_ge(S("l1_e"), p + 1)
                link(V.tensor_reduce(g_sm[:, HB * p:HB * (p + 1)], g_z[:, HB * p:HB * (p + 1), :], AX.X, ALU.add))
                link(V.reciprocal(g_rc[:, HB * p:HB * (p + 1)], g_sm[:, HB * p:HB * (p + 1)]))
            for p in range(2):
                av = g_av[:, HB * p:HB * (p + 1), :]
                s2 = g_sq[:, HB * p:HB * (p + 1), :]
                dve.wait_ge(S("l1_weighed"), p + 1)
                link(V.tensor_tensor(av, bank(2 + p).rearrange("p (b d) -> p b d", b=HB),
                                     g_rc[:, HB * p:HB * (p + 1)].unsqueeze(2).to_broadcast([P, HB, P]), ALU.mult))
                link(V.tensor_tensor(s2, av, av, ALU.mult))
                link(V.tensor_reduce(g_in[:, HB * p:HB * (p + 1)], s2, AX.X, ALU.add))
                V.tensor_scalar(g_in[:, HB * p:HB * (p + 1)], g_in[:, HB * p:HB * (p + 1)], 1e-8, None, ALU.max).then_inc(S("l1_in"), 1)
            for p in range(2):
                av = g_av[:, HB * p:HB * (p + 1), :]
                dve.wait_ge(S("l1_root"), p + 2)
                V.tensor_tensor(av, av, g_in[:, HB * p:HB * (p + 1)].unsqueeze(2).to_broadcast([P, HB, P]), ALU.mult).then_inc(S("l1_out"), 1)
            dve.wait_ge(S("mask_loaded"), 16)
            V.tensor_scalar(maskb[:, :], mask8[:, :], NEG, None, ALU.mult).then_inc(S("maskb"), 1)
            piece(dve, "x1_bk")
            residual_norm_vector(dve, 3, meanwhile=lambda: narrow_keys_vector(dve, "x1", range(0, 10), W("x1_bk")))

            narrow_vector(dve, "x1")
            residual_norm_vector(dve, 4, W("x1_bo"))

            wait_x(dve, 5)
            at = PACK_AT["f1_gate"][0]
            wts = pack[:, at:at + 9 * P].rearrange("p (a k) -> p a k", k=32)
            link(V.tensor_reduce(q_ab, wts, AX.X, ALU.max, apply_absolute_value=True))
            link(V.tensor_scalar(q_sc, q_ab, 1.0 / 7.0, 1e-12, ALU.mult, ALU.max))
            link(V.reciprocal(q_inv, q_sc))
            link(V.tensor_tensor(q_w, wts, q_inv.unsqueeze(2).to_broadcast([P, 36, 32]), ALU.mult))
            link(V.tensor_scalar(q_w, q_w, ROUND, ROUND, ALU.add, ALU.subtract))
            V.tensor_tensor(q_w, q_w, q_sc.unsqueeze(2).to_broadcast([P, 36, 32]), ALU.mult).then_inc(S("f1_wq"), 1)

            def largest(n, src):
                V.tensor_reduce(q_col[:, n:n + 1], src, AX.X, ALU.max, apply_absolute_value=True).then_inc(S("f1_col"), 1)
                dve.wait_ge(S("f1_colT"), n + 1)
                V.tensor_reduce(q_top[:, n:n + 1], ps[0:1, 0, 0:P], AX.X, ALU.max).then_inc(S("f1_top"), 1)
                dve.wait_ge(S("f1_topB"), n + 1)
                link(V.tensor_scalar(q_s[:, n:n + 1], ps[:, 1, 0:1], 1.0 / QMAX, 1e-12, ALU.mult, ALU.max))
                link(V.reciprocal(q_i[:, n:n + 1], q_s[:, n:n + 1]))

            def quantise(n, dst, src):
                link(V.tensor_scalar(dst, src, q_i[:, n:n + 1], ROUND, ALU.mult, ALU.add))
                return V.tensor_scalar(dst, dst, ROUND, q_s[:, n:n + 1], ALU.subtract, ALU.mult)

            largest(0, xT[:, :])
            quantise(0, q_x, xT[:, :]).then_inc(S("f1_xq"), 1)
            dve.wait_ge(S("f1_up"), 6)
            largest(1, q_up)
            link(quantise(1, q_up, q_up))
            dve.wait_ge(S("f1_gate"), 6)
            largest(2, q_gate)
            quantise(2, q_gate, q_gate).then_inc(S("f1_gq"), 1)
            dve.wait_ge(S("f1_sig"), 1)
            link(V.tensor_scalar(q_sig, q_sig, 65536.0, ROUND, ALU.mult, ALU.add))
            link(V.tensor_scalar(q_sig, q_sig, ROUND, 65535.0, ALU.subtract, ALU.min))
            link(V.scalar_tensor_tensor(out=q_gate, in0=q_sig, scalar=1.0 / 65536.0, in1=q_gate, op0=ALU.mult, op1=ALU.mult))
            largest(3, q_gate)
            link(quantise(3, q_gate, q_gate))
            link(V.tensor_tensor(q_up, q_gate, q_up, ALU.mult))
            largest(4, q_up)
            quantise(4, q_up, q_up).then_inc(S("f1_o"), 1)
            residual_norm_vector(dve, 5)

            piece(dve, "l2_mk")
            for p in range(2):
                dve.wait_ge(S("l2_prev"), p + 1)
                prev = r_prev[:, HB * p:HB * (p + 1), :].rearrange("p b t -> p (b t)")
                link(V.tensor_tensor(half(r_diff, p), half(xT, p), prev, ALU.subtract))
                for name, dst in (("l2_mk", r_k), ("l2_mv", r_v), ("l2_mr", r_r)):
                    V.scalar_tensor_tensor(out=half(dst, p), in0=half(r_diff, p), scalar=W(name), in1=prev,
                                           op0=ALU.mult, op1=ALU.add).then_inc(S("l2_mix"), 1)
            dve.wait_ge(S("l2_decay"), 3)
            dve.wait_ge(S("l2_zero"), 3)
            for p in range(2):
                seqs = range(HB * p, HB * (p + 1))
                dve.wait_ge(S("l2_ek"), p + 1)
                dve.wait_ge(S("l2_wv_mm"), p + 1)
                link(V.tensor_tensor(half(r_ekv, p), half(r_ek, p), bank(2 + p), ALU.mult))
                dve.wait_ge(S("l2_bsum"), p + 1)
                for b in seqs:
                    ins = V.tensor_tensor_scan(r_sa[:, b, 1:P + 1], r_dec.to_broadcast([P, P]), r_ekv[:, b * P:(b + 1) * P],
                                               0.0, ALU.mult, ALU.add)
                    ins = V.tensor_tensor_scan(r_sb[:, b, 1:P + 1], r_dec.to_broadcast([P, P]),
                                               ps[:, 6 + p, (b % HB) * P:(b % HB + 1) * P], 0.0, ALU.mult, ALU.add)
                link(ins)
                ha = r_sa[:, HB * p:HB * (p + 1), 0:P]
                hb = r_sb[:, HB * p:HB * (p + 1), 0:P]
                den = half(r_den, p).rearrange("p (b t) -> p b t", b=HB)
                num = half(r_ekv, p).rearrange("p (b t) -> p b t", b=HB)
                link(V.scalar_tensor_tensor(out=num, in0=num, scalar=r_u, in1=ha, op0=ALU.mult, op1=ALU.add))
                link(V.scalar_tensor_tensor(out=den, in0=bank(6 + p).rearrange("p (b t) -> p b t", b=HB), scalar=r_u, in1=hb,
                                            op0=ALU.mult, op1=ALU.add))
                link(V.tensor_scalar(half(r_den, p), half(r_den, p), 1e-6, None, ALU.max))
                link(V.reciprocal(half(r_den, p), half(r_den, p)))
                link(V.tensor_tensor(half(r_den, p), half(r_den, p), half(r_ekv, p), ALU.mult))
                dve.wait_ge(S("l2_sig"), p + 1)
                V.tensor_tensor(half(r_k, p), half(r_den, p), half(r_sig, p), ALU.mult).then_inc(S("l2_out"), 1)
            piece(dve, "x2_bk")
            residual_norm_vector(dve, 6, meanwhile=lambda: narrow_keys_vector(dve, "x2", range(0, 10), W("x2_bk")))

            narrow_vector(dve, "x2")
            residual_norm_vector(dve, 7, W("x2_bo"))

            piece(dve, "f2_ln1")
            for p in range(2):
                dve.wait_ge(S("norm_rstd"), nth("rms1", p))
                V.scalar_tensor_tensor(out=half(f_h, p), in0=half(xT, p), scalar=W("f2_ln1"), in1=half(rstd, p),
                                       op0=ALU.mult, op1=ALU.mult).then_inc(S("f2_h"), 1)
            narrow_rope_vector(dve, "f2")
            narrow_spread_vector(dve, "f2", range(0, 8))
            narrow_vector(dve, "f2")
            for p in range(2):
                dve.wait_ge(S("f2_attn"), p + 1)
                V.tensor_tensor(half(f_x2, p), bank(p), half(xT, p), ALU.add).then_inc(S("f2_x2"), 1)
            dve.wait_ge(S("f2_x2"), 2)
            link(V.tensor_tensor(f_res, f_x2, xT[:, :], ALU.add))
            for p in range(2):
                dve.wait_ge(S("norm_rstd"), nth("rms2", p))
                V.scalar_tensor_tensor(out=half(m_x2, p), in0=half(f_x2, p), scalar=W("f2_ln2"), in1=half(rstd, p),
                                       op0=ALU.mult, op1=ALU.mult).then_inc(S("f2_h"), 1)
            route_vector(dve, "m2", 0.0, link)
            mix_vector(dve, "m2", m_x2, M2_CH, M2_ROWS)
            residual_norm_vector(dve, 8, None, f_res)

            dve.wait_ge(S("l3_a"), 1)
            for p in range(2):
                dve.wait_ge(S("l3_sig"), p + 1)
                dve.wait_ge(S("l3_bmm"), p + 1)
                link(V.tensor_tensor(half(s_u, p)[0:64, :], half(s_sig, p)[0:64, :], ps[0:64, 4 + p, :], ALU.mult))
                for b in range(HB * p, HB * (p + 1)):
                    V.tensor_tensor_scan(s_st[0:64, b * P:(b + 1) * P], s_a[0:64, :].to_broadcast([64, P]),
                                         s_u[0:64, b * P:(b + 1) * P], 0.0, ALU.mult, ALU.add).then_inc(S("l3_state"), 1)
            for p in range(2):
                dve.wait_ge(S("l3_ymm"), p + 1)
                link(V.scalar_tensor_tensor(out=half(s_h, p), in0=half(xT, p), scalar=W("l3_d"), in1=bank(6 + p),
                                            op0=ALU.mult, op1=ALU.add))
                V.tensor_tensor(half(s_h, p), half(s_h, p), half(xT, p), ALU.add).then_inc(S("l3_h"), 1)
            for p in range(2):
                dve.wait_ge(S("norm_rstd"), nth("inner", p))
                link(V.tensor_tensor(half(s_hn, p), bank(2 + p), half(rstd, p), ALU.mult))
                V.tensor_scalar(half(s_hn, p), half(s_hn, p), W("l3_gamma"), W("l3_beta"), ALU.mult, ALU.add).then_inc(S("l3_hn"), 1)
            residual_norm_vector(dve, 9, W("l3_bout"))

            residual_norm_vector(dve, 10)

            waits(dve, "m3")("_logits", 1)
            for k in range(3):
                b0, b1 = 3 * k, min(3 * k + 3, B)
                V.tensor_tensor(t_p[:, b0:b1, :], ps[:, 2 + k, 0:(b1 - b0) * NE].rearrange("p (b e) -> p b e", e=NE),
                                W("m3_bias").unsqueeze(1).to_broadcast([P, b1 - b0, NE]), ALU.add).then_inc(S("m3_biased"), 1)
            dve.wait_ge(S("m3_prob"), 1)
            for b in range(B):
                ins = V.max(t_top[:, b, :], t_p[:, b, :])
            link(ins)
            for b in range(B):
                ins = V.match_replace(t_rep[:, b, :], t_top[:, b, :], t_p[:, b, :], 0.0)
            link(ins)
            link(V.tensor_tensor(t_w, t_p, t_rep, ALU.subtract))
            link(V.tensor_reduce(t_s, t_top, AX.X, ALU.add))
            link(V.tensor_scalar(t_s, t_s, 1e-9, None, ALU.add))
            link(V.reciprocal(t_s, t_s))
            link(V.tensor_scalar(t_s, t_s, 2.5, None, ALU.mult))
            link(V.tensor_tensor(t_w, t_w, t_s.unsqueeze(2).to_broadcast([P, B, NE]), ALU.mult))
            waits(dve, "m3")("_pad", 1)
            w4 = t_w.rearrange("p b (s e) -> p b s e", s=SETS)
            for k in range(3):
                part = t_parts[:, :, :, k:3 * SETE:3]
                V.tensor_copy(part, w4).then_inc(R("m3", "_parts"), 1)
                if k < 2:
                    waits(dve, "m3")("_parts", k + 1)
                    link(V.tensor_tensor(w4, w4, part, ALU.subtract))
            for s in range(SETS):
                waits(dve, "m3")("_wturned", s + 1)
                V.tensor_copy(t_combT[:, s, :], bankb(2 + s)).then_inc(R("m3", "_wT"), 1)
            with dve.Fori(0, GROUPS * CHUNKS) as i:
                for p in range(2):
                    waits(dve, "m3")("_silu", 2 * i + p + 1)
                    waits(dve, "m3")("_spread", 2 * i + p + 1)
                    V.tensor_tensor(t_hid[:, p], t_sg[:, p], bank(4 + p), ALU.mult).then_inc(R("m3", "_hid"), 1)
            residual_norm_vector(dve, 11)

        @block.gpsimd
        def _(pool):
            G = nc.gpsimd
            G.memset(eps5, EPS).then_inc(S("filled"), 1)
            G.memset(eps6, 1e-6).then_inc(S("filled"), 1)
            G.memset(ones1[:, :], 1.0).then_inc(S("filled"), 1)
            G.memset(zeros[:, :], 0.0).then_inc(S("filled"), 1)
            def x_slices(b, slot):
                G.tensor_copy(x_qs[:, slot], x_q[:, :, bass.ds(b * P, P)]).then_inc(S("x0_slices"), 1)
                G.tensor_copy(x_kvs[:, slot], x_kv[:, bass.ds(b, 1), :, :].rearrange("p o s d -> p (o s) d")).then_inc(S("x0_slices"), 1)
                G.tensor_copy(x_kvts[:, slot], x_kvt[:, bass.ds(b, 1), :, :].rearrange("p o s d -> p (o s) d")).then_inc(S("x0_slices"), 1)
            pool.wait_ge(S("norm_out"), 4)
            pool.wait_ge(S("x0_kvt_sb"), 4)
            pool.wait_ge(S("x0_q"), 2 * XH)
            x_slices(0, 0)
            x_slices(1, 1)
            with pool.Fori(1, B // 2) as i:
                for slot in range(2):
                    pool.wait_ge(S("x0_weighed"), 4 * i + 2 * slot - 2)
                    x_slices(2 * i + slot, slot)

            def padding(t, ready):
                ready()
                G.memset(m_parts[:, :, :], 0.0).then_inc(R(t, "_pad"), 1)

            padding("m0", lambda: wait_x(pool, 2))
            narrow_gpsimd(pool, "x1", False, lambda: wait_x(pool, 4))
            wait_x(pool, 6)
            G.memset(r_sa[:, :, 0], 0.0).then_inc(S("l2_zero"), 1)
            G.memset(r_sb[:, :, 0], 0.0).then_inc(S("l2_zero"), 1)
            G.memset(r_prev[:, :, 0], 0.0).then_inc(S("l2_zero"), 1)
            pool.wait_ge(S("l2_zero"), 3)
            for p in range(2):
                G.tensor_copy(r_prev[:, HB * p:HB * (p + 1), 1:P],
                              half(xT, p).rearrange("p (b t) -> p b t", b=HB)[:, :, 0:P - 1]).then_inc(S("l2_prev"), 1)
            narrow_gpsimd(pool, "x2", False, lambda: wait_x(pool, 7))
            narrow_gpsimd(pool, "f2", True, lambda: wait_x(pool, 8))
            padding("m2", lambda: pool.wait_ge(S("f2_x2"), 2))
            wait_x(pool, 11)
            G.memset(t_parts[:, :, :, :], 0.0).then_inc(R("m3", "_pad"), 1)


def _pack(i):
    import numpy as np
    f = np.float32

    def rows(w):
        out = np.zeros((P, w.shape[1]), f)
        out[0:w.shape[0]] = w
        return out

    def col(v):
        return rows(v.reshape(-1, 1))

    def doubled(w):
        return np.repeat(w.reshape(P, 8, HD), 2, axis=1).reshape(P, P)

    def swapped(w):
        return w.reshape(P, NH, 2, HD // 2)[:, :, ::-1, :].reshape(P, P)

    by_head = lambda w: w.reshape(P, XH, P)
    turned = lambda w: by_head(w).transpose(2, 1, 0).reshape(P, XH * P)
    n = np.arange(P)
    swap = np.zeros((P, P), f)
    swap[n[0::2], n[1::2]] = 1
    swap[n[1::2], n[0::2]] = -1
    inv_freq = (1.0 / np.power(f(10000.0), np.arange(0, HD, 2, dtype=f) / f(HD), dtype=f)).astype(f)
    ang = np.arange(P, dtype=f)[:, None] * inv_freq[None, :]
    cos = np.tile(np.concatenate([np.cos(ang), np.cos(ang)], 1).T, (NH, 1))
    sin = np.tile(np.concatenate([-np.sin(ang), np.sin(ang)], 1).T, (NH, 1))
    before = (n[:E, None] > n[None, :E]).astype(f).reshape(1, E * E)
    kv = i["L0_xattn_Wkv"]
    rot = i["L1_attn_rot_w"].reshape(3, P // 2, 2)
    natural = lambda w: w.reshape(3, P, P).transpose(1, 0, 2).reshape(P, 3 * P)
    wk2, wv2 = doubled(i["L2_ffn_wk"]), doubled(i["L2_ffn_wv"])
    parts = {
        "center": np.eye(P, dtype=f) - f(1 / P), "mean": np.full((P, P), 1 / P, f), "ident": np.eye(P, dtype=f),
        "l0_wk": i["L0_attn_Wk"].T, "l0_wr": i["L0_attn_Wr"].T, "l0_wv": i["L0_attn_Wv"].T, "l0_td": col(i["L0_attn_time_decay"]),
        "x0_wq": turned(i["L0_xattn_Wq"]), "x0_wk": turned(kv[:, :XH * P]), "x0_wv": turned(kv[:, XH * P:]),
        "x0_wo": i["L0_xattn_Wo"].reshape(XH, P, P).transpose(1, 0, 2).reshape(P, XH * P),
        "x0_bq": i["L0_xattn_bq"].reshape(XH, P).T, "x0_bv": i["L0_xattn_bkv"][XH * P:].reshape(XH, P).T,
        "x0_bo": col(i["L0_xattn_bo"]), "x0_gm": col(i["L0_xattn_gamma_media"]), "x0_bm": col(i["L0_xattn_beta_media"]),
        "x0_gl": col(i["L0_xattn_gamma_lat"]), "x0_bl": col(i["L0_xattn_beta_lat"]),
        "m0_router": i["L0_ffn_router_w"].T, "before": np.broadcast_to(before, (P, E * E)),
        "l1_rc": np.repeat(rot[:, :, 0], 2, axis=1).T, "l1_rs": np.repeat(rot[:, :, 1], 2, axis=1).T,
        "l1_scale": np.broadcast_to(i["L1_attn_scale"].reshape(1, 1), (P, 1)),
        "l1_bias": np.broadcast_to(i["L1_attn_bias"].reshape(1, 1), (P, 1)), "swap": swap,
        "headmask": (n[:, None] // HD == n[None, 0:NH]).astype(f),
        "x1_wq": i["L1_xattn_Wq"], "x1_wk": i["L1_xattn_Wk"], "x1_wv": i["L1_xattn_Wv"], "x1_wo": i["L1_xattn_Wo"],
        "x1_bq": col(i["L1_xattn_bq"]), "x1_bk": col(i["L1_xattn_bk"]), "x1_bv": col(i["L1_xattn_bv"]), "x1_bo": col(i["L1_xattn_bo"]),
        "f1_gate": natural(i["L1_ffn_w_gate"]), "f1_up": natural(i["L1_ffn_w_up"]), "f1_down": i["L1_ffn_w_down"],
        "l2_mk": col(i["L2_attn_mix_k"]), "l2_mv": col(i["L2_attn_mix_v"]), "l2_mr": col(i["L2_attn_mix_r"]),
        "l2_td": col(np.repeat(i["L2_attn_time_decay"], HD)), "l2_tf": col(np.repeat(i["L2_attn_time_first"], HD)),
        "l2_wk": i["L2_attn_W_key"].T, "l2_wv": i["L2_attn_W_value"].T, "l2_wr": i["L2_attn_W_receptance"].T, "l2_wo": i["L2_attn_W_output"].T,
        "headsum": (n[:, None] // HD == n[None, :] // HD).astype(f),
        "x2_wq": i["L2_xattn_wq"].T, "x2_wk": i["L2_xattn_wk"].T, "x2_wv": i["L2_xattn_wv"].T, "x2_wo": i["L2_xattn_wo"].T,
        "x2_bq": col(i["L2_xattn_bq"]), "x2_bk": col(i["L2_xattn_bk"]), "x2_bv": col(i["L2_xattn_bv"]), "x2_bo": col(i["L2_xattn_bo"]),
        "f2_ln1": col(i["L2_ffn_ln1_w"]), "f2_ln2": col(i["L2_ffn_ln2_w"]),
        "f2_wq": i["L2_ffn_wq"], "f2_wqr": swapped(i["L2_ffn_wq"]),
        "f2_wk": wk2, "f2_wkr": swapped(wk2), "f2_wv": wv2, "f2_wo": i["L2_ffn_wo"],
        "m2_router": i["L2_ffn_router_w"], "cos": cos, "sin": sin,
        "l3_alog": col(i["L3_attn_A_log"]), "l3_bg": col(i["L3_attn_bg"]), "l3_d": col(i["L3_attn_D"]), "l3_bout": col(i["L3_attn_bout"]),
        "l3_gamma": col(i["L3_attn_gamma"]), "l3_beta": col(i["L3_attn_beta"]),
        "l3_wb": i["L3_attn_WB"].T, "l3_wg": i["L3_attn_Wg"].T, "l3_wc": rows(i["L3_attn_WC"].T), "l3_wout": i["L3_attn_Wout"].T,
        "m3_router": i["L3_ffn_router_w"].T, "m3_sgate": i["L3_ffn_w_gate_shared"].T, "m3_sdown": rows(i["L3_ffn_w_down_shared"].T),
        "m3_bias": np.broadcast_to(i["L3_ffn_expert_bias"].reshape(1, NE), (P, NE)),
    }
    return np.concatenate([np.asarray(parts[name], f).reshape(P, cols) for name, cols in PACK], axis=1)


def kernel(**inputs):
    import ml_dtypes
    import numpy as np
    import concourse.bacc as bacc
    from concourse.bass_utils import run_bass_kernel_spmd

    i = {k: np.asarray(v) for k, v in inputs.items()}
    bf = ml_dtypes.bfloat16
    feature_major = lambda a: np.ascontiguousarray(a.transpose(2, 0, 1).reshape(P, T))
    token_major = lambda a: np.ascontiguousarray(a.transpose(1, 0, 2).reshape(P, T))

    sel8 = np.zeros((P, E, P), np.float32)
    for e in range(E):
        sel8[3 * e:3 * e + 3, e, :] = 1
    sel160 = np.zeros((P, 20, 2, 64), np.float32)
    for q in range(20):
        for el in range(2):
            sel160[(2 * q + el) * 3:(2 * q + el) * 3 + 3, q, el, :] = 1
    pairs = np.array([[20 * (j // 2) + 10 * (j % 2) + g for j in range(CHUNKS)] for g in range(GROUPS)])
    gate = i["L3_ffn_w_gate"].reshape(NE // 2, P, P).transpose(0, 2, 1)
    down = i["L3_ffn_w_down"].transpose(0, 2, 1).reshape(NE // 2, P, P)
    m3 = np.stack([gate[pairs], down[pairs]], axis=2).reshape(2 * GROUPS, 4, 2, P, P)
    m3 = m3.transpose(0, 3, 1, 2, 4).reshape(2 * GROUPS, P, 1024)
    w13, w2 = i["L0_ffn_w13"], i["L0_ffn_w2"]
    chunked = lambda w, ch, rows: w.reshape(E, ch, rows, P).transpose(0, 2, 1, 3).reshape(E, rows, ch * P)
    arrays = {
        "xT_in": feature_major(i["x"]), "ctxT_in": feature_major(i["ctx_1024"]), "ctx_in": token_major(i["ctx_1024"]),
        "mask_in": i["mask_Bx1xSxS2_bk1"].reshape(B, P, P).transpose(1, 0, 2).reshape(P, T),
        "pack_in": _pack(i),
        "sel8_in": sel8.reshape(P, E * P).astype(bf), "sel160_in": sel160.reshape(P, 20 * P).astype(bf),
        "caus_in": np.where(np.tril(np.ones((P, P), bool)), 0.0, -1e30).astype(bf), "identb_in": np.eye(P).astype(bf),
        "m0_up_in": w13, "m0_down_in": chunked(w2, M0_CH, M0_ROWS),
        "m2_up_in": np.concatenate([i["L2_ffn_w_gate"], i["L2_ffn_w_up"]], axis=2), "m2_down_in": chunked(i["L2_ffn_w_down"], M2_CH, M2_ROWS),
        "m3_in": m3,
    }
    nc = bacc.Bacc("TRN2", target_bir_lowering=False, num_devices=1)
    args = []
    for name, a in arrays.items():
        arrays[name] = a = np.ascontiguousarray(a)
        args.append(nc.dram_tensor(name, a.shape, mybir.dt.from_np(a.dtype), kind="ExternalInput").ap())
    args.append(nc.dram_tensor("out", (P, T), F32, kind="ExternalOutput").ap())
    program(nc, *args)
    r = run_bass_kernel_spmd(nc, [arrays], core_ids=[0])
    return np.ascontiguousarray(r.results[0]["out"].reshape(P, B, P).transpose(1, 2, 0))
```

```python
from contextlib import ExitStack

import concourse.bass as bass
from concourse import mybir

F32 = mybir.dt.float32
F32R = mybir.dt.float32r
BF16 = mybir.dt.bfloat16
U8 = mybir.dt.uint8
ALU = mybir.AluOpType
ACT = mybir.ActivationFunctionType
AX = mybir.AxisListType

P = 128
B = 8
T = B * P
HALF = T // 2
HB = B // 2
NH, HD = 16, 8
VA = HD + 1
XH = 8
E = 8
NE, TOPK = 160, 8
GROUPS, CHUNKS = 10, 8
SETS = 4
SETE = NE // SETS
EPS = 1e-5
ROUND = 1.5 * 2.0 ** 23
QMAX = 32767.0
NEG = -1e15

PACK = [
    ("center", P), ("mean", P), ("ident", P),
    ("l0_wk", P), ("l0_wr", P), ("l0_wv", P), ("l0_td", 1),
    ("x0_wq", XH * P), ("x0_wk", XH * P), ("x0_wv", XH * P), ("x0_wo", XH * P),
    ("x0_bq", XH), ("x0_bv", XH), ("x0_bo", 1), ("x0_gm", 1), ("x0_bm", 1), ("x0_gl", 1), ("x0_bl", 1),
    ("m0_router", E),
    ("l1_rc", 3), ("l1_rs", 3), ("l1_scale", 1), ("l1_bias", 1), ("swap", P),
    ("headmask", NH), ("x1_wq", P), ("x1_wk", P), ("x1_wv", P), ("x1_wo", P),
    ("x1_bq", 1), ("x1_bk", 1), ("x1_bv", 1), ("x1_bo", 1),
    ("f1_gate", 3 * P), ("f1_up", 3 * P), ("f1_down", 3 * P),
    ("l2_mk", 1), ("l2_mv", 1), ("l2_mr", 1), ("l2_td", 1), ("l2_tf", 1),
    ("l2_wk", P), ("l2_wv", P), ("l2_wr", P), ("l2_wo", P), ("headsum", P),
    ("x2_wq", P), ("x2_wk", P), ("x2_wv", P), ("x2_wo", P),
    ("x2_bq", 1), ("x2_bk", 1), ("x2_bv", 1), ("x2_bo", 1),
    ("f2_ln1", 1), ("f2_ln2", 1), ("f2_wq", P), ("f2_wqr", P), ("f2_wk", P), ("f2_wkr", P),
    ("f2_wv", P), ("f2_wo", P), ("m2_router", E), ("cos", P), ("sin", P),
    ("l3_alog", 1), ("l3_bg", 1), ("l3_d", 1), ("l3_bout", 1), ("l3_gamma", 1), ("l3_beta", 1),
    ("l3_wb", 64), ("l3_wg", 64), ("l3_wc", P), ("l3_wout", P),
    ("m3_router", NE), ("m3_sgate", 64), ("m3_sdown", P), ("m3_bias", NE),
]
PACK_AT = {}
PACK_COLS = 0
for _name, _cols in PACK:
    PACK_AT[_name] = (PACK_COLS, _cols)
    PACK_COLS += _cols
PIECES = ["x0_wq", "m0_router", "headmask", "l2_mk", "f2_ln1", None]
PIECE_ENDS = [PACK_AT[n][0] if n else PACK_COLS for n in PIECES]

M0_CH, M0_ROWS = 2, 128
M2_CH, M2_ROWS = 4, 112
LAYERS = 12
RING = 1408
ARENA = 27792
PARTS = 9600
PARTS_COLS = 4 * RING + 6 * T + 4 * HALF


def program(nc, xT_in, ctxT_in, ctx_in, mask_in, pack_in, sel8_in, sel160_in, caus_in, identb_in,
            m0_up_in, m0_down_in, m2_up_in, m2_down_in, m3_in, out):
    ctx = ExitStack()
    with ctx:
        def sb(name, shape, dt=F32):
            return ctx.enter_context(nc.sbuf_tensor(name, shape, dt))

        sems = {}

        def S(name):
            if name not in sems:
                sems[name] = ctx.enter_context(nc.semaphore(name))
            return sems[name]

        ps = ctx.enter_context(nc.psum_tensor("ps", [P, 8, 512], F32))

        pack = sb("pack", [P, PACK_COLS])

        def W(name, lo=0, n=None):
            at, cols = PACK_AT[name]
            return pack[:, at + lo:at + (cols if n is None else lo + n)]

        xT = sb("xT", [P, T])
        ctxT = sb("ctxT", [P, T])
        ctx_tm = sb("ctx_tm", [P, T])
        mask8 = sb("mask8", [P, T], U8)
        maskb = sb("maskb", [P, T], BF16)
        caus = sb("caus", [P, P], BF16)
        identb = sb("identb", [P, P], BF16)
        sel8 = sb("sel8", [P, E * P], BF16)
        sel160 = sb("sel160", [P, 20 * P], BF16)
        hsum = sb("hsum", [P, T])
        sq = sb("sq", [P, T])
        rstd = sb("rstd", [P, T])
        small = sb("small", [P, 64])
        eps5 = small[:, 0:1]
        eps6 = small[:, 1:2]
        round_up, round_down = small[:, 2:3], small[:, 3:4]
        ring = sb("ring", [P, 2, RING])
        with ExitStack() as overlaid:
            overlaid.enter_context(nc.sbuf_tensor("below_parts", [P, PARTS], F32))
            parts = overlaid.enter_context(nc.sbuf_tensor("parts", [P, PARTS_COLS], F32R))
        arena = sb("arena", [P, ARENA])

        def A(lo, *shape):
            n = 1
            for s in shape:
                n *= s
            v = arena[:, lo:lo + n]
            if len(shape) == 2:
                v = v.rearrange("p (a b) -> p a b", a=shape[0])
            elif len(shape) == 3:
                v = v.rearrange("p (a b c) -> p a b c", a=shape[0], b=shape[1])
            elif len(shape) == 4:
                v = v.rearrange("p (a b c d) -> p a b c d", a=shape[0], b=shape[1], c=shape[2])
            return v

        def half(buf, p):
            return buf[:, p * HALF:(p + 1) * HALF]

        def bank(n):
            return ps[:, n, :]

        ident = W("ident")

        def linked(eng, name):
            count = [0]

            def link(ins):
                count[0] += 1
                ins.then_inc(S(name), 1)
                eng.wait_ge(S(name), count[0])
            return link

        def piece(eng, name):
            n = next(i for i, e in enumerate(PIECE_ENDS) if PACK_AT[name][0] < e)
            eng.wait_ge(S(f"pack_{n}"), 16)

        block = ctx.enter_context(nc.Block())

        NORMS = ["ctx", "0", "lat", "1", "2", "3", "4", "5", "6", "7", "rms1", "rms2", "8", "inner", "9", "10", "11"]

        def nth(tag, p):
            return 2 * NORMS.index(tag) + p + 1

        def wait_x(eng, l, p=1):
            if l == 0:
                eng.wait_ge(S("x_loaded"), 16)
            else:
                eng.wait_ge(S("x_ready"), 2 * (l - 1) + p + 1)


        def norm_deviations(pe, src, ready, d_bank=2):
            for p in range(2):
                ready(p)
                nc.tensor.matmul(bank(d_bank + p), W("center"), half(src, p), start=True, stop=True).then_inc(S("norm_d"), 1)

        def norm_tensor(pe, tag, src, ready):
            norm_deviations(pe, src, ready)
            norm_mean(pe, tag)

        def norm_mean(pe, tag, var_bank=4):
            for p in range(2):
                pe.wait_ge(S("norm_sq"), nth(tag, p))
                nc.tensor.matmul(bank(var_bank + p), W("mean"), half(sq, p), start=True, stop=True).then_inc(S("norm_var"), 1)

        def log_tables():
            nc.scalar.preload_act_table_set("natural_log_exp_and_others")

        def norm_scalar(act, tag, eps=None, src=None, root=False, d_bank=2, var_bank=4):
            for p in range(2):
                if src is None:
                    act.wait_ge(S("norm_d"), nd(tag, p))
                nc.scalar.activation(half(sq, p), bank(d_bank + p) if src is None else half(src, p),
                                     ACT.Square).then_inc(S("norm_sq"), 1)
            if root:
                for p in range(2):
                    act.wait_ge(S("norm_var"), nth(tag, p))
                    nc.scalar.activation(half(rstd, p), bank(var_bank + p), ACT.Sqrt, bias=eps5).then_inc(S("norm_root"), 1)
                log_tables()
            for p in range(2):
                if root:
                    act.wait_ge(S("norm_root"), p + 1)
                else:
                    act.wait_ge(S("norm_var"), nth(tag, p))
                nc.scalar.activation(half(rstd, p), half(rstd, p) if root else bank(var_bank + p), ACT.Ln,
                                     bias=0.0 if root else eps5 if eps is None else eps).then_inc(S("norm_ln"), 1)
                act.wait_ge(S("norm_ln"), nth(tag, p))
                nc.scalar.activation(half(rstd, p), half(rstd, p), ACT.Exp, scale=-1.0 if root else -0.5).then_inc(S("norm_rstd"), 1)

        def nd(tag, p):
            n = NORMS.index(tag)
            return 2 * (n - sum(NORMS.index(r) < n for r in ("rms1", "rms2"))) + p + 1

        def residual_norm_tensor(pe, l):
            def ready(p):
                pe.wait_ge(S("sum_ready"), 2 * l + p + 1)
            norm_tensor(pe, str(l), hsum, ready)

        def residual_norm_vector(dve, l, bias=None, res=None, meanwhile=None):
            for p in range(2):
                dve.wait_ge(S("y_ready"), 2 * l + p + 1)
                nc.vector.scalar_tensor_tensor(out=half(hsum, p), in0=bank(p), scalar=0.0 if bias is None else bias,
                                               in1=half(xT if res is None else res, p),
                                               op0=ALU.add, op1=ALU.add).then_inc(S("sum_ready"), 1)
            if meanwhile:
                meanwhile()
            for p in range(2):
                dve.wait_ge(S("norm_rstd"), nth(str(l), p))
                nc.vector.tensor_tensor(half(xT, p), bank(2 + p), half(rstd, p), ALU.mult).then_inc(S("x_ready"), 1)

        x_q = A(0, XH, T)
        x_kv = A(8192, B, 2, P)
        x_kvt = A(10240, B, 2, P)
        x_m = A(12288, XH, P)
        x_u = A(13312, XH, P)
        x_c = A(14336, XH)
        x_qs = A(14400, 2, XH, P)
        x_kvts = A(16960, 2, 2, P)
        x_p = A(17472, 2, 4, 2 * P)
        x_pt = A(19520, 2, 2, 512)
        x_nm = A(21568, 2, 4)
        x_sum = A(21576, 2, 4)
        x_rec = A(21584, 2, 4)
        x_bo = A(21592, 1)

        a_kb = A(0, NH, T)
        a_q = A(16384, T)
        a_k = A(17408, T)
        a_v = A(18432, B, NH, VA)
        a_vflat = A(18432, B * NH * VA)
        a_qs = A(19584, 2, P)
        a_p = A(19840, 2, NH // 2, P)
        a_pt = A(21888, 2, NH // 2, P)
        a_rope = A(19840, 2, 2, 2, HALF)
        a_cn = A(23936, B, P)
        a_oT = a_q
        a_mx = A(24960, 2, NH // 2)
        a_rec = A(24976, 2, NH)
        f_h = A(25024, T)
        f_x2 = A(6528, T)
        f_res = A(7552, T)

        m_lg = A(0, B, E)
        m_e = A(64, B, E)
        m_mx = A(128, B)
        m_ahead = A(192, B * E * E)
        m_rank = A(1216, B, E)
        m_w = A(1280, B, E)
        m_s = A(1344, B)
        m_z = A(1352, B)
        m_d = A(1360, B)
        m_parts = A(1408, B * P // 2).bitcast(BF16).rearrange("p (b c) -> p b c", b=B)
        m_wT = A(1920, T // 2).bitcast(BF16)
        m_sg = A(2432, 2, HALF)
        zeros = sb("zeros", [P, HALF], BF16)
        def parts_of(lo, n, cols):
            return parts[:, lo:lo + n * cols].rearrange("p (a b) -> p a b", a=n)
        m_wh, m_wl = parts_of(0, 2, RING), parts_of(2 * RING, 2, RING)
        m_xh, m_xl = parts[:, 4 * RING:4 * RING + T], parts[:, 4 * RING + T:4 * RING + 2 * T]
        m_xwh, m_xwl = parts_of(4 * RING + 2 * T, 2, T), parts_of(4 * RING + 4 * T, 2, T)
        m_hh, m_hl = parts_of(4 * RING + 6 * T, 2, HALF), parts_of(4 * RING + 6 * T + 2 * HALF, 2, HALF)
        m_x2 = A(8576, T)

        g_c = small[:, 8:11]
        g_s = small[:, 11:14]
        g_n = small[:, 14:17]
        g_n2 = small[:, 17:20]
        g_a = small[:, 20:21]
        g_b = small[:, 21:22]
        g_rot = A(19584, 3, P)
        g_t = A(19968, 3, P)
        g_q = A(20352, T)
        g_k = A(21376, T)
        g_v = A(22400, B, P)
        g_z = A(23424, B, P)
        g_pt = A(24448, B, P)
        g_av = A(25472, B, P)
        g_sq = A(26496, B, P)
        g_mx = A(27520, B)
        g_sm = A(27528, B)
        g_rc = A(27536, B)
        g_in = A(27544, B)

        q_w = A(25024, 36, 32)
        q_wT = A(26176, 9, P)
        q_ab = A(27328, 36)
        q_sc = A(27364, 36)
        q_inv = A(27400, 36)
        q_part = A(0, 2, 6)
        q_x = A(2432, T)
        q_up = A(3456, 3 * T)
        q_gate = A(6528, 3 * T)
        q_sig = A(9600, 3 * T)
        q_col = small[:, 24:29]
        q_s = small[:, 32:37]
        q_i = small[:, 40:45]
        ones1 = sb("ones1", [1, P])
        q_top = sb("q_top", [1, 8])

        r_prev = A(19584, B, P)
        r_ekv = A(19584, T)
        r_diff = A(20608, T)
        r_den = r_diff
        r_k = A(21632, T)
        r_v = A(22656, T)
        r_r = A(23680, T)
        r_sig = r_r
        r_ek = A(24704, T)
        r_sa = A(25728, B, P + 1)
        r_sb = A(26760, B, P + 1)
        r_dec = small[:, 48:49]
        r_u = small[:, 49:50]
        r_e = small[:, 50:51]

        s_sig = A(0, T)
        s_u = A(1024, T)
        s_st = A(2048, T)
        s_h = A(3072, T)
        s_hn = A(4096, T)
        s_a = small[:, 51:52]

        d_r = A(0, T)
        d_s = A(1024, T)
        d_w = small[:, 52:53]
        d_e = small[:, 53:54]

        e_a = A(0, T)

        t_p = A(0, B, NE)
        t_rep = A(1280, B, NE)
        t_top = A(2560, B, TOPK)
        t_s = A(2624, B)
        t_w = A(2688, B, NE)
        t_scaled = A(3968, B, NE)
        t_parts = A(5248, B * SETS * P // 2).bitcast(BF16).rearrange("p (b s c) -> p b s c", b=B, s=SETS)
        t_combT = A(7296, SETS * T // 2).bitcast(BF16).rearrange("p (s t) -> p s t", s=SETS)
        t_sg = A(23424, 2, HALF)
        t_sh = A(24448, T)

        def bankb(n):
            return ps[:, n, :].bitcast(BF16)

        CREDIT = {"a_pt": 1, "a_cn": 2, "m_down": 1}

        def credited(eng, *names):
            for name in names:
                eng.sem_inc(S(name), CREDIT.get(name, 1))

        WAVES, UNITS = 2 * B, (E * 2 * M0_CH, E * 2 * M2_CH)
        LEFT = {"a_kproj": 2, "a_qproj": 2, "a_q_ready": 2, "a_k_ready": 2, "a_kb0": NH, "a_kb1": NH, "a_vproj": 1, "a_v_ready": 1,
                "a_ones": 1, "a_slices": B, "a_scores": WAVES, "a_mx": WAVES, "a_z": WAVES, "a_p": WAVES, "a_turned": WAVES,
                "a_pt": WAVES, "a_weighed": WAVES, "a_rec": B, "a_cn": B, "a_oturned": 2, "a_oT": 2, "a_rope_k": 0, "a_rope_q": 0,
                "m_logits": 1, "m_lg": 1, "m_e": 1, "m_pad": 1, "m_parts": 3, "m_wturned": 1, "m_wT": 1, "m_spread": 2 * E, "m_xw": 2 * E,
                "m_xwh": 2 * E, "m_xwl": 2 * E,
                "m_xh": 2, "m_xl": 2, "m_wh": 2 * E, "m_split": E,
                "m_gate": UNITS, "m_silu": UNITS, "m_up": UNITS, "m_hid": UNITS, "m_hh": UNITS, "m_hl": UNITS, "m_down": (UNITS[0] - 2, UNITS[1] - 2),
                "m_load0": 16 * E, "m_load1": 16 * E}
        RUN = {"x1": ("a", 0), "x2": ("a", 1), "f2": ("a", 2), "m0": ("m", 0), "m2": ("m", 1), "m3": ("m", 2)}

        def R(t, name):
            return S(RUN[t][0] + name)

        def waits(eng, t):
            kind, run = RUN[t]

            def before(name):
                left = LEFT[kind + name]
                return sum(left[0:run]) if isinstance(left, tuple) else run * left
            return lambda name, v: eng.wait_ge(S(kind + name), v + before(name) + CREDIT.get(kind + name, 0))

        def credited_once(eng, t, *names):
            if RUN[t][1] == 0:
                credited(eng, *(RUN[t][0] + name for name in names))



        def narrow_keys_tensor(pe, t):
            piece(pe, t + "_wk")
            pe.wait_ge(S("ctx_loaded"), 16)
            for p in range(2):
                nc.tensor.matmul(bank(6 + p), W(t + "_wk"), half(ctxT, p), start=True, stop=True).then_inc(R(t, "_kproj"), 1)

        def narrow_values_tensor(pe, t, src, first):
            for b in range(B):
                ins = nc.tensor.matmul(ps[:, first + b // HB, (b % HB) * P:(b % HB + 1) * P], src[:, b * P:(b + 1) * P], W(t + "_wv"),
                                       start=True, stop=True, skip_group_check=True)
            ins.then_inc(R(t, "_vproj"), 1)

        def narrow_tensor(pe, t, qsrc, rope, mask, wo, done="y_ready"):
            wait = waits(pe, t)
            mm = nc.tensor.matmul
            if rope:
                for first, names, signal in ((4, ("_wk", "_wkr"), "_kproj"), (0, ("_wq", "_wqr"), "_qproj")):
                    for p in range(2):
                        pe.wait_ge(S("f2_h"), p + 1)
                        for k, name in enumerate(names):
                            ins = mm(bank(first + 2 * k + p), W(t + name), half(qsrc, p), start=True, stop=True)
                        ins.then_inc(R(t, signal), 1)
                wait("_rope_k", 4)
                narrow_values_tensor(pe, t, qsrc, 6)
            else:
                for p in range(2):
                    mm(bank(2 + p), W(t + "_wq"), half(qsrc, p), start=True, stop=True).then_inc(R(t, "_qproj"), 1)

            def scores(b, v, slot):
                if v == 0:
                    wait("_slices", b + 1)
                for jj in range(2):
                    sbank = 2 * v + jj
                    if mask is not None:
                        rows = mask if mask is caus else mask[:, bass.ds(b * P, P)]
                        mm(bank(sbank), identb[:, :], (rows[:, :] if mask is caus else rows).unsqueeze(1).to_broadcast([P, 4, P]),
                           start=True, stop=False, skip_group_check=True)
                    ins = mm(bank(sbank), a_qs[:, slot, :], a_kb[:, 4 * sbank:4 * sbank + 4, bass.ds(b * P, P)],
                             start=mask is None, stop=True, skip_group_check=True)
                ins.then_inc(R(t, "_scores"), 1)

            def turn(v, w, first=4):
                wait("_p", w + 1)
                if first == 4:
                    wait("_pt", w)
                for n in range(NH // 2):
                    ins = nc.tensor.transpose(ps[:, first + n // 4, (n % 4) * P:(n % 4 + 1) * P], a_p[:, v, n, :], ident)
                ins.then_inc(R(t, "_turned"), 1)

            def weigh(b, v, w, slot):
                if v == 0:
                    wait("_cn", b - 1)
                wait("_pt", w + 1)
                for n in range(NH // 2):
                    h = NH // 2 * v + n
                    ins = mm(ps[:, 6 + slot, h * VA:(h + 1) * VA], a_pt[:, v, n, :],
                             a_vflat[:, bass.ds(b * (NH * VA) + h * VA, VA)], start=True, stop=True, skip_group_check=True)
                ins.then_inc(R(t, "_weighed"), 1)

            def turn_outputs(p):
                wait("_cn", HB * (p + 1))
                for b in range(HB):
                    ins = nc.tensor.transpose(ps[:, 2 + p, b * P:(b + 1) * P], a_cn[:, HB * p + b, :], ident)
                ins.then_inc(R(t, "_oturned"), 1)

            def body(i, final):
                for k in range(4):
                    b, v, w = 2 * i + k // 2, k % 2, 4 * i + k
                    if not (final and k == 3):
                        turn(v, w)
                    if final and k == 2:
                        turn(1, w + 1, 0)
                        turn_outputs(0)
                    if not (final and k >= 2):
                        wait("_kb1", NH)
                        scores(2 * i + k // 2 + 1, v, (k // 2 + 1) % 2)
                    if k == 0:
                        wait("_v_ready", 1)
                    weigh(b, v, w, k // 2)

            wait("_kb0", NH)
            if rope:
                wait("_rope_q", 4)
            scores(0, 0, 0)
            if not rope:
                wait("_q_ready", 2)
            scores(0, 1, 0)
            with pe.Fori(0, B // 2 - 1) as i:
                body(i, False)
            body(B // 2 - 1, True)
            for p in range(2):
                wait("_oT", p + 1)
                if p == 0:
                    turn_outputs(1)
                mm(bank(p), wo, half(a_oT, p), start=True, stop=True).then_inc(S(done), 1)

        def spread_keys(eng, t, heads, scaled):
            for p, (lo, hi) in enumerate(((0, P), (P, T))):
                waits(eng, t)("_k_ready", p + 1)
                for h in heads[p]:
                    scaled(a_kb[:, h, lo:hi], a_k[:, lo:hi], W("headmask")[:, h:h + 1]).then_inc(R(t, f"_kb{p}"), 1)

        def narrow_keys_scalar(act, t, bk):
            for p in range(2):
                waits(act, t)("_kproj", p + 1)
                nc.scalar.activation(half(a_k, p), bank(6 + p), ACT.Identity, bias=bk).then_inc(R(t, "_k_ready"), 1)

        def narrow_spread_scalar(act, t, *heads):
            spread_keys(act, t, heads, lambda dst, src, col: nc.scalar.activation(dst, src, ACT.Copy, scale=col))

        def narrow_values_scalar(act, t, first):
            waits(act, t)("_vproj", 1)
            waits(act, t)("_ones", 1)
            for p in range(2):
                ins = nc.scalar.activation(a_v[:, HB * p:HB * (p + 1), :, 0:HD].rearrange("p b h d -> p (b h) d"),
                                           bank(first + p).rearrange("p (n d) -> p n d", d=HD), ACT.Copy)
            ins.then_inc(R(t, "_v_ready"), 1)

        def narrow_scalar(act, t, rope, bv, scale, bq=None, meanwhile=None):
            wait = waits(act, t)
            credited_once(act, t, "_pt")
            if not rope:
                for p in range(2):
                    wait("_qproj", p + 1)
                    if p == 0:
                        for b in range(2):
                            nc.scalar.activation(a_qs[:, b], ps[:, 2, b * P:(b + 1) * P], ACT.Identity, bias=bq).then_inc(R(t, "_slices"), 1)
                    nc.scalar.activation(half(a_q, p), bank(2 + p), ACT.Identity, bias=bq).then_inc(R(t, "_q_ready"), 1)

            def exps(v, w):
                wait("_z", w + 1)
                nc.scalar.activation(a_p[:, v], a_p[:, v], ACT.Exp, scale=scale).then_inc(R(t, "_p"), 1)

            def copies(v, w, first=4):
                wait("_turned", w + 1)
                nc.scalar.activation(a_pt[:, v], ps[:, first:first + 2, :].rearrange("p a (n q) -> p (a n) q", n=4), ACT.Copy).then_inc(R(t, "_pt"), 1)

            def body(i, final):
                for k in range(4):
                    w = 4 * i + k
                    copies(k % 2, w, 0 if final and k == 3 else 4)
                    if not (final and k >= 2):
                        exps((k + 1) % 2, w + 1)
                    if final and k == 1:
                        exps(1, w + 2)

            exps(0, 0)
            if meanwhile:
                meanwhile()
            if rope:
                wait("_q_ready", 2)
            with act.Fori(0, B // 2 - 1) as i:
                body(i, False)
            body(B // 2 - 1, True)
            for p in range(2):
                wait("_oturned", p + 1)
                nc.scalar.activation(half(a_oT, p), bank(2 + p), ACT.Identity, bias=0.0 if bv is None else bv).then_inc(R(t, "_oT"), 1)

        def narrow_spread_vector(dve, t, *heads):
            spread_keys(dve, t, heads, lambda dst, src, col: nc.vector.tensor_scalar(dst, src, col, None, ALU.mult))

        def narrow_rope_vector(dve, t):
            wait = waits(dve, t)
            for k, (first, proj, part) in enumerate(((4, "_kproj", "_rope_k"), (0, "_qproj", "_rope_q"))):
                for p in range(2):
                    wait(proj, p + 1)
                    for m, tab in enumerate(("cos", "sin")):
                        nc.vector.tensor_tensor(a_rope[:, k, m, p].rearrange("p (b t) -> p b t", b=HB),
                                                bank(first + 2 * m + p).rearrange("p (b t) -> p b t", b=HB),
                                                W(tab).unsqueeze(1).to_broadcast([P, HB, P]), ALU.mult).then_inc(R(t, part), 1)
                if k == 0:
                    for p in range(2):
                        wait("_rope_k", 2 * p + 2)
                        nc.vector.tensor_tensor(half(a_k, p), a_rope[:, 0, 0, p], a_rope[:, 0, 1, p], ALU.add).then_inc(R(t, "_k_ready"), 1)

        def narrow_vector(dve, t, meanwhile=None):
            wait = waits(dve, t)
            credited_once(dve, t, "_cn")

            def maxima(v, w, first=False):
                wait("_scores", w + 1)
                sc = ps[:, 2 * v:2 * v + 2, :].rearrange("p a (g k) -> p (a g) k", g=4)
                nc.vector.tensor_reduce(a_mx[:, v], sc, AX.X, ALU.max).then_inc(R(t, "_mx"), 1)
                wait("_mx", w + 1)
                if not first:
                    wait("_turned", w - 1)
                nc.vector.tensor_tensor(a_p[:, v], sc, a_mx[:, v].unsqueeze(2).to_broadcast([P, NH // 2, P]),
                                        ALU.subtract).then_inc(R(t, "_z"), 1)

            def outputs(b, slot):
                wait("_weighed", 2 * b + 2)
                o = ps[:, 6 + slot, 0:NH * VA].rearrange("p (h d) -> p h d", d=VA)
                nc.vector.reciprocal(a_rec[:, slot], o[:, :, HD]).then_inc(R(t, "_rec"), 1)
                wait("_rec", b + 1)
                nc.vector.tensor_tensor(a_cn[:, bass.ds(b, 1), :].rearrange("p o (h d) -> p (o h) d", d=HD), o[:, :, 0:HD],
                                        a_rec[:, slot].unsqueeze(2).to_broadcast([P, NH, HD]), ALU.mult).then_inc(R(t, "_cn"), 1)

            def body(i, final):
                for k in range(4):
                    if not (final and k >= 2):
                        maxima(k % 2, 4 * i + k + 2)
                    if k % 2 == 1:
                        outputs(2 * i + k // 2, k // 2)
                    if final and k == 1 and meanwhile:
                        meanwhile()

            maxima(0, 0, True)
            maxima(1, 1, True)
            with dve.Fori(0, B // 2 - 1) as i:
                body(i, False)
            body(B // 2 - 1, True)

        def narrow_ones(pool, t):
            nc.gpsimd.memset(a_v[:, :, :, HD], 1.0).then_inc(R(t, "_ones"), 1)

        def narrow_spread_gpsimd(pool, t, *heads):
            spread_keys(pool, t, heads, lambda dst, src, col: nc.gpsimd.tensor_tensor(dst, src, col.to_broadcast(list(src.shape)), ALU.mult))

        def narrow_gpsimd(pool, t, rope, *heads):
            wait = waits(pool, t)

            def slices(b, slot):
                nc.gpsimd.tensor_copy(a_qs[:, slot], a_q[:, bass.ds(b * P, P)]).then_inc(R(t, "_slices"), 1)

            if rope:
                narrow_spread_gpsimd(pool, t, heads[0], ())
                for p in range(2):
                    cos, sin = a_rope[:, 1, 0, p], a_rope[:, 1, 1, p]
                    wait("_rope_q", 2 * p + 2)
                    if p == 0:
                        for b in range(2):
                            at = slice(b * P, (b + 1) * P)
                            nc.gpsimd.tensor_tensor(a_qs[:, b], cos[:, at], sin[:, at], ALU.add).then_inc(R(t, "_slices"), 1)
                    nc.gpsimd.tensor_tensor(half(a_q, p), cos, sin, ALU.add).then_inc(R(t, "_q_ready"), 1)
                narrow_spread_gpsimd(pool, t, (), heads[1])
            wait("_q_ready", 2)
            with pool.Fori(1, B // 2) as i:
                for slot in range(2):
                    wait("_scores", 4 * i + 2 * slot - 2)
                    slices(2 * i + slot, slot)


        def mm3(dst, w_high, w_low, x_high, x_low, start, stop):
            nc.tensor.matmul(dst, w_high, x_high, start=start, stop=False, skip_group_check=True)
            nc.tensor.matmul(dst, w_high, x_low, start=False, stop=False, skip_group_check=True)
            return nc.tensor.matmul(dst, w_low, x_high, start=False, stop=stop, skip_group_check=True)

        def input_high(act, t, src, ready):
            for p in range(2):
                ready(p)
                nc.scalar.activation(half(m_xh, p), half(src, p), ACT.Copy).then_inc(R(t, "_xh"), 1)

        def input_low(eng, engine, t, src):
            for p in range(2):
                waits(eng, t)("_xh", p + 1)
                engine.tensor_tensor(half(m_xl, p), half(src, p), half(m_xh, p), ALU.subtract).then_inc(R(t, "_xl"), 1)

        def split_weights(pool, t, slot, areas, count):
            for rows, cols in areas:
                ins = nc.gpsimd.tensor_tensor(m_wh[0:rows, slot, cols], ring[0:rows, slot, cols],
                                              zeros[0:rows, 0:1].to_broadcast([rows, cols.stop - cols.start]), ALU.add)
                ins.then_inc(R(t, "_wh"), 1)
            waits(pool, t)("_wh", count + len(areas))
            for rows, cols in areas:
                ins = nc.gpsimd.tensor_tensor(m_wl[0:rows, slot, cols], ring[0:rows, slot, cols], m_wh[0:rows, slot, cols], ALU.subtract)
            ins.then_inc(R(t, "_split"), 1)


        def hidden_high(act, t, n, p, rows, src):
            waits(act, t)("_hid", n + 1)
            nc.scalar.activation(m_hh[0:rows, p], ps[0:rows, src, :], ACT.Copy).then_inc(R(t, "_hh"), 1)

        def hidden_low(dve, t, n, p, rows, src):
            waits(dve, t)("_hh", n + 1)
            nc.vector.tensor_tensor(m_hl[0:rows, p], ps[0:rows, src, :], m_hh[0:rows, p], ALU.subtract).then_inc(R(t, "_hl"), 1)


        def route_tensor(pe, t, src):
            for b in range(B):
                ins = nc.tensor.matmul(ps[:, 2, b * E:(b + 1) * E], src[:, b * P:(b + 1) * P], W(t + "_router"),
                                       start=True, stop=True, skip_group_check=True)
            ins.then_inc(R(t, "_logits"), 1)
            waits(pe, t)("_parts", 3)
            waits(pe, t)("_pad", 1)
            for b in range(B):
                ins = nc.tensor.transpose(bankb(3)[:, b * P:(b + 1) * P], m_parts[:, b, :], identb[:, :])
            ins.then_inc(R(t, "_wturned"), 1)

        def route_scalar(act, t):
            waits(act, t)("_lg", 1)
            nc.scalar.activation(m_e[:, :, :], m_lg[:, :, :], ACT.Exp).then_inc(R(t, "_e"), 1)

        def route_vector(dve, t, zterm, link):
            V = nc.vector
            waits(dve, t)("_logits", 1)
            lg = ps[:, 2, 0:B * E].rearrange("p (b e) -> p b e", b=B)
            link(V.tensor_reduce(m_mx, lg, AX.X, ALU.max))
            V.tensor_tensor(m_lg, lg, m_mx.unsqueeze(2).to_broadcast([P, B, E]), ALU.subtract).then_inc(R(t, "_lg"), 1)
            waits(dve, t)("_e", 1)
            flat = m_e.rearrange("p b e -> p (b e)")
            for size, col in ((4, 0), (2, 4), (1, 6)):
                two = flat.rearrange("p (g h i) -> p g h i", h=2, i=size)
                rows = m_ahead.rearrange("p (g h i c) -> p g h i c", h=2, i=size, c=E)
                n = B * E // (2 * size)
                for mine, others, ahead in ((0, 1, ALU.is_gt), (1, 0, ALU.is_ge)):
                    ins = V.tensor_tensor(rows[:, :, mine, :, col:col + size],
                                          two[:, :, others, :].unsqueeze(2).to_broadcast([P, n, size, size]),
                                          two[:, :, mine, :].unsqueeze(3).to_broadcast([P, n, size, size]), ahead)
            link(ins)
            link(V.tensor_reduce(m_rank, m_ahead.rearrange("p (b e c) -> p b e c", b=B, c=E)[:, :, :, 0:E - 1], AX.X, ALU.add))
            if zterm:
                link(V.tensor_reduce(m_z, m_e, AX.X, ALU.add))
            link(V.scalar_tensor_tensor(out=m_w, in0=m_rank, scalar=1.5, in1=m_e, op0=ALU.is_lt, op1=ALU.mult))
            link(V.tensor_reduce(m_s, m_w, AX.X, ALU.add))
            if zterm:
                link(V.scalar_tensor_tensor(out=m_s, in0=m_z, scalar=zterm, in1=m_s, op0=ALU.mult, op1=ALU.add))
            link(V.reciprocal(m_d, m_s))
            link(V.tensor_tensor(m_w, m_w, m_d.unsqueeze(2).to_broadcast([P, B, E]), ALU.mult))
            waits(dve, t)("_pad", 1)
            for k in range(3):
                part = m_parts[:, :, k:3 * E:3]
                ins = V.tensor_copy(part, m_w)
                ins.then_inc(R(t, "_parts"), 1)
                if k < 2:
                    waits(dve, t)("_parts", k + 1)
                    link(V.tensor_tensor(m_w, m_w, part, ALU.subtract))
            waits(dve, t)("_wturned", 1)
            V.tensor_copy(m_wT, bankb(3)).then_inc(R(t, "_wT"), 1)

        def spread_bank(e, p):
            return 6 if isinstance(e, int) and e == 0 and p == 1 else 7

        def mix_tensor(pe, t, CH, ROWS):
            wait = waits(pe, t)
            mm = nc.tensor.matmul
            UPE = 2 * CH
            pe.wait_ge(S("filled"), 6)
            for p in range(2):
                mm(bank(p), zeros[:, 0:P], zeros[:, :], start=True, stop=False, skip_group_check=True)

            def spread(e, p):
                if not isinstance(e, int) or e > 0:
                    wait("_xwl", 2 * e + p)
                mm(bank(spread_bank(e, p)), sel8[:, bass.ds(e * P, P)], half(m_wT, p), start=True, stop=True).then_inc(R(t, "_spread"), 1)

            def weights(slot, at, n, rows=P):
                return m_wh[0:rows, slot, at:at + n], m_wl[0:rows, slot, at:at + n]

            def gate(e, slot, u, n):
                c, p = u // 2, u % 2
                if u == 0:
                    wait("_split", e + 1)
                if not isinstance(n, int) or n >= 1:
                    wait("_silu", n)
                mm3(ps[0:ROWS, 2, :], *weights(slot, c * ROWS, ROWS), half(m_xh, p), half(m_xl, p), True, True).then_inc(R(t, "_gate"), 1)

            def up(e, slot, u, n):
                c, p = u // 2, u % 2
                if c == 0:
                    wait("_xwl", 2 * e + p + 1)
                mm3(ps[0:ROWS, 3 + u % 4, :], *weights(slot, (CH + c) * ROWS, ROWS), half(m_xwh[:, slot], p), half(m_xwl[:, slot], p),
                    True, True).then_inc(R(t, "_up"), 1)

            def gate_up(*unit):
                gate(*unit)
                up(*unit)

            def down(slot, c, p, n, final):
                wait("_hl", n + 1)
                mm3(bank(p), *weights(slot, 2 * CH * ROWS + c * P, P, ROWS), m_hh[0:ROWS, p], m_hl[0:ROWS, p],
                    False, final).then_inc(S("y_ready") if final else R(t, "_down"), 1)

            def body(i, last_pair):
                for slot in range(2):
                    e = 2 * i + slot
                    last_expert = last_pair and slot == 1
                    for u in range(UPE):
                        n = UPE * e + u
                        if u == 0 and not last_expert:
                            spread(e + 1, 0)
                        if u < UPE - 2:
                            gate_up(e, slot, u + 2, n + 2)
                        elif not last_expert:
                            gate_up(e + 1, 1 - slot, u + 2 - UPE, n + 2)
                        down(slot, u // 2, u % 2, n, last_expert and u >= UPE - 2)
                        if u == 1 and not last_expert:
                            spread(e + 1, 1)

            wait("_xl", 2)
            gate(0, 0, 0, 0)
            wait("_wT", 1)
            for p in range(2):
                spread(0, p)
            up(0, 0, 0, 0)
            gate_up(0, 0, 1, 1)
            with pe.Fori(0, E // 2 - 1) as i:
                body(i, False)
            body(E // 2 - 1, True)

        def mix_scalar(act, t, CH, ROWS):
            wait = waits(act, t)
            UPE = 2 * CH

            def silu(n, p):
                wait("_gate", n + 1)
                nc.scalar.activation(m_sg[0:ROWS, p], ps[0:ROWS, 2, :], ACT.Silu).then_inc(R(t, "_silu"), 1)

            def weighted_high(e, slot, p):
                wait("_xw", 2 * e + p + 1)
                nc.scalar.activation(half(m_xwh[:, slot], p), bank(spread_bank(e, p)), ACT.Copy).then_inc(R(t, "_xwh"), 1)

            def body(i, last_pair):
                for slot in range(2):
                    e = 2 * i + slot
                    last_expert = last_pair and slot == 1
                    for u in range(UPE):
                        n = UPE * e + u
                        if not (last_expert and u == UPE - 1):
                            wait("_down", n)
                            hidden_high(act, t, n + 1, (u + 1) % 2, ROWS, 3 + (u + 1) % 4)
                        if not (last_expert and u >= UPE - 2):
                            silu(n + 2, u % 2)
                        if u in (0, 2) and not last_expert:
                            weighted_high(e + 1, 1 - slot, u // 2)

            nc.scalar.preload_act_table(ACT.Silu)
            silu(0, 0)
            for p in range(2):
                weighted_high(0, 0, p)
            hidden_high(act, t, 0, 0, ROWS, 3)
            silu(1, 1)
            credited_once(act, t, "_down")
            with act.Fori(0, E // 2 - 1) as i:
                body(i, False)
            body(E // 2 - 1, True)
            log_tables()

        def mix_vector(dve, t, src, CH, ROWS):
            wait = waits(dve, t)
            UPE = 2 * CH

            def weighted(e, p):
                wait("_spread", 2 * e + p + 1)
                weights = bank(spread_bank(e, p))
                nc.vector.tensor_tensor(weights, half(src, p), weights, ALU.mult).then_inc(R(t, "_xw"), 1)

            def weighted_low(e, slot, p):
                wait("_xwh", 2 * e + p + 1)
                nc.vector.tensor_tensor(half(m_xwl[:, slot], p), bank(spread_bank(e, p)), half(m_xwh[:, slot], p), ALU.subtract).then_inc(R(t, "_xwl"), 1)

            def hidden(n, u):
                wait("_silu", n + 1)
                wait("_up", n + 1)
                nc.vector.tensor_tensor(ps[0:ROWS, 3 + u % 4, :], m_sg[0:ROWS, u % 2], ps[0:ROWS, 3 + u % 4, :], ALU.mult).then_inc(R(t, "_hid"), 1)

            def body(i, last_pair):
                for slot in range(2):
                    e = 2 * i + slot
                    last_expert = last_pair and slot == 1
                    for u in range(UPE):
                        n = UPE * e + u
                        if not (last_expert and u == UPE - 1):
                            hidden(n + 1, u + 1)
                        if u in (0, 2) and not last_expert:
                            weighted(e + 1, u // 2)
                        hidden_low(dve, t, n, u % 2, ROWS, 3 + u % 4)
                        if u in (1, 3) and not last_expert:
                            weighted_low(e + 1, 1 - slot, u // 2)

            for p in range(2):
                weighted(0, p)
            for p in range(2):
                weighted_low(0, 0, p)
            hidden(0, 0)
            with dve.Fori(0, E // 2 - 1) as i:
                body(i, False)
            body(E // 2 - 1, True)

        def mix_gpsimd(pool, t, src, CH, ROWS):
            UPE = 2 * CH
            areas = [(P, slice(0, 2 * CH * ROWS)), (ROWS, slice(2 * CH * ROWS, 2 * CH * ROWS + CH * P))]

            def split(e, slot):
                waits(pool, t)(f"_load{slot}", 16 * (e - slot) + 32)
                split_weights(pool, t, slot, areas, 2 * e)

            split(0, 0)
            input_low(pool, nc.gpsimd, t, src)
            split(1, 1)
            with pool.Fori(1, E // 2) as i:
                for slot in range(2):
                    waits(pool, t)("_down", UPE * (2 * i + slot - 1))
                    split(2 * i + slot, slot)

        def mix_load(sp, t, up_in, down_in, CH, ROWS):

            def load(e, slot):
                sp.dma_start(ring[:, slot, 0:2 * CH * ROWS], up_in[bass.ds(e, 1), :, :].rearrange("e p n -> p (e n)")).then_inc(R(t, f"_load{slot}"), 16)
                sp.dma_start(ring[0:ROWS, slot, 2 * CH * ROWS:2 * CH * ROWS + CH * P],
                             down_in[bass.ds(e, 1), :, :].rearrange("e p n -> p (e n)")).then_inc(R(t, f"_load{slot}"), 16)

            load(0, 0)
            load(1, 1)
            with sp.Fori(1, E // 2) as i:
                for slot in range(2):
                    waits(sp, t)("_split", 2 * i + slot - 1)
                    load(2 * i + slot, slot)

        SCALE8 = HD ** -0.5

        @block.sync
        def _(sp):
            def load_piece(n):
                lo = PIECE_ENDS[n - 1] if n else 0
                sp.dma_start(pack[:, lo:PIECE_ENDS[n]], pack_in[:, lo:PIECE_ENDS[n]]).then_inc(S(f"pack_{n}"), 16)
            sp.dma_start(xT[:, :], xT_in).then_inc(S("x_loaded"), 16)
            load_piece(0)
            sp.dma_start(ctxT[:, :], ctxT_in).then_inc(S("ctx_loaded"), 16)
            load_piece(1)
            sp.dma_start(identb[:, :], identb_in).then_inc(S("consts"), 16)
            sp.dma_start(sel8[:, :], sel8_in).then_inc(S("consts"), 16)
            sp.dma_start(caus[:, :], caus_in).then_inc(S("consts"), 16)
            sp.dma_start(sel160[:, :], sel160_in).then_inc(S("consts"), 16)
            load_piece(2)
            sp.dma_start(mask8[:, :], mask_in).then_inc(S("mask_loaded"), 16)
            for n in range(3, len(PIECES)):
                load_piece(n)
            sp.dma_start(ctx_tm[:, :], ctx_in).then_inc(S("ctxtm_loaded"), 16)
            mix_load(sp, "m0", m0_up_in, m0_down_in, M0_CH, M0_ROWS)
            waits(sp, "m0")("_split", E)
            mix_load(sp, "m2", m2_up_in, m2_down_in, M2_CH, M2_ROWS)
            waits(sp, "m2")("_split", E)

            def load(n, slot):
                sp.dma_start(ring[:, slot, 0:1024], m3_in[bass.ds(n, 1), :, :].rearrange("e p n -> p (e n)")).then_inc(R("m3", f"_load{slot}"), 16)
            load(0, 0)
            load(1, 1)
            with sp.Fori(1, GROUPS) as i:
                for slot in range(2):
                    waits(sp, "m3")("_split", 2 * i + slot - 1)
                    load(2 * i + slot, slot)
            for p in range(2):
                sp.wait_ge(S("x_ready"), 2 * (LAYERS - 1) + p + 1)
                sp.dma_start(half(out, p), half(xT, p)).then_inc(S("stored"), 16)
            sp.wait_ge(S("stored"), 32)

        @block.tensor
        def _(pe):
            mm = nc.tensor.matmul
            pe.wait_ge(S("pack_0"), 16)

            wait_x(pe, 0)
            for p in range(2):
                mm(bank(2 + p), W("l0_wk"), half(xT, p), start=True, stop=True).then_inc(S("l0_mm"), 1)
                mm(bank(4 + p), W("l0_wr"), half(xT, p), start=True, stop=True).then_inc(S("l0_mm"), 1)
            pe.wait_ge(S("ctx_loaded"), 16)
            norm_deviations(pe, ctxT, lambda p: None, d_bank=6)
            for p in range(2):
                pe.wait_ge(S("l0_gated"), p + 1)
                mm(bank(p), W("l0_wv"), half(d_s, p), start=True, stop=True).then_inc(S("y_ready"), 1)
            norm_mean(pe, "ctx", var_bank=2)
            for p in range(2):
                pe.wait_ge(S("norm_ln"), p + 1)
            residual_norm_tensor(pe, 0)

            piece(pe, "x0_wq")
            pe.wait_ge(S("norm_out"), 2)
            for h in range(XH):
                ins = mm(ps[:, 6 + h // 4, (h % 4) * P:(h % 4 + 1) * P], W("x0_wq", h * P, P), W("x0_wk", h * P, P),
                         start=True, stop=True, skip_group_check=True)
            ins.then_inc(S("x0_mw"), 1)
            for h in range(XH):
                ins = mm(ps[:, h // 4, (h % 4) * P:(h % 4 + 1) * P], W("x0_wv", h * P, P), W("x0_wo", h * P, P),
                         start=True, stop=True, skip_group_check=True)
            ins.then_inc(S("x0_mw"), 1)

            norm_tensor(pe, "lat", xT, lambda p: wait_x(pe, 1, p))
            pe.wait_ge(S("x0_m"), 1)
            for h in range(XH):
                ins = mm(ps[:, 6, h:h + 1], W("x0_wk", h * P, P), W("x0_bq", h, 1), start=True, stop=True, skip_group_check=True)
            for h in range(XH):
                ins = mm(ps[:, 7, 0:1], W("x0_wo", h * P, P), W("x0_bv", h, 1), start=(h == 0), stop=(h == XH - 1), skip_group_check=True)
            ins.then_inc(S("x0_mw"), 1)
            pe.wait_ge(S("norm_out"), 4)
            pe.wait_ge(S("x0_u"), 2)
            pe.wait_ge(S("x0_m"), 2)
            for b in range(B):
                for s in range(2):
                    ins = nc.tensor.transpose(ps[:, b // 2, (b % 2 * 2 + s) * P:(b % 2 * 2 + s + 1) * P], x_kv[:, b, s, :], ident)
                ins.then_inc(S("x0_kvt"), 1)
            for p in range(2):
                for h in range(XH):
                    n = XH * p + h
                    if n >= 4:
                        pe.wait_ge(S(f"x0_q{n % 2}"), n // 2 - 1)
                    mm(bank(4 + n % 4), x_m[:, h, :], x_kv[:, HB * p:HB * (p + 1), 1, :], start=True, stop=True).then_inc(S("x0_qmm"), 1)
            pe.wait_ge(S("x0_q0"), XH)
            pe.wait_ge(S("x0_q1"), XH)
            pe.wait_ge(S("x0_kvt_sb"), 4)

            def x_scores(b, v, slot):
                if v == 0:
                    pe.wait_ge(S("x0_qs"), b + 1)
                for i in range(4):
                    ins = mm(ps[:, 2 * v + i // 2, (i % 2) * 256:(i % 2 + 1) * 256], x_qs[:, slot, 4 * v + i, :],
                             x_kv[:, bass.ds(b, 1), :, :].rearrange("p o s k -> p (o s k)"), start=True, stop=True, skip_group_check=True)
                ins.then_inc(S("x0_scores"), 1)

            def x_turn(v, w):
                pe.wait_ge(S("x0_pn"), 4 * (w + 1))
                pe.wait_ge(S("x0_ptA"), w + 1)
                pe.wait_ge(S("x0_ptB"), w + 1)
                for s in range(2):
                    for i in range(4):
                        ins = nc.tensor.transpose(ps[:, 4 + s, i * P:(i + 1) * P], x_p[:, v, i, s * P:(s + 1) * P], ident)
                ins.then_inc(S("x0_turned"), 1)

            def x_weigh(b, v, w, slot):
                if v == 0:
                    pe.wait_ge(S("x0_kvts"), b + 1)
                pe.wait_ge(S("x0_ptA"), w + 2)
                pe.wait_ge(S("x0_ptB"), w + 2)
                pe.wait_ge(S("x0_o"), w + 1)
                for s in range(2):
                    ins = mm(bank(6 + v), x_kvts[:, slot, s, :], x_pt[:, v, s, :], start=(s == 0), stop=(s == 1))
                ins.then_inc(S("x0_weighed"), 1)

            def x_body(i, final):
                for k in range(4):
                    w = 4 * i + k
                    x_turn(k % 2, w)
                    if not (final and k >= 2):
                        x_scores(2 * i + k // 2 + 1, k % 2, (k // 2 + 1) % 2)
                    x_weigh(2 * i + k // 2, k % 2, w, k // 2)

            x_scores(0, 0, 0)
            x_scores(0, 1, 0)
            with pe.Fori(0, B // 2 - 1) as i:
                x_body(i, False)
            x_body(B // 2 - 1, True)
            pe.wait_ge(S("x0_o"), 2 * B + 2)
            for p in range(2):
                for h in range(XH):
                    ins = mm(bank(p), x_u[:, h, :], half(x_q[:, h, :], p), start=(h == 0), stop=(h == XH - 1))
                ins.then_inc(S("y_ready"), 1)
            residual_norm_tensor(pe, 1)

            piece(pe, "m0_router")
            pe.wait_ge(S("consts"), 64)
            wait_x(pe, 2)
            route_tensor(pe, "m0", xT)
            mix_tensor(pe, "m0", M0_CH, M0_ROWS)
            residual_norm_tensor(pe, 2)

            narrow_keys_tensor(pe, "x1")
            pe.wait_ge(S("l1_rot"), 1)
            wait_x(pe, 3)
            for p in range(2):
                mm(bank(p), g_rot[:, 0, :], half(xT, p), start=True, stop=True).then_inc(S("l1_mm"), 1)
                mm(bank(2 + p), g_rot[:, 1, :], half(xT, p), start=True, stop=True).then_inc(S("l1_mm"), 1)
                for b in range(HB * p, HB * (p + 1)):
                    ins = mm(ps[:, 4 + p, (b % HB) * P:(b % HB + 1) * P], xT[:, b * P:(b + 1) * P], g_rot[:, 2, :],
                             start=True, stop=True, skip_group_check=True)
                ins.then_inc(S("l1_mm"), 1)
            waits(pe, "x1")("_k_ready", 2)
            for p in range(2):
                pe.wait_ge(S("l1_qv"), 2 * p + 1)
                pe.wait_ge(S("l1_k"), p + 1)
                for b in range(HB * p, HB * (p + 1)):
                    ins = mm(ps[:, 6 + p, (b % HB) * P:(b % HB + 1) * P], g_q[:, b * P:(b + 1) * P], g_k[:, b * P:(b + 1) * P],
                             start=True, stop=True, skip_group_check=True)
                ins.then_inc(S("l1_scores"), 1)
            pe.wait_ge(S("l1_qv"), 4)
            narrow_values_tensor(pe, "x1", ctxT, 4)
            for p in range(2):
                pe.wait_ge(S("l1_e"), p + 1)
                for b in range(HB * p, HB * (p + 1)):
                    ins = nc.tensor.transpose(ps[:, p, (b % HB) * P:(b % HB + 1) * P], g_z[:, b, :], ident)
                ins.then_inc(S("l1_turned"), 1)
            for p in range(2):
                pe.wait_ge(S("l1_pt"), p + 1)
                pe.wait_ge(S("l1_qv"), 2 * p + 2)
                for b in range(HB * p, HB * (p + 1)):
                    ins = mm(ps[:, 2 + p, (b % HB) * P:(b % HB + 1) * P], g_pt[:, b, :], g_v[:, b, :],
                             start=True, stop=True, skip_group_check=True)
                ins.then_inc(S("l1_weighed"), 1)
            for p in range(2):
                pe.wait_ge(S("l1_out"), p + 1)
                for b in range(HB * p, HB * (p + 1)):
                    ins = nc.tensor.transpose(ps[:, p, (b % HB) * P:(b % HB + 1) * P], g_av[:, b, :], ident)
                ins.then_inc(S("y_ready"), 1)
            waits(pe, "x1")("_v_ready", 1)
            residual_norm_tensor(pe, 3)

            pe.wait_ge(S("maskb"), 1)
            wait_x(pe, 4)
            narrow_tensor(pe, "x1", xT, False, maskb, W("x1_wo"))
            residual_norm_tensor(pe, 4)

            pe.wait_ge(S("f1_wq"), 1)
            for n in range(9):
                ins = nc.tensor.transpose(ps[:, (6, 7, 1)[n // 4], (n % 4) * P:(n % 4 + 1) * P],
                                          q_w[:, 4 * n:4 * n + 4, :].rearrange("p a k -> p (a k)"), ident)
            ins.then_inc(S("f1_wturned"), 1)

            def largest(n):
                pe.wait_ge(S("f1_col"), n + 1)
                nc.tensor.transpose(ps[0:1, 0, 0:P], q_col[:, n:n + 1], ident).then_inc(S("f1_colT"), 1)
                pe.wait_ge(S("f1_top"), n + 1)
                mm(ps[:, 1, 0:1], ones1[:, :], q_top[:, n:n + 1], start=True, stop=True).then_inc(S("f1_topB"), 1)

            pe.wait_ge(S("filled"), 6)
            wait_x(pe, 5)
            pe.wait_ge(S("f1_wT"), 2)
            largest(0)
            pe.wait_ge(S("f1_xq"), 1)
            for k in range(2):
                for c in range(3):
                    for p in range(2):
                        if k:
                            pe.wait_ge(S("f1_up_gate"), 2 * c + p + 1)
                        mm(bank(2 + 2 * c + p), q_wT[:, 3 * (1 - k) + c, :], half(q_x, p), start=True, stop=True).then_inc(S("f1_mm"), 1)
            for n in range(1, 5):
                largest(n)
            for c in range(3):
                pe.wait_ge(S("f1_o"), c + 1)
                for p in range(2):
                    ins = mm(bank(p), q_wT[:, 6 + c, :], q_up[:, c * T + p * HALF:c * T + (p + 1) * HALF], start=(c == 0), stop=(c == 2),
                             skip_group_check=True)
                    if c == 2:
                        ins.then_inc(S("y_ready"), 1)
            residual_norm_tensor(pe, 5)

            narrow_keys_tensor(pe, "x2")
            piece(pe, "l2_wk")
            for p in range(2):
                for k, (name, src) in enumerate((("l2_wk", r_k), ("l2_wv", r_v), ("l2_wr", r_r))):
                    pe.wait_ge(S("l2_mix"), 3 * p + k + 1)
                    mm(bank(2 * k + p), W(name), half(src, p), start=True, stop=True).then_inc(S("l2_mm"), 1)
                waits(pe, "x2")("_k_ready", p + 1)
                pe.wait_ge(S("l2_ek"), p + 1)
                mm(bank(6 + p), W("headsum"), half(r_ek, p), start=True, stop=True).then_inc(S("l2_bsum"), 1)
            pe.wait_ge(S("l2_sig"), 2)
            narrow_values_tensor(pe, "x2", ctxT, 4)
            for p in range(2):
                pe.wait_ge(S("l2_out"), p + 1)
                mm(bank(p), W("l2_wo"), half(r_k, p), start=True, stop=True).then_inc(S("y_ready"), 1)
            waits(pe, "x2")("_v_ready", 1)
            residual_norm_tensor(pe, 6)

            wait_x(pe, 7)
            narrow_tensor(pe, "x2", xT, False, None, W("x2_wo"))
            residual_norm_tensor(pe, 7)

            norm_mean(pe, "rms1")
            piece(pe, "f2_wq")
            narrow_tensor(pe, "f2", f_h, True, caus, W("f2_wo"), "f2_attn")
            norm_mean(pe, "rms2")
            pe.wait_ge(S("f2_h"), 4)
            route_tensor(pe, "m2", m_x2)
            mix_tensor(pe, "m2", M2_CH, M2_ROWS)
            residual_norm_tensor(pe, 8)

            for p in range(2):
                wait_x(pe, 9, 1)
                mm(ps[0:64, 2 + p, :], W("l3_wg"), half(xT, p), start=True, stop=True).then_inc(S("l3_mm"), 1)
                mm(ps[0:64, 4 + p, :], W("l3_wb"), half(xT, p), start=True, stop=True).then_inc(S("l3_mm"), 1)
            for p in range(2):
                pe.wait_ge(S("l3_state"), 4 * p + 4)
                mm(bank(6 + p), W("l3_wc")[0:64, :], half(s_st, p)[0:64, :], start=True, stop=True).then_inc(S("l3_ymm"), 1)

            def inner_ready(p):
                pe.wait_ge(S("l3_h"), p + 1)
            norm_tensor(pe, "inner", s_h, inner_ready)
            for p in range(2):
                pe.wait_ge(S("l3_hn"), p + 1)
                mm(bank(p), W("l3_wout"), half(s_hn, p), start=True, stop=True).then_inc(S("y_ready"), 1)
            residual_norm_tensor(pe, 9)

            pe.wait_ge(S("ctxtm_loaded"), 16)
            for p in range(2):
                wait_x(pe, 10, 1)
                for b in range(HB * p, HB * (p + 1)):
                    ins = mm(ps[:, 6 + p, (b % HB) * P:(b % HB + 1) * P], ctxT[:, b * P:(b + 1) * P], xT[:, b * P:(b + 1) * P],
                             start=True, stop=True, skip_group_check=True)
                ins.then_inc(S("e_up"), 1)
            for p in range(2):
                pe.wait_ge(S("e_act"), p + 1)
                for b in range(HB * p, HB * (p + 1)):
                    ins = mm(ps[:, p, (b % HB) * P:(b % HB + 1) * P], ctx_tm[:, b * P:(b + 1) * P], e_a[:, b * P:(b + 1) * P],
                             start=True, stop=True, skip_group_check=True)
                ins.then_inc(S("y_ready"), 1)
            residual_norm_tensor(pe, 10)

            wait_x(pe, 11)
            for b in range(B):
                ins = mm(ps[:, 2 + b // 3, (b % 3) * NE:(b % 3 + 1) * NE], xT[:, b * P:(b + 1) * P], W("m3_router"),
                         start=True, stop=True, skip_group_check=True)
            ins.then_inc(R("m3", "_logits"), 1)
            for p in range(2):
                mm(ps[0:64, 6 + p, :], W("m3_sgate"), half(xT, p), start=True, stop=True).then_inc(S("m3_shared"), 1)
            for p in range(2):
                pe.wait_ge(S("m3_sact"), p + 1)
                mm(bank(p), W("m3_sdown")[0:64, :], half(t_sh, p)[0:64, :], start=True, stop=False, skip_group_check=True)
            wait = waits(pe, "m3")

            def weights(j, at):
                at += (j % 4) * 2 * P
                return m_wh[:, j // 4, at:at + P], m_wl[:, j // 4, at:at + P]

            def gate(i, j, p, n):
                if j % 4 == 0 and p == 0:
                    wait("_split", 2 * i + j // 4 + 1)
                if not isinstance(n, int) or n >= 2:
                    wait("_hid", n - 1)
                mm3(bank(2 + p), *weights(j, 0), half(m_xh, p), half(m_xl, p), True, True).then_inc(R("m3", "_gate"), 1)

            def spread(i, j, p):
                mm(bank(4 + p), sel160[:, bass.ds((10 * (j % 2) + i) * P, P)], half(t_combT[:, j // 2, :], p),
                   start=True, stop=True).then_inc(R("m3", "_spread"), 1)

            def down(j, p, n, final):
                wait("_hl", n + 1)
                mm3(bank(p), *weights(j, P), m_hh[:, p], m_hl[:, p], False, final).then_inc(S("y_ready") if final else R("m3", "_down"), 1)

            def body(i, final):
                for u in range(2 * CHUNKS):
                    n = 2 * CHUNKS * i + u
                    j, p = (u + 3) // 2, (u + 1) % 2
                    if j < CHUNKS:
                        gate(i, j, p, n + 3)
                        spread(i, j, p)
                    elif not final:
                        gate(i + 1, j - CHUNKS, p, n + 3)
                        spread(i + 1, j - CHUNKS, p)
                    down(u // 2, u % 2, n, final and u >= 2 * CHUNKS - 2)

            wait("_xl", 2)
            pe.wait_ge(S("m3_route"), 3)
            for p in range(2):
                gate(0, 0, p, p)
            for s in range(SETS):
                wait("_parts", 2 * SETS + s + 1)
                for b in range(B):
                    ins = nc.tensor.transpose(bankb(4 + s)[:, b * P:(b + 1) * P], t_parts[:, b, s, :], identb[:, :])
                ins.then_inc(R("m3", "_wturned"), 1)
            for p in range(2):
                wait("_wT", p + 1)
                spread(0, 0, p)
            wait("_wT", SETS)
            gate(0, 1, 0, 2)
            spread(0, 1, 0)
            with pe.Fori(0, GROUPS - 1) as i:
                body(i, False)
            body(GROUPS - 1, True)
            residual_norm_tensor(pe, 11)

        @block.scalar
        def _(act):
            A_ = nc.scalar.activation
            act.wait_ge(S("filled"), 4)
            piece(act, "l0_td")
            A_(d_e, W("l0_td"), ACT.Exp).then_inc(S("l0_e"), 1)
            for p in range(2):
                act.wait_ge(S("l0_mm"), 2 * p + 2)
                A_(bank(4 + p), bank(4 + p), ACT.Sigmoid).then_inc(S("l0_sig"), 1)
            log_tables()
            norm_scalar(act, "ctx", d_bank=6, var_bank=2)
            act.wait_ge(S("norm_out"), 2)
            norm_scalar(act, "0", root=True)

            act.wait_ge(S("x0_mw"), 1)
            A_(x_m.rearrange("p h d -> p (h d)"), ps[:, 6:8, :].rearrange("p a c -> p (a c)"), ACT.Copy,
               scale=P ** -0.5).then_inc(S("x0_m"), 1)
            norm_scalar(act, "lat")
            act.wait_ge(S("x0_mw"), 3)
            A_(x_c, ps[:, 6, 0:XH], ACT.Copy, scale=P ** -0.5).then_inc(S("x0_m"), 1)
            act.wait_ge(S("x0_m"), 2)
            for n in range(0, 2 * XH, 2):
                h, p = n % XH, n // XH
                act.wait_ge(S("x0_qmm"), n + 1)
                A_(half(x_q[:, h, :], p), bank(4 + n % 4), ACT.Identity, bias=x_c[:, h:h + 1]).then_inc(S("x0_q0"), 1)

            def x_exps(v, w, first=False):
                act.wait_ge(S("x0_nm"), w + 1)
                if not first:
                    act.wait_ge(S("x0_turned"), w - 1)
                for i in range(4):
                    A_(x_p[:, v, i, :], ps[:, 2 * v + i // 2, (i % 2) * 256:(i % 2 + 1) * 256], ACT.Exp,
                       bias=x_nm[:, v, i:i + 1], accum_out=x_sum[:, v, i:i + 1]).then_inc(S("x0_p"), 1)

            def x_outputs(b, v, w):
                act.wait_ge(S("x0_weighed"), w + 1)
                A_(x_q[:, 4 * v:4 * v + 4, bass.ds(b * P, P)], bank(6 + v).rearrange("p (h t) -> p h t", h=4),
                   ACT.Copy).then_inc(S("x0_o"), 1)

            def x_body(i, final):
                for k in range(4):
                    w = 4 * i + k
                    act.wait_ge(S("x0_turned"), w + 1)
                    A_(x_pt[:, k % 2, 0, :], bank(4), ACT.Copy).then_inc(S("x0_ptA"), 1)
                    if k > 0:
                        x_outputs(2 * i + (k - 1) // 2, (k - 1) % 2, w - 1)
                    if not (final and k >= 2):
                        x_exps(k % 2, w + 2)
                x_outputs(2 * i + 1, 1, 4 * i + 3)

            for name in ("x0_ptA", "x0_o", "x0_o"):
                credited(act, name)
            x_exps(0, 0, True)
            x_exps(1, 1, True)
            with act.Fori(0, B // 2 - 1) as i:
                x_body(i, False)
            x_body(B // 2 - 1, True)
            norm_scalar(act, "1")

            input_high(act, "m0", xT, lambda p: wait_x(act, 2, p))
            route_scalar(act, "m0")
            mix_scalar(act, "m0", M0_CH, M0_ROWS)
            act.wait_ge(S("l1_norm"), 1)
            A_(g_n2, g_n, ACT.Ln).then_inc(S("l1_log"), 1)
            act.wait_ge(S("l1_log"), 1)
            A_(g_n, g_n2, ACT.Exp, scale=-0.5).then_inc(S("l1_root"), 1)
            norm_scalar(act, "2")

            piece(act, "x1_bk")
            narrow_keys_scalar(act, "x1", W("x1_bk"))
            for p in range(2):
                act.wait_ge(S("l1_mm"), 3 * p + 1)
                A_(half(g_q, p), bank(p), ACT.Copy).then_inc(S("l1_qv"), 1)
                act.wait_ge(S("l1_mm"), 3 * p + 3)
                A_(g_v[:, HB * p:HB * (p + 1), :], bank(4 + p).rearrange("p (b d) -> p b d", b=HB), ACT.Copy).then_inc(S("l1_qv"), 1)
            narrow_spread_scalar(act, "x1", range(13, NH), range(13, NH))
            for p in range(2):
                act.wait_ge(S("l1_z"), p + 1)
                A_(g_z[:, HB * p:HB * (p + 1), :], g_z[:, HB * p:HB * (p + 1), :], ACT.Exp).then_inc(S("l1_e"), 1)
            for p in range(2):
                act.wait_ge(S("l1_turned"), p + 1)
                A_(g_pt[:, HB * p:HB * (p + 1), :], bank(p).rearrange("p (b d) -> p b d", b=HB), ACT.Copy).then_inc(S("l1_pt"), 1)
            narrow_values_scalar(act, "x1", 4)
            for p in range(2):
                act.wait_ge(S("l1_in"), p + 1)
                A_(g_in[:, HB * p:HB * (p + 1)], g_in[:, HB * p:HB * (p + 1)], ACT.Ln).then_inc(S("l1_log"), 1)
                act.wait_ge(S("l1_log"), p + 2)
                A_(g_in[:, HB * p:HB * (p + 1)], g_in[:, HB * p:HB * (p + 1)], ACT.Exp, scale=-0.5).then_inc(S("l1_root"), 1)
            norm_scalar(act, "3")

            piece(act, "x1_bq")
            narrow_scalar(act, "x1", False, W("x1_bv"), SCALE8, W("x1_bq"))
            norm_scalar(act, "4")

            act.wait_ge(S("f1_wturned"), 1)
            A_(q_wT[:, 0:8, :].rearrange("p a k -> p (a k)"), ps[:, 6:8, :].rearrange("p a c -> p (a c)"), ACT.Copy).then_inc(S("f1_wT"), 1)
            A_(q_wT[:, 8, :], ps[:, 1, 0:P], ACT.Copy).then_inc(S("f1_wT"), 1)
            for k, dst in enumerate((q_up, q_gate)):
                for n in range(6):
                    act.wait_ge(S("f1_mm"), 6 * k + n + 1)
                    A_(dst[:, n * HALF:(n + 1) * HALF], bank(2 + n), ACT.Copy).then_inc(S("f1_up_gate"), 1)
            for c in range(3):
                act.wait_ge(S("f1_gq"), c + 2)
                A_(q_sig[:, c * T:(c + 1) * T], q_gate[:, c * T:(c + 1) * T], ACT.Sigmoid).then_inc(S("f1_sig"), 1)
            for m, (scale, bias) in enumerate(((q_i[:, 2:3], round_up), (1.0, round_down))):
                for c in range(3):
                    act.wait_ge(S("f1_up_gate"), 12 + m * (c + 1))
                    A_(q_up[:, c * T:(c + 1) * T], q_up[:, c * T:(c + 1) * T], ACT.Identity, scale=scale, bias=bias).then_inc(S("f1_up_gate"), 1)
            log_tables()
            norm_scalar(act, "5")

            piece(act, "x2_bk")
            narrow_keys_scalar(act, "x2", W("x2_bk"))
            piece(act, "l2_td")
            A_(r_e, W("l2_td"), ACT.Exp).then_inc(S("l2_decay"), 1)
            A_(r_u, W("l2_tf"), ACT.Exp).then_inc(S("l2_decay"), 1)
            act.wait_ge(S("l2_decay"), 2)
            A_(r_dec, r_e, ACT.Exp, scale=-1.0).then_inc(S("l2_decay"), 1)
            for p in range(2):
                act.wait_ge(S("l2_mm"), 3 * p + 1)
                A_(half(r_ek, p), bank(p), ACT.Exp).then_inc(S("l2_ek"), 1)
            for p in range(2):
                act.wait_ge(S("l2_mm"), 3 * p + 3)
                A_(half(r_sig, p), bank(4 + p), ACT.Sigmoid).then_inc(S("l2_sig"), 1)
            log_tables()
            narrow_values_scalar(act, "x2", 4)
            narrow_spread_scalar(act, "x2", range(11, NH), range(11, NH))
            norm_scalar(act, "6")

            piece(act, "x2_bq")
            narrow_scalar(act, "x2", False, W("x2_bv"), SCALE8, W("x2_bq"))
            norm_scalar(act, "7")

            wait_x(act, 8)
            norm_scalar(act, "rms1", eps6, xT)
            narrow_spread_scalar(act, "f2", range(3, 11), ())
            narrow_values_scalar(act, "f2", 6)
            narrow_spread_scalar(act, "f2", (), range(5, 10))
            narrow_scalar(act, "f2", True, None, SCALE8, meanwhile=lambda: narrow_spread_scalar(act, "f2", (), range(10, 12)))
            act.wait_ge(S("f2_x2"), 2)
            norm_scalar(act, "rms2", eps6, f_x2)
            input_high(act, "m2", m_x2, lambda p: act.wait_ge(S("f2_h"), p + 3))
            route_scalar(act, "m2")
            mix_scalar(act, "m2", M2_CH, M2_ROWS)
            norm_scalar(act, "8")

            A_(s_a, W("l3_alog"), ACT.Exp).then_inc(S("l3_a"), 1)
            for p in range(2):
                act.wait_ge(S("l3_mm"), 2 * p + 1)
                A_(half(s_sig, p)[0:64, :], ps[0:64, 2 + p, :], ACT.Sigmoid, bias=W("l3_bg")[0:64, :]).then_inc(S("l3_sig"), 1)
            log_tables()
            norm_scalar(act, "inner")
            norm_scalar(act, "9")

            for p in range(2):
                act.wait_ge(S("e_up"), p + 1)
                A_(half(e_a, p), bank(6 + p), ACT.Gelu_apprx_tanh).then_inc(S("e_act"), 1)
            log_tables()
            norm_scalar(act, "10")

            input_high(act, "m3", xT, lambda p: wait_x(act, 11, p))
            for k in range(3):
                act.wait_ge(S("m3_route"), k + 1)
                A_(t_p[:, 3 * k:min(3 * k + 3, B), :], t_p[:, 3 * k:min(3 * k + 3, B), :], ACT.Sigmoid).then_inc(S("m3_prob"), 1)
            for p in range(2):
                act.wait_ge(S("m3_shared"), p + 1)
                A_(half(t_sh, p)[0:64, :], ps[0:64, 6 + p, :], ACT.Silu).then_inc(S("m3_sact"), 1)

            act.wait_ge(S("m3_route"), 4)
            for b in range(HB):
                A_(t_scaled[:, b, :], t_p[:, b, :], ACT.Copy, scale=t_s[:, b:b + 1]).then_inc(S("m3_prob"), 1)
            waits(act, "m3")("_pad", 1)
            for k in range(3):
                for s in range(SETS):
                    act.wait_ge(S("m3_route"), 4 + SETS * k + s + 1)
                    A_(t_parts[:, :, s, k:3 * SETE:3], t_w[:, :, s * SETE:(s + 1) * SETE], ACT.Copy).then_inc(R("m3", "_parts"), 1)

            def m3_silu(n, p):
                waits(act, "m3")("_gate", n + 1)
                A_(t_sg[:, p], bank(2 + p), ACT.Silu).then_inc(R("m3", "_silu"), 1)

            def m3_high(n, p):
                if not isinstance(n, int) or n >= 2:
                    waits(act, "m3")("_down", n - 1)
                hidden_high(act, "m3", n, p, P, 6 + p)

            for p in range(2):
                m3_silu(p, p)
            for p in range(2):
                m3_high(p, p)
                m3_silu(p + 2, p)
            with act.Fori(1, GROUPS * CHUNKS - 1) as i:
                for p in range(2):
                    m3_high(2 * i + p, p)
                    m3_silu(2 * i + p + 2, p)
            for p in range(2):
                m3_high(2 * (GROUPS * CHUNKS - 1) + p, p)
            log_tables()
            norm_scalar(act, "11")

        @block.vector
        def _(dve):
            V = nc.vector
            link = linked(dve, "dve_step")

            def affine_norm(tag, s, g, b, d_bank=2):
                for p in range(2):
                    dst = x_kv[:, HB * p:HB * (p + 1), s, :]
                    dve.wait_ge(S("norm_rstd"), nth(tag, p))
                    link(V.tensor_tensor(dst, bank(d_bank + p).rearrange("p (b t) -> p b t", b=HB),
                                         half(rstd, p).rearrange("p (b t) -> p b t", b=HB), ALU.mult))
                    V.tensor_scalar(dst, dst, W(g), W(b), ALU.mult, ALU.add).then_inc(S("norm_out"), 1)

            dve.wait_ge(S("l0_e"), 1)
            link(V.tensor_scalar(d_w, d_e, -1.0, None, ALU.mult))
            for p in range(2):
                dve.wait_ge(S("l0_mm"), 2 * p + 1)
                for b in range(HB * p, HB * (p + 1)):
                    ins = V.tensor_tensor_scan(d_s[:, b * P:(b + 1) * P], d_w.to_broadcast([P, P]),
                                               ps[:, 2 + p, (b % HB) * P:(b % HB + 1) * P], 0.0, ALU.mult, ALU.add)
                    link(ins)
                dve.wait_ge(S("l0_sig"), p + 1)
                V.tensor_tensor(half(d_s, p), half(d_s, p), bank(4 + p), ALU.mult).then_inc(S("l0_gated"), 1)
            piece(dve, "x0_gm")
            residual_norm_vector(dve, 0, meanwhile=lambda: affine_norm("ctx", 0, "x0_gm", "x0_bm", d_bank=6))

            dve.wait_ge(S("x0_mw"), 2)
            V.tensor_copy(x_u.rearrange("p h d -> p (h d)"), ps[:, 0:2, :].rearrange("p a c -> p (a c)")).then_inc(S("x0_u"), 1)
            affine_norm("lat", 1, "x0_gl", "x0_bl")
            dve.wait_ge(S("x0_mw"), 3)
            V.tensor_tensor(x_bo, ps[:, 7, 0:1], W("x0_bo"), ALU.add).then_inc(S("x0_u"), 1)
            for n in range(4):
                dve.wait_ge(S("x0_kvt"), 2 * n + 2)
                V.tensor_copy(x_kvt[:, 2 * n:2 * n + 2].rearrange("p b s d -> p (b s d)"), bank(n)).then_inc(S("x0_kvt_sb"), 1)

            dve.wait_ge(S("x0_m"), 2)
            for n in range(1, 2 * XH, 2):
                h, p = n % XH, n // XH
                dve.wait_ge(S("x0_qmm"), n + 1)
                V.tensor_scalar(half(x_q[:, h, :], p), bank(4 + n % 4), x_c[:, h:h + 1], None, ALU.add).then_inc(S("x0_q1"), 1)

            def x_maxima(v, w):
                dve.wait_ge(S("x0_scores"), w + 1)
                V.tensor_reduce(x_nm[:, v], ps[:, 2 * v:2 * v + 2, :].rearrange("p a (h k) -> p (a h) k", h=2), AX.X, ALU.max,
                                negate=True).then_inc(S("x0_nm"), 1)

            def x_normalise(v, w):
                dve.wait_ge(S("x0_p"), 4 * (w + 1))
                V.reciprocal(x_rec[:, v], x_sum[:, v]).then_inc(S("x0_rec"), 1)
                dve.wait_ge(S("x0_rec"), w + 1)
                for i in range(4):
                    V.tensor_scalar(x_p[:, v, i, :], x_p[:, v, i, :], x_rec[:, v, i:i + 1], None, ALU.mult).then_inc(S("x0_pn"), 1)

            def x_body(i, final):
                for k in range(4):
                    w = 4 * i + k
                    dve.wait_ge(S("x0_turned"), w + 1)
                    V.tensor_copy(x_pt[:, k % 2, 1, :], bank(5)).then_inc(S("x0_ptB"), 1)
                    if not (final and k == 3):
                        x_normalise((k + 1) % 2, w + 1)
                    if not (final and k >= 2):
                        x_maxima(k % 2, w + 2)

            credited(dve, "x0_ptB")
            x_maxima(0, 0)
            x_maxima(1, 1)
            x_normalise(0, 0)
            with dve.Fori(0, B // 2 - 1) as i:
                x_body(i, False)
            x_body(B // 2 - 1, True)
            residual_norm_vector(dve, 1, x_bo)

            route_vector(dve, "m0", 1e-6, link)
            mix_vector(dve, "m0", xT, M0_CH, M0_ROWS)
            def rotations():
                link(V.tensor_tensor(g_n, W("l1_rc"), W("l1_rc"), ALU.mult))
                link(V.tensor_tensor(g_n2, W("l1_rs"), W("l1_rs"), ALU.mult))
                V.tensor_tensor(g_n, g_n, g_n2, ALU.add).then_inc(S("l1_norm"), 1)
                link(V.reciprocal(g_a, W("l1_scale")))
                link(V.tensor_scalar(g_a, g_a, 2.0, None, ALU.mult))
                link(V.tensor_tensor(g_b, g_a, W("l1_bias"), ALU.add))
                dve.wait_ge(S("l1_root"), 1)
                link(V.tensor_tensor(g_c, W("l1_rc"), g_n, ALU.mult))
                link(V.tensor_tensor(g_s, W("l1_rs"), g_n, ALU.mult))
                for k in range(3):
                    link(V.tensor_scalar(g_t[:, k], W("swap"), g_s[:, k:k + 1], None, ALU.mult))
                    ins = V.scalar_tensor_tensor(out=g_rot[:, k], in0=ident, scalar=g_c[:, k:k + 1], in1=g_t[:, k], op0=ALU.mult, op1=ALU.add)
                ins.then_inc(S("l1_rot"), 1)

            residual_norm_vector(dve, 2, meanwhile=rotations)

            for p in range(2):
                dve.wait_ge(S("l1_mm"), 3 * p + 2)
                V.tensor_copy(half(g_k, p), bank(2 + p)).then_inc(S("l1_k"), 1)
            for p in range(2):
                z = g_z[:, HB * p:HB * (p + 1), :]
                mx = g_mx[:, HB * p:HB * (p + 1)]
                dve.wait_ge(S("l1_scores"), p + 1)
                link(V.tensor_scalar(z, bank(6 + p).rearrange("p (b k) -> p b k", b=HB), g_a, g_b, ALU.mult, ALU.add))
                link(V.tensor_reduce(mx, z, AX.X, ALU.max))
                V.tensor_tensor(z, z, mx.unsqueeze(2).to_broadcast([P, HB, P]), ALU.subtract).then_inc(S("l1_z"), 1)
            for p in range(2):
                dve.wait_ge(S("l1_e"), p + 1)
                link(V.tensor_reduce(g_sm[:, HB * p:HB * (p + 1)], g_z[:, HB * p:HB * (p + 1), :], AX.X, ALU.add))
                link(V.reciprocal(g_rc[:, HB * p:HB * (p + 1)], g_sm[:, HB * p:HB * (p + 1)]))
            for p in range(2):
                av = g_av[:, HB * p:HB * (p + 1), :]
                s2 = g_sq[:, HB * p:HB * (p + 1), :]
                dve.wait_ge(S("l1_weighed"), p + 1)
                link(V.tensor_tensor(av, bank(2 + p).rearrange("p (b d) -> p b d", b=HB),
                                     g_rc[:, HB * p:HB * (p + 1)].unsqueeze(2).to_broadcast([P, HB, P]), ALU.mult))
                link(V.tensor_tensor(s2, av, av, ALU.mult))
                link(V.tensor_reduce(g_in[:, HB * p:HB * (p + 1)], s2, AX.X, ALU.add))
                V.tensor_scalar(g_in[:, HB * p:HB * (p + 1)], g_in[:, HB * p:HB * (p + 1)], 1e-8, None, ALU.max).then_inc(S("l1_in"), 1)
            for p in range(2):
                av = g_av[:, HB * p:HB * (p + 1), :]
                dve.wait_ge(S("l1_root"), p + 2)
                V.tensor_tensor(av, av, g_in[:, HB * p:HB * (p + 1)].unsqueeze(2).to_broadcast([P, HB, P]), ALU.mult).then_inc(S("l1_out"), 1)
            dve.wait_ge(S("mask_loaded"), 16)
            V.tensor_scalar(maskb[:, :], mask8[:, :], NEG, None, ALU.mult).then_inc(S("maskb"), 1)
            residual_norm_vector(dve, 3)

            def four_bits():
                at = PACK_AT["f1_gate"][0]
                wts = pack[:, at:at + 9 * P].rearrange("p (a k) -> p a k", k=32)
                link(V.tensor_reduce(q_ab, wts, AX.X, ALU.max, apply_absolute_value=True))
                link(V.tensor_scalar(q_sc, q_ab, 1.0 / 7.0, 1e-12, ALU.mult, ALU.max))
                link(V.reciprocal(q_inv, q_sc))
                link(V.tensor_tensor(q_w, wts, q_inv.unsqueeze(2).to_broadcast([P, 36, 32]), ALU.mult))
                link(V.tensor_scalar(q_w, q_w, ROUND, ROUND, ALU.add, ALU.subtract))
                V.tensor_tensor(q_w, q_w, q_sc.unsqueeze(2).to_broadcast([P, 36, 32]), ALU.mult).then_inc(S("f1_wq"), 1)

            narrow_vector(dve, "x1", four_bits)
            residual_norm_vector(dve, 4, W("x1_bo"))

            wait_x(dve, 5)

            def over_partitions(n):
                dve.wait_ge(S("f1_colT"), n + 1)
                V.tensor_reduce(q_top[:, n:n + 1], ps[0:1, 0, 0:P], AX.X, ALU.max).then_inc(S("f1_top"), 1)
                dve.wait_ge(S("f1_topB"), n + 1)

            def quantum(n):
                over_partitions(n)
                link(V.tensor_scalar(q_s[:, n:n + 1], ps[:, 1, 0:1], 1.0 / QMAX, 1e-12, ALU.mult, ALU.max))
                link(V.reciprocal(q_i[:, n:n + 1], q_s[:, n:n + 1]))

            def largest(n, src):
                return V.tensor_reduce(q_col[:, n:n + 1], src, AX.X, ALU.max, apply_absolute_value=True)

            def steps(n, src):
                link(V.tensor_scalar(src, src, q_i[:, n:n + 1], ROUND, ALU.mult, ALU.add))

            def from_steps(n, dst, src):
                return V.tensor_scalar(dst, src, ROUND, q_s[:, n:n + 1], ALU.subtract, ALU.mult)

            largest(0, xT[:, :]).then_inc(S("f1_col"), 1)
            quantum(0)
            link(V.tensor_scalar(q_x, xT[:, :], q_i[:, 0:1], ROUND, ALU.mult, ALU.add))
            from_steps(0, q_x, q_x).then_inc(S("f1_xq"), 1)
            for k, buf in enumerate((q_up, q_gate)):
                for n in range(6):
                    dve.wait_ge(S("f1_up_gate"), 6 * k + n + 1)
                    ins = V.tensor_reduce(q_part[:, k, n:n + 1], buf[:, n * HALF:(n + 1) * HALF], AX.X, ALU.max, apply_absolute_value=True)
                link(ins)
            largest(1, q_part[:, 1, :]).then_inc(S("f1_col"), 1)
            largest(2, q_part[:, 0, :]).then_inc(S("f1_col"), 1)
            quantum(1)
            steps(1, q_gate)
            over_partitions(2)
            link(V.tensor_scalar(q_s[:, 2:3], ps[:, 1, 0:1], 1.0 / QMAX, 1e-12, ALU.mult, ALU.max))
            V.reciprocal(q_i[:, 2:3], q_s[:, 2:3]).then_inc(S("f1_gq"), 1)
            third = lambda buf, c: buf[:, c * T:(c + 1) * T]
            for c in range(3):
                from_steps(1, third(q_gate, c), third(q_gate, c)).then_inc(S("f1_gq"), 1)
            for c in range(3):
                dve.wait_ge(S("f1_sig"), c + 1)
                link(V.tensor_scalar(third(q_sig, c), third(q_sig, c), 65535.0 / 65536.0, 192.0, ALU.min, ALU.add))
                link(V.scalar_tensor_tensor(out=third(q_gate, c), in0=third(q_sig, c), scalar=192.0, in1=third(q_gate, c),
                                            op0=ALU.subtract, op1=ALU.mult))
            largest(3, q_gate).then_inc(S("f1_col"), 1)
            quantum(3)
            steps(3, q_gate)
            dve.wait_ge(S("f1_up_gate"), 18)
            link(V.scalar_tensor_tensor(out=q_up, in0=q_gate, scalar=ROUND, in1=q_up, op0=ALU.subtract, op1=ALU.mult))
            largest(4, q_up).then_inc(S("f1_col"), 1)
            over_partitions(4)
            link(V.tensor_tensor(q_s[:, 3:4], q_s[:, 3:4], q_s[:, 2:3], ALU.mult))
            link(V.tensor_scalar(q_s[:, 4:5], ps[:, 1, 0:1], q_s[:, 3:4], 1.0 / QMAX, ALU.mult, ALU.mult))
            link(V.tensor_scalar(q_s[:, 4:5], q_s[:, 4:5], 1e-12, None, ALU.max))
            link(V.reciprocal(q_i[:, 4:5], q_s[:, 4:5]))
            link(V.tensor_tensor(q_i[:, 4:5], q_i[:, 4:5], q_s[:, 3:4], ALU.mult))
            steps(4, q_up)
            for c in range(3):
                from_steps(4, third(q_up, c), third(q_up, c)).then_inc(S("f1_o"), 1)
            residual_norm_vector(dve, 5)

            piece(dve, "l2_mk")
            for p in range(2):
                dve.wait_ge(S("l2_prev"), p + 1)
                prev = r_prev[:, HB * p:HB * (p + 1), :].rearrange("p b t -> p (b t)")
                link(V.tensor_tensor(half(r_diff, p), half(xT, p), prev, ALU.subtract))
                for name, dst in (("l2_mk", r_k), ("l2_mv", r_v), ("l2_mr", r_r)):
                    V.scalar_tensor_tensor(out=half(dst, p), in0=half(r_diff, p), scalar=W(name), in1=prev,
                                           op0=ALU.mult, op1=ALU.add).then_inc(S("l2_mix"), 1)
            dve.wait_ge(S("l2_decay"), 3)
            dve.wait_ge(S("l2_zero"), 3)
            for p in range(2):
                seqs = range(HB * p, HB * (p + 1))
                dve.wait_ge(S("l2_ek"), p + 1)
                dve.wait_ge(S("l2_mm"), 3 * p + 2)
                link(V.tensor_tensor(half(r_ekv, p), half(r_ek, p), bank(2 + p), ALU.mult))
                dve.wait_ge(S("l2_bsum"), p + 1)
                for b in seqs:
                    ins = V.tensor_tensor_scan(r_sa[:, b, 1:P + 1], r_dec.to_broadcast([P, P]), r_ekv[:, b * P:(b + 1) * P],
                                               0.0, ALU.mult, ALU.add)
                    ins = V.tensor_tensor_scan(r_sb[:, b, 1:P + 1], r_dec.to_broadcast([P, P]),
                                               ps[:, 6 + p, (b % HB) * P:(b % HB + 1) * P], 0.0, ALU.mult, ALU.add)
                link(ins)
                ha = r_sa[:, HB * p:HB * (p + 1), 0:P]
                hb = r_sb[:, HB * p:HB * (p + 1), 0:P]
                den = half(r_den, p).rearrange("p (b t) -> p b t", b=HB)
                num = half(r_ekv, p).rearrange("p (b t) -> p b t", b=HB)
                link(V.scalar_tensor_tensor(out=num, in0=num, scalar=r_u, in1=ha, op0=ALU.mult, op1=ALU.add))
                link(V.scalar_tensor_tensor(out=den, in0=bank(6 + p).rearrange("p (b t) -> p b t", b=HB), scalar=r_u, in1=hb,
                                            op0=ALU.mult, op1=ALU.add))
                link(V.tensor_scalar(half(r_den, p), half(r_den, p), 1e-6, None, ALU.max))
                link(V.reciprocal(half(r_den, p), half(r_den, p)))
                link(V.tensor_tensor(half(r_den, p), half(r_den, p), half(r_ekv, p), ALU.mult))
                dve.wait_ge(S("l2_sig"), p + 1)
                V.tensor_tensor(half(r_k, p), half(r_den, p), half(r_sig, p), ALU.mult).then_inc(S("l2_out"), 1)
            residual_norm_vector(dve, 6)

            narrow_vector(dve, "x2")
            residual_norm_vector(dve, 7, W("x2_bo"))

            piece(dve, "f2_ln1")
            for p in range(2):
                dve.wait_ge(S("norm_rstd"), nth("rms1", p))
                V.scalar_tensor_tensor(out=half(f_h, p), in0=half(xT, p), scalar=W("f2_ln1"), in1=half(rstd, p),
                                       op0=ALU.mult, op1=ALU.mult).then_inc(S("f2_h"), 1)
            narrow_rope_vector(dve, "f2")
            narrow_spread_vector(dve, "f2", range(0, 3), range(0, 5))
            narrow_vector(dve, "f2")
            for p in range(2):
                dve.wait_ge(S("f2_attn"), p + 1)
                V.tensor_tensor(half(f_x2, p), bank(p), half(xT, p), ALU.add).then_inc(S("f2_x2"), 1)
            dve.wait_ge(S("f2_x2"), 2)
            link(V.tensor_tensor(f_res, f_x2, xT[:, :], ALU.add))
            for p in range(2):
                dve.wait_ge(S("norm_rstd"), nth("rms2", p))
                V.scalar_tensor_tensor(out=half(m_x2, p), in0=half(f_x2, p), scalar=W("f2_ln2"), in1=half(rstd, p),
                                       op0=ALU.mult, op1=ALU.mult).then_inc(S("f2_h"), 1)
            route_vector(dve, "m2", 0.0, link)
            mix_vector(dve, "m2", m_x2, M2_CH, M2_ROWS)
            residual_norm_vector(dve, 8, None, f_res)

            dve.wait_ge(S("l3_a"), 1)
            for p in range(2):
                dve.wait_ge(S("l3_sig"), p + 1)
                dve.wait_ge(S("l3_mm"), 2 * p + 2)
                link(V.tensor_tensor(half(s_u, p)[0:64, :], half(s_sig, p)[0:64, :], ps[0:64, 4 + p, :], ALU.mult))
                for b in range(HB * p, HB * (p + 1)):
                    V.tensor_tensor_scan(s_st[0:64, b * P:(b + 1) * P], s_a[0:64, :].to_broadcast([64, P]),
                                         s_u[0:64, b * P:(b + 1) * P], 0.0, ALU.mult, ALU.add).then_inc(S("l3_state"), 1)
            for p in range(2):
                dve.wait_ge(S("l3_ymm"), p + 1)
                link(V.scalar_tensor_tensor(out=half(s_h, p), in0=half(xT, p), scalar=W("l3_d"), in1=bank(6 + p),
                                            op0=ALU.mult, op1=ALU.add))
                V.tensor_tensor(half(s_h, p), half(s_h, p), half(xT, p), ALU.add).then_inc(S("l3_h"), 1)
            for p in range(2):
                dve.wait_ge(S("norm_rstd"), nth("inner", p))
                link(V.tensor_tensor(half(s_hn, p), bank(2 + p), half(rstd, p), ALU.mult))
                V.tensor_scalar(half(s_hn, p), half(s_hn, p), W("l3_gamma"), W("l3_beta"), ALU.mult, ALU.add).then_inc(S("l3_hn"), 1)
            residual_norm_vector(dve, 9, W("l3_bout"))

            residual_norm_vector(dve, 10)

            input_low(dve, V, "m3", xT)
            waits(dve, "m3")("_logits", 1)
            for k in range(3):
                b0, b1 = 3 * k, min(3 * k + 3, B)
                V.tensor_tensor(t_p[:, b0:b1, :], ps[:, 2 + k, 0:(b1 - b0) * NE].rearrange("p (b e) -> p b e", e=NE),
                                W("m3_bias").unsqueeze(1).to_broadcast([P, b1 - b0, NE]), ALU.add).then_inc(S("m3_route"), 1)
            for b in range(B):
                dve.wait_ge(S("m3_prob"), b // 3 + 1)
                ins = V.max(t_top[:, b, :], t_p[:, b, :])
            link(ins)
            link(V.tensor_reduce(t_s, t_top, AX.X, ALU.add))
            link(V.tensor_scalar(t_s, t_s, 1e-9, None, ALU.add))
            link(V.reciprocal(t_s, t_s))
            V.tensor_scalar(t_s, t_s, 2.5, None, ALU.mult).then_inc(S("m3_route"), 1)
            for b in range(B):
                ins = V.match_replace(t_rep[:, b, :], t_top[:, b, :], t_p[:, b, :], -1.0)
            link(ins)
            dve.wait_ge(S("m3_prob"), 3 + HB + 1)
            sets = [slice(s * SETE, (s + 1) * SETE) for s in range(SETS)]
            for s in range(SETS):
                V.scalar_tensor_tensor(out=t_w[:, :, sets[s]], in0=t_rep[:, :, sets[s]], scalar=-1.0, in1=t_scaled[:, :, sets[s]],
                                       op0=ALU.is_equal, op1=ALU.mult).then_inc(S("m3_route"), 1)
            for k in range(2):
                for s in range(SETS):
                    waits(dve, "m3")("_parts", SETS * k + s + 1)
                    V.tensor_tensor(t_w[:, :, sets[s]], t_w[:, :, sets[s]], t_parts[:, :, s, k:3 * SETE:3],
                                    ALU.subtract).then_inc(S("m3_route"), 1)
            for s in range(SETS):
                waits(dve, "m3")("_wturned", s + 1)
                V.tensor_copy(t_combT[:, s, :], bankb(4 + s)).then_inc(R("m3", "_wT"), 1)

            def m3_hidden(n, p):
                if not isinstance(n, int) or n >= 2:
                    waits(dve, "m3")("_hl", n - 1)
                waits(dve, "m3")("_silu", n + 1)
                waits(dve, "m3")("_spread", n + 1)
                V.tensor_tensor(bank(6 + p), t_sg[:, p], bank(4 + p), ALU.mult).then_inc(R("m3", "_hid"), 1)

            waits(dve, "m3")("_wT", SETS)
            m3_hidden(0, 0)
            m3_hidden(1, 1)
            hidden_low(dve, "m3", 0, 0, P, 6)
            m3_hidden(2, 0)
            hidden_low(dve, "m3", 1, 1, P, 7)
            with dve.Fori(1, GROUPS * CHUNKS - 1) as i:
                for p in range(2):
                    m3_hidden(2 * i + p + 1, 1 - p)
                    hidden_low(dve, "m3", 2 * i + p, p, P, 6 + p)
            m3_hidden(2 * GROUPS * CHUNKS - 1, 1)
            for p in range(2):
                hidden_low(dve, "m3", 2 * (GROUPS * CHUNKS - 1) + p, p, P, 6 + p)
            residual_norm_vector(dve, 11)

        @block.gpsimd
        def _(pool):
            G = nc.gpsimd
            G.memset(eps5, EPS).then_inc(S("filled"), 1)
            G.memset(eps6, 1e-6).then_inc(S("filled"), 1)
            G.memset(round_up, ROUND).then_inc(S("filled"), 1)
            G.memset(round_down, -ROUND).then_inc(S("filled"), 1)
            G.memset(ones1[:, :], 1.0).then_inc(S("filled"), 1)
            G.memset(zeros[:, :], 0.0).then_inc(S("filled"), 1)
            def x_queries(b, slot):
                G.tensor_copy(x_qs[:, slot], x_q[:, :, bass.ds(b * P, P)]).then_inc(S("x0_qs"), 1)

            def x_keys_values(b, slot):
                G.tensor_copy(x_kvts[:, slot], x_kvt[:, bass.ds(b, 1), :, :].rearrange("p o s d -> p (o s) d")).then_inc(S("x0_kvts"), 1)

            pool.wait_ge(S("x0_kvt_sb"), 4)
            for slot in range(2):
                x_keys_values(slot, slot)
            for k in range(2):
                pool.wait_ge(S(f"x0_q{k}"), XH // 2)
            for slot in range(2):
                x_queries(slot, slot)
            for k in range(2):
                pool.wait_ge(S(f"x0_q{k}"), XH)
            with pool.Fori(1, B // 2) as i:
                for slot in range(2):
                    pool.wait_ge(S("x0_scores"), 4 * i + 2 * slot - 2)
                    x_queries(2 * i + slot, slot)
                    pool.wait_ge(S("x0_weighed"), 4 * i + 2 * slot - 2)
                    x_keys_values(2 * i + slot, slot)

            def padding(t, ready):
                ready()
                G.memset(m_parts[:, :, :], 0.0).then_inc(R(t, "_pad"), 1)

            padding("m0", lambda: wait_x(pool, 2))
            mix_gpsimd(pool, "m0", xT, M0_CH, M0_ROWS)
            pool.wait_ge(S("y_ready"), 6)
            narrow_ones(pool, "x1")
            narrow_spread_gpsimd(pool, "x1", range(0, 13), range(0, 13))
            narrow_gpsimd(pool, "x1", False)
            wait_x(pool, 6)
            G.memset(r_sa[:, :, 0], 0.0).then_inc(S("l2_zero"), 1)
            G.memset(r_sb[:, :, 0], 0.0).then_inc(S("l2_zero"), 1)
            G.memset(r_prev[:, :, 0], 0.0).then_inc(S("l2_zero"), 1)
            pool.wait_ge(S("l2_zero"), 3)
            for p in range(2):
                G.tensor_copy(r_prev[:, HB * p:HB * (p + 1), 1:P],
                              half(xT, p).rearrange("p (b t) -> p b t", b=HB)[:, :, 0:P - 1]).then_inc(S("l2_prev"), 1)
            narrow_ones(pool, "x2")
            narrow_spread_gpsimd(pool, "x2", range(0, 11), range(0, 11))
            narrow_gpsimd(pool, "x2", False)
            wait_x(pool, 8)
            narrow_ones(pool, "f2")
            narrow_gpsimd(pool, "f2", True, range(11, NH), range(12, NH))
            padding("m2", lambda: pool.wait_ge(S("f2_x2"), 2))
            mix_gpsimd(pool, "m2", m_x2, M2_CH, M2_ROWS)
            def m3_split(n, slot):
                waits(pool, "m3")(f"_load{slot}", 8 * (n - slot) + 16)
                split_weights(pool, "m3", slot, [(P, slice(0, 1024))], n)

            wait_x(pool, 9)
            m3_split(0, 0)
            m3_split(1, 1)
            wait_x(pool, 11)
            G.memset(t_parts[:, :, :, :], 0.0).then_inc(R("m3", "_pad"), 1)
            pool.wait_ge(S("m3_route"), 4)
            G.tensor_tensor(t_scaled[:, HB:B, :], t_p[:, HB:B, :], t_s[:, HB:B].unsqueeze(2).to_broadcast([P, HB, NE]),
                            ALU.mult).then_inc(S("m3_prob"), 1)
            with pool.Fori(1, GROUPS) as i:
                for slot in range(2):
                    waits(pool, "m3")("_down", 16 * i + 8 * slot - 8)
                    m3_split(2 * i + slot, slot)


def _pack(i):
    import numpy as np
    f = np.float32

    def rows(w):
        out = np.zeros((P, w.shape[1]), f)
        out[0:w.shape[0]] = w
        return out

    def col(v):
        return rows(v.reshape(-1, 1))

    def doubled(w):
        return np.repeat(w.reshape(P, 8, HD), 2, axis=1).reshape(P, P)

    def swapped(w):
        return w.reshape(P, NH, 2, HD // 2)[:, :, ::-1, :].reshape(P, P)

    by_head = lambda w: w.reshape(P, XH, P)
    turned = lambda w: by_head(w).transpose(2, 1, 0).reshape(P, XH * P)
    n = np.arange(P)
    swap = np.zeros((P, P), f)
    swap[n[0::2], n[1::2]] = 1
    swap[n[1::2], n[0::2]] = -1
    inv_freq = (1.0 / np.power(f(10000.0), np.arange(0, HD, 2, dtype=f) / f(HD), dtype=f)).astype(f)
    ang = np.arange(P, dtype=f)[:, None] * inv_freq[None, :]
    cos = np.tile(np.concatenate([np.cos(ang), np.cos(ang)], 1).T, (NH, 1))
    sin = np.tile(np.concatenate([-np.sin(ang), np.sin(ang)], 1).T, (NH, 1))
    kv = i["L0_xattn_Wkv"]
    rot = i["L1_attn_rot_w"].reshape(3, P // 2, 2)
    natural = lambda w: w.reshape(3, P, P).transpose(1, 0, 2).reshape(P, 3 * P)
    wk2, wv2 = doubled(i["L2_ffn_wk"]), doubled(i["L2_ffn_wv"])
    parts = {
        "center": np.eye(P, dtype=f) - f(1 / P), "mean": np.full((P, P), 1 / P, f), "ident": np.eye(P, dtype=f),
        "l0_wk": i["L0_attn_Wk"].T, "l0_wr": i["L0_attn_Wr"].T, "l0_wv": i["L0_attn_Wv"].T, "l0_td": col(i["L0_attn_time_decay"]),
        "x0_wq": turned(i["L0_xattn_Wq"]), "x0_wk": turned(kv[:, :XH * P]), "x0_wv": turned(kv[:, XH * P:]),
        "x0_wo": i["L0_xattn_Wo"].reshape(XH, P, P).transpose(1, 0, 2).reshape(P, XH * P),
        "x0_bq": i["L0_xattn_bq"].reshape(XH, P).T, "x0_bv": i["L0_xattn_bkv"][XH * P:].reshape(XH, P).T,
        "x0_bo": col(i["L0_xattn_bo"]), "x0_gm": col(i["L0_xattn_gamma_media"]), "x0_bm": col(i["L0_xattn_beta_media"]),
        "x0_gl": col(i["L0_xattn_gamma_lat"]), "x0_bl": col(i["L0_xattn_beta_lat"]),
        "m0_router": i["L0_ffn_router_w"].T,
        "l1_rc": np.repeat(rot[:, :, 0], 2, axis=1).T, "l1_rs": np.repeat(rot[:, :, 1], 2, axis=1).T,
        "l1_scale": np.broadcast_to(i["L1_attn_scale"].reshape(1, 1), (P, 1)),
        "l1_bias": np.broadcast_to(i["L1_attn_bias"].reshape(1, 1), (P, 1)), "swap": swap,
        "headmask": (n[:, None] // HD == n[None, 0:NH]).astype(f),
        "x1_wq": i["L1_xattn_Wq"], "x1_wk": i["L1_xattn_Wk"], "x1_wv": i["L1_xattn_Wv"], "x1_wo": i["L1_xattn_Wo"],
        "x1_bq": col(i["L1_xattn_bq"]), "x1_bk": col(i["L1_xattn_bk"]), "x1_bv": col(i["L1_xattn_bv"]), "x1_bo": col(i["L1_xattn_bo"]),
        "f1_gate": natural(i["L1_ffn_w_gate"]), "f1_up": natural(i["L1_ffn_w_up"]), "f1_down": i["L1_ffn_w_down"],
        "l2_mk": col(i["L2_attn_mix_k"]), "l2_mv": col(i["L2_attn_mix_v"]), "l2_mr": col(i["L2_attn_mix_r"]),
        "l2_td": col(np.repeat(i["L2_attn_time_decay"], HD)), "l2_tf": col(np.repeat(i["L2_attn_time_first"], HD)),
        "l2_wk": i["L2_attn_W_key"].T, "l2_wv": i["L2_attn_W_value"].T, "l2_wr": i["L2_attn_W_receptance"].T, "l2_wo": i["L2_attn_W_output"].T,
        "headsum": (n[:, None] // HD == n[None, :] // HD).astype(f),
        "x2_wq": i["L2_xattn_wq"].T, "x2_wk": i["L2_xattn_wk"].T, "x2_wv": i["L2_xattn_wv"].T, "x2_wo": i["L2_xattn_wo"].T,
        "x2_bq": col(i["L2_xattn_bq"]), "x2_bk": col(i["L2_xattn_bk"]), "x2_bv": col(i["L2_xattn_bv"]), "x2_bo": col(i["L2_xattn_bo"]),
        "f2_ln1": col(i["L2_ffn_ln1_w"]), "f2_ln2": col(i["L2_ffn_ln2_w"]),
        "f2_wq": i["L2_ffn_wq"], "f2_wqr": swapped(i["L2_ffn_wq"]),
        "f2_wk": wk2, "f2_wkr": swapped(wk2), "f2_wv": wv2, "f2_wo": i["L2_ffn_wo"],
        "m2_router": i["L2_ffn_router_w"], "cos": cos, "sin": sin,
        "l3_alog": col(i["L3_attn_A_log"]), "l3_bg": col(i["L3_attn_bg"]), "l3_d": col(i["L3_attn_D"]), "l3_bout": col(i["L3_attn_bout"]),
        "l3_gamma": col(i["L3_attn_gamma"]), "l3_beta": col(i["L3_attn_beta"]),
        "l3_wb": i["L3_attn_WB"].T, "l3_wg": i["L3_attn_Wg"].T, "l3_wc": rows(i["L3_attn_WC"].T), "l3_wout": i["L3_attn_Wout"].T,
        "m3_router": i["L3_ffn_router_w"].T, "m3_sgate": i["L3_ffn_w_gate_shared"].T, "m3_sdown": rows(i["L3_ffn_w_down_shared"].T),
        "m3_bias": np.broadcast_to(i["L3_ffn_expert_bias"].reshape(1, NE), (P, NE)),
    }
    return np.concatenate([np.asarray(parts[name], f).reshape(P, cols) for name, cols in PACK], axis=1)


def kernel(**inputs):
    import ml_dtypes
    import numpy as np
    import concourse.bacc as bacc
    from concourse.bass_utils import run_bass_kernel_spmd

    i = {k: np.asarray(v) for k, v in inputs.items()}
    bf = ml_dtypes.bfloat16
    feature_major = lambda a: np.ascontiguousarray(a.transpose(2, 0, 1).reshape(P, T))
    token_major = lambda a: np.ascontiguousarray(a.transpose(1, 0, 2).reshape(P, T))

    sel8 = np.zeros((P, E, P), np.float32)
    for e in range(E):
        sel8[3 * e:3 * e + 3, e, :] = 1
    sel160 = np.zeros((P, 20, 2, 64), np.float32)
    for q in range(20):
        for el in range(2):
            sel160[(2 * q + el) * 3:(2 * q + el) * 3 + 3, q, el, :] = 1
    pairs = np.array([[20 * (j // 2) + 10 * (j % 2) + g for j in range(CHUNKS)] for g in range(GROUPS)])
    gate = i["L3_ffn_w_gate"].reshape(NE // 2, P, P).transpose(0, 2, 1)
    down = i["L3_ffn_w_down"].transpose(0, 2, 1).reshape(NE // 2, P, P)
    m3 = np.stack([gate[pairs], down[pairs]], axis=2).reshape(2 * GROUPS, 4, 2, P, P)
    m3 = m3.transpose(0, 3, 1, 2, 4).reshape(2 * GROUPS, P, 1024)
    w13, w2 = i["L0_ffn_w13"], i["L0_ffn_w2"]
    chunked = lambda w, ch, rows: w.reshape(E, ch, rows, P).transpose(0, 2, 1, 3).reshape(E, rows, ch * P)
    arrays = {
        "xT_in": feature_major(i["x"]), "ctxT_in": feature_major(i["ctx_1024"]), "ctx_in": token_major(i["ctx_1024"]),
        "mask_in": i["mask_Bx1xSxS2_bk1"].reshape(B, P, P).transpose(1, 0, 2).reshape(P, T),
        "pack_in": _pack(i),
        "sel8_in": sel8.reshape(P, E * P).astype(bf), "sel160_in": sel160.reshape(P, 20 * P).astype(bf),
        "caus_in": np.where(np.tril(np.ones((P, P), bool)), 0.0, -1e30).astype(bf), "identb_in": np.eye(P).astype(bf),
        "m0_up_in": w13, "m0_down_in": chunked(w2, M0_CH, M0_ROWS),
        "m2_up_in": np.concatenate([i["L2_ffn_w_gate"], i["L2_ffn_w_up"]], axis=2), "m2_down_in": chunked(i["L2_ffn_w_down"], M2_CH, M2_ROWS),
        "m3_in": m3,
    }
    nc = bacc.Bacc("TRN2", target_bir_lowering=False, num_devices=1)
    args = []
    for name, a in arrays.items():
        arrays[name] = a = np.ascontiguousarray(a)
        args.append(nc.dram_tensor(name, a.shape, mybir.dt.from_np(a.dtype), kind="ExternalInput").ap())
    args.append(nc.dram_tensor("out", (P, T), F32, kind="ExternalOutput").ap())
    program(nc, *args)
    r = run_bass_kernel_spmd(nc, [arrays], core_ids=[0])
    return np.ascontiguousarray(r.results[0]["out"].reshape(P, B, P).transpose(1, 2, 0))
```
